# Optimizing a Trainium2 kernel written in Bass

```python
import numpy as np
import jax
import jax.numpy as jnp

def _softmax(x, axis=-1):
    return jax.nn.softmax(x, axis=axis)

def _gelu(x):
    return jax.nn.gelu(x, approximate=True)

def _silu(x):
    return jax.nn.silu(x)

def _sigmoid(x):
    return jax.nn.sigmoid(x)

def _layernorm(x, axis=-1, eps=1e-05):
    m = jnp.mean(x, axis=axis, keepdims=True)
    v = jnp.var(x, axis=axis, keepdims=True)
    return (x - m) / jnp.sqrt(v + eps)

def _scatter_add(tgt, idx, src, axis=0):
    return tgt.at[idx].add(src)

def _segment_sum(src, seg, n):
    return jax.ops.segment_sum(src, seg, n)
kernel_name = 'mk_prb_d1_jaxref_r2_1632b0'

def setup_inputs(seed: int=0):
    np.random.seed(seed)
    _w = jnp.asarray

    def _L0_attn_setup():
        import jax, jax.numpy as jnp
        import numpy as np
        B, S, D = (4, 2048, 512)
        H = 16
        K = D // H
        M = 128
        FF = 2048
        EPS = 1e-06

        def _layernorm(x, g, b):
            mu = jnp.mean(x, axis=-1, keepdims=True)
            var = jnp.mean(jnp.square(x - mu), axis=-1, keepdims=True)
            return (x - mu) * jax.lax.rsqrt(var + EPS) * g + b

        def _phi(u, omega):
            proj = jnp.einsum('bhsk,mk->bhsm', u, omega)
            sq = 0.5 * jnp.sum(u * u, axis=-1, keepdims=True)
            stab = jnp.max(proj, axis=-1, keepdims=True)
            m = jnp.asarray(M, u.dtype)
            return jnp.exp(proj - sq - stab) / jnp.sqrt(m) + 1e-06

        def _performer_attn(x, wq, wk, wv, wo, omega):
            q = jnp.einsum('bsd,dhk->bhsk', x, wq)
            k = jnp.einsum('bsd,dhk->bhsk', x, wk)
            v = jnp.einsum('bsd,dhk->bhsk', x, wv)
            scale = jnp.asarray(K, x.dtype) ** (-0.25)
            pq = _phi(q * scale, omega)
            pk = _phi(k * scale, omega)
            kv = jnp.einsum('bhsm,bhsk->bhmk', pk, v)
            z = jnp.sum(pk, axis=2)
            num = jnp.einsum('bhsm,bhmk->bhsk', pq, kv)
            den = jnp.einsum('bhsm,bhm->bhs', pq, z)
            out = num / den[..., None]
            out = out.transpose(0, 2, 1, 3).reshape(x.shape[0], x.shape[1], H * K)
            return out @ wo
        key = jax.random.key(seed)
        ks = jax.random.split(key, 12)
        s_in = 1.0 / np.sqrt(D)
        s_ff = 1.0 / np.sqrt(FF)
        return {'x': jax.random.normal(ks[0], (B, S, D), jnp.float32), 'wq': jax.random.normal(ks[1], (D, H, K), jnp.float32) * s_in, 'wk': jax.random.normal(ks[2], (D, H, K), jnp.float32) * s_in, 'wv': jax.random.normal(ks[3], (D, H, K), jnp.float32) * s_in, 'wo': jax.random.normal(ks[4], (H * K, D), jnp.float32) * s_in, 'omega': jax.random.normal(ks[5], (M, K), jnp.float32), 'ln1_g': jnp.ones((D,), jnp.float32), 'ln1_b': jnp.zeros((D,), jnp.float32), 'w1': jax.random.normal(ks[6], (D, FF), jnp.float32) * s_in, 'b1': jnp.zeros((FF,), jnp.float32), 'w2': jax.random.normal(ks[7], (FF, D), jnp.float32) * s_ff, 'b2': jnp.zeros((D,), jnp.float32), 'ln2_g': jnp.ones((D,), jnp.float32), 'ln2_b': jnp.zeros((D,), jnp.float32)}
    _L0_attn_in = _L0_attn_setup()

    def _L0_ffn_setup():
        import jax, jax.numpy as jnp
        import numpy as np
        DIM = 512

        def _reference_tuple_inner(x, W_r, W_k, W_v, mu_r, mu_k):
            B, T, C = x.shape
            x_prev = jnp.concatenate([jnp.zeros((B, 1, C), x.dtype), x[:, :-1, :]], axis=1)
            xr = mu_r * x + (1.0 - mu_r) * x_prev
            xk = mu_k * x + (1.0 - mu_k) * x_prev
            r = jax.nn.sigmoid(jnp.einsum('btc,dc->btd', xr, W_r))
            k = jnp.einsum('btc,dc->btd', xk, W_k)
            k_act = jnp.square(jax.nn.relu(k))
            out = r * jnp.einsum('btc,dc->btd', k_act, W_v)
            new_state = x[:, -1, :]
            return (out, new_state)
        key = jax.random.key(seed)
        ks = jax.random.split(key, 6)
        B, T, C = (8, 1024, DIM)
        x = jax.random.normal(ks[0], (B, T, C), dtype=jnp.float32)
        s = 1.0 / np.sqrt(C)
        W_r = jax.random.uniform(ks[1], (C, C), jnp.float32, -s, s)
        W_k = jax.random.uniform(ks[2], (C, C), jnp.float32, -s, s)
        W_v = jax.random.uniform(ks[3], (C, C), jnp.float32, -s, s)
        mu_r = jax.random.uniform(ks[4], (C,), jnp.float32)
        mu_k = jax.random.uniform(ks[5], (C,), jnp.float32)
        return {'x': x, 'W_r': W_r, 'W_k': W_k, 'W_v': W_v, 'mu_r': mu_r, 'mu_k': mu_k}
    _L0_ffn_in = _L0_ffn_setup()
    _d = {'L0_attn_x': _L0_attn_in['x'], 'L0_attn_wq': _L0_attn_in['wq'], 'L0_attn_wk': _L0_attn_in['wk'], 'L0_attn_wv': _L0_attn_in['wv'], 'L0_attn_wo': _L0_attn_in['wo'], 'L0_attn_omega': _L0_attn_in['omega'], 'L0_attn_ln1_g': _L0_attn_in['ln1_g'], 'L0_attn_ln1_b': _L0_attn_in['ln1_b'], 'L0_attn_w1': _L0_attn_in['w1'], 'L0_attn_b1': _L0_attn_in['b1'], 'L0_attn_w2': _L0_attn_in['w2'], 'L0_attn_b2': _L0_attn_in['b2'], 'L0_attn_ln2_g': _L0_attn_in['ln2_g'], 'L0_attn_ln2_b': _L0_attn_in['ln2_b'], 'L0_ffn_W_r': _L0_ffn_in['W_r'], 'L0_ffn_W_k': _L0_ffn_in['W_k'], 'L0_ffn_W_v': _L0_ffn_in['W_v'], 'L0_ffn_mu_r': _L0_ffn_in['mu_r'], 'L0_ffn_mu_k': _L0_ffn_in['mu_k']}
    _x0 = _d['L0_attn_x']
    _d['L0_attn_x'] = jax.random.normal(jax.random.fold_in(jax.random.key(seed), 1), (8, 1024, 512), dtype=_x0.dtype)
    del _x0
    return _d

def reference(L0_attn_x, L0_attn_wq, L0_attn_wk, L0_attn_wv, L0_attn_wo, L0_attn_omega, L0_attn_ln1_g, L0_attn_ln1_b, L0_attn_w1, L0_attn_b1, L0_attn_w2, L0_attn_b2, L0_attn_ln2_g, L0_attn_ln2_b, L0_ffn_W_r, L0_ffn_W_k, L0_ffn_W_v, L0_ffn_mu_r, L0_ffn_mu_k):

    def _L0_attn_ref(x, wq, wk, wv, wo, omega, ln1_g, ln1_b, w1, b1, w2, b2, ln2_g, ln2_b):
        import jax, jax.numpy as jnp
        import numpy as np
        B, S, D = (4, 2048, 512)
        H = 16
        K = D // H
        M = 128
        FF = 2048
        EPS = 1e-06

        def _layernorm(x, g, b):
            mu = jnp.mean(x, axis=-1, keepdims=True)
            var = jnp.mean(jnp.square(x - mu), axis=-1, keepdims=True)
            return (x - mu) * jax.lax.rsqrt(var + EPS) * g + b

        def _phi(u, omega):
            proj = jnp.einsum('bhsk,mk->bhsm', u, omega)
            sq = 0.5 * jnp.sum(u * u, axis=-1, keepdims=True)
            stab = jnp.max(proj, axis=-1, keepdims=True)
            m = jnp.asarray(M, u.dtype)
            return jnp.exp(proj - sq - stab) / jnp.sqrt(m) + 1e-06

        def _performer_attn(x, wq, wk, wv, wo, omega):
            q = jnp.einsum('bsd,dhk->bhsk', x, wq)
            k = jnp.einsum('bsd,dhk->bhsk', x, wk)
            v = jnp.einsum('bsd,dhk->bhsk', x, wv)
            scale = jnp.asarray(K, x.dtype) ** (-0.25)
            pq = _phi(q * scale, omega)
            pk = _phi(k * scale, omega)
            kv = jnp.einsum('bhsm,bhsk->bhmk', pk, v)
            z = jnp.sum(pk, axis=2)
            num = jnp.einsum('bhsm,bhmk->bhsk', pq, kv)
            den = jnp.einsum('bhsm,bhm->bhs', pq, z)
            out = num / den[..., None]
            out = out.transpose(0, 2, 1, 3).reshape(x.shape[0], x.shape[1], H * K)
            return out @ wo
        h = _performer_attn(x, wq, wk, wv, wo, omega)
        x = _layernorm(x + h, ln1_g, ln1_b)
        h2 = jax.nn.gelu(x @ w1 + b1, approximate=False) @ w2 + b2
        x = _layernorm(x + h2, ln2_g, ln2_b)
        return x

    def _L0_ffn_ref(x, W_r, W_k, W_v, mu_r, mu_k):
        import jax, jax.numpy as jnp
        import numpy as np
        DIM = 512

        def _reference_tuple_inner(x, W_r, W_k, W_v, mu_r, mu_k):
            B, T, C = x.shape
            x_prev = jnp.concatenate([jnp.zeros((B, 1, C), x.dtype), x[:, :-1, :]], axis=1)
            xr = mu_r * x + (1.0 - mu_r) * x_prev
            xk = mu_k * x + (1.0 - mu_k) * x_prev
            r = jax.nn.sigmoid(jnp.einsum('btc,dc->btd', xr, W_r))
            k = jnp.einsum('btc,dc->btd', xk, W_k)
            k_act = jnp.square(jax.nn.relu(k))
            out = r * jnp.einsum('btc,dc->btd', k_act, W_v)
            new_state = x[:, -1, :]
            return (out, new_state)
        return _reference_tuple_inner(x, W_r, W_k, W_v, mu_r, mu_k)[0]
    x = L0_attn_x
    xn = _layernorm(x, axis=-1)
    x = x + _L0_attn_ref(xn, L0_attn_wq, L0_attn_wk, L0_attn_wv, L0_attn_wo, L0_attn_omega, L0_attn_ln1_g, L0_attn_ln1_b, L0_attn_w1, L0_attn_b1, L0_attn_w2, L0_attn_b2, L0_attn_ln2_g, L0_attn_ln2_b) + _L0_ffn_ref(xn, L0_ffn_W_r, L0_ffn_W_k, L0_ffn_W_v, L0_ffn_mu_r, L0_ffn_mu_k)
    return x

_drawn_inputs = setup_inputs


def setup_inputs(seed=0):
    import zlib

    import numpy as np

    out = dict(_drawn_inputs(seed))
    spreads = {'L0_attn_ln1_g': (1.0, 0.2),
     'L0_attn_ln1_b': (0.0, 0.1),
     'L0_attn_b1': (0.0, 0.271),
     'L0_attn_b2': (0.0, 0.1),
     'L0_attn_ln2_g': (1.0, 0.2),
     'L0_attn_ln2_b': (0.0, 0.1)}
    factors = {'L0_ffn_W_r': 6.077, 'L0_ffn_mu_r': 8.0}
    for name, (base, spread) in spreads.items():
        noise = np.random.default_rng([zlib.crc32(name.encode()), seed]).standard_normal(out[name].shape)
        drawn = base * np.exp(spread * noise) if base else spread * noise
        out[name] = jnp.asarray(drawn.astype(out[name].dtype))
    for name, factor in factors.items():
        out[name] = (out[name] * factor).astype(out[name].dtype)
    return out
```

```python
import concourse.bass as bass
from concourse import mybir
from contextlib import ExitStack

FP32 = mybir.dt.float32
FP32R = mybir.dt.float32r
ALU = mybir.AluOpType
ACT = mybir.ActivationFunctionType
AX = mybir.AxisListType

P = 128
D = 512
H = 16
KD = D // H
M = 128
FF = 2048
NC = D // P
HC = P // KD
FC = FF // P
TG = 2
GT = TG * P
W = D

USCALE = float(KD) ** -0.25
FLOOR = 1e-6 * float(M) ** 0.5
EPS0, EPS1 = 1e-5, 1e-6

TERMS = ((0, 0), (0, 1), (1, 0))


class Scope:

    def __init__(self, nc, name):
        self.nc, self.name, self.sems = nc, name, []

    def sbuf_tensor(self, name, shape, dt):
        return self.nc.sbuf_tensor(self.name + name, shape, dt)

    def psum_tensor(self, name, shape, dt):
        return self.nc.psum_tensor(self.name + name, shape, dt)

    def sem(self, name):
        self.sems.append(self.nc.alloc_semaphore(self.name + name))
        return self.sems[-1]

    def end(self):
        self.nc.all_engine_barrier()
        self.nc.clear_and_free_semaphores(self.sems)
        self.nc.all_engine_barrier()


class Bank:

    def __init__(self, mem, ctx, name):
        self.t = ctx.enter_context(mem.psum_tensor(name, [P, W], FP32))
        self.full = mem.sem(name + "_full")
        self.free = mem.sem(name + "_free")


class Pair:

    def __init__(self, mem, ctx, name, shape):
        self.hi = ctx.enter_context(mem.sbuf_tensor(name + "_hi", shape, FP32R))
        self.lo = ctx.enter_context(mem.sbuf_tensor(name + "_lo", shape, FP32R))

    def __getitem__(self, key):
        return (self.hi[key], self.lo[key])


def f32(ap):
    return ap.bitcast(FP32)


def wait(eng, sem, value):
    if isinstance(value, int) and value <= 0:
        return
    eng.wait_ge(sem, value)


def wait_alone(eng, sem, value, passed):
    wait(eng, sem, value)
    eng.sem_inc(passed, 1)


def product(pe, out, stationary, moving, start, stop):
    for n, (a, b) in enumerate(TERMS):
        last = pe.matmul(out, stationary[a], moving[b], start=start and n == 0,
                         stop=stop and n == len(TERMS) - 1)
    return last


def halves(bank):
    return bank.t[:, :].rearrange("p (a n) -> p a n", a=2)


def by_group(dram):
    return dram.rearrange("(g t p) d -> g p t d", t=TG, p=P)


def row_on_all(vector, n):
    return vector.rearrange("(a n) -> a n", a=1).broadcast_to([P, n])


def make_identity(pool, ident, made):
    pool.memset(ident[:, :], 0.0).then_inc(made, 1)
    pool.wait_ge(made, 1)
    pool.affine_select(out=ident[:, :], in_=ident[:, :], compare_op=ALU.not_equal, fill=1.0, base=0,
                       pattern=[[-1, P]], channel_multiplier=1).then_inc(made, 1)


def split_weights(mem, ctx, name, weights, stages, banks=(), ident=None):
    loaded = [mem.sem(f"{name}_loaded{s}") for s in range(len(stages))]
    turned_full = mem.sem(name + "_turned")
    rounded = mem.sem(name + "_rounded")
    done = mem.sem(name + "_split")
    ns = len(stages)
    steps, through, fills = [], [], 0
    for n, (_, dst, turned) in enumerate(weights):
        if turned:
            for m in range(TG):
                cols = tuple(d[:, :, m * P:(m + 1) * P] for d in dst)
                bank = banks[fills % len(banks)].t[:, :].rearrange("p (c n) -> p c n", c=NC)
                steps.append((n, bank, cols, fills, m))
                fills += 1
        else:
            steps.append((n, stages[n % ns], dst, None, None))
        through.append(len(steps))

    def load(sp):
        for n, (src, _, _) in enumerate(weights):
            if n >= ns:
                sp.wait_ge(done, through[n - ns])
            sp.dma_start(stages[n % ns], src).then_inc(loaded[n % ns], 16)

    def turn(pe):
        for k, (n, _, _, fill, m) in enumerate(steps):
            if fill is None:
                continue
            pe.wait_ge(loaded[n % ns], 16 * (n // ns + 1))
            if fill >= len(banks):
                pe.wait_ge(done, k - len(banks) + 1)
            for c in range(NC):
                last = pe.transpose(banks[fill % len(banks)].t[:, c * P:(c + 1) * P],
                                    stages[n % ns][:, m, c * P:(c + 1) * P], ident[:, :])
            last.then_inc(turned_full, 1)

    def hi(act):
        for n, src, dst, fill, _ in steps:
            if fill is None:
                act.wait_ge(loaded[n % ns], 16 * (n // ns + 1))
            else:
                act.wait_ge(turned_full, fill + 1)
            act.activation(dst[0], src, ACT.Copy).then_inc(rounded, 1)

    def lo(dve):
        for k, (_, src, dst, _, _) in enumerate(steps):
            dve.wait_ge(rounded, k + 1)
            dve.tensor_tensor(dst[1], src, f32(dst[0]), ALU.subtract).then_inc(done, 1)

    return load, turn, hi, lo, done, through


def omega_transposed(mem, ctx, omega, om4, bd, ident, ident_made, bank):
    loaded = mem.sem("omega_loaded")
    cleared = mem.sem("omega_cleared")
    turned = mem.sem("omega_turned")
    rounded = mem.sem("omega_rounded")
    ready = mem.sem("omega_ready")

    def load(sp):
        for j in range(HC):
            sp.dma_start(om4[:, j * KD:(j + 1) * KD], omega).then_inc(loaded, 16)

    def clear(pool):
        pool.memset(f32(bd.hi[:, :]), 0.0).then_inc(cleared, 1)
        pool.memset(f32(bd.lo[:, :]), 0.0).then_inc(cleared, 1)

    def transpose(pe):
        pe.wait_ge(loaded, 16 * HC)
        pe.wait_ge(ident_made, 2)
        pe.transpose(bank.t[:, 0:P], om4[:, :], ident[:, :]).then_inc(turned, 1)

    def hi(act):
        act.wait_ge(turned, 1)
        act.wait_ge(cleared, 2)
        for j in range(HC):
            q = slice(j * KD, (j + 1) * KD)
            last = act.activation(bd.hi[q, j * M:(j + 1) * M], bank.t[q, 0:M], ACT.Copy)
        last.then_inc(rounded, 1)

    def lo(dve):
        dve.wait_ge(rounded, 1)
        for j in range(HC):
            q = slice(j * KD, (j + 1) * KD)
            last = dve.tensor_tensor(bd.lo[q, j * M:(j + 1) * M], bank.t[q, 0:M],
                                     f32(bd.hi[q, j * M:(j + 1) * M]), ALU.subtract)
        last.then_inc(ready, 1)

    return load, clear, transpose, hi, lo, ready


class Norm:

    def __init__(self, mem, ctx, name, eps):
        def sb(n, shape):
            return ctx.enter_context(mem.sbuf_tensor(f"{name}_{n}", shape, FP32))
        self.eps = eps
        self.stats = sb("stats", [P, TG, 6])
        self.mv = sb("mv", [P, TG, 2])
        self.base = sb("base", [P, TG])
        self.negmean = sb("negmean", [P, TG])
        self.power = sb("power", [P, TG])
        self.rstd = sb("rstd", [P, TG])
        self.shift = sb("shift", [P, TG])
        self.chain = mem.sem(name + "_chain")
        self.passed = mem.sem(name + "_passed")
        self.root = mem.sem(name + "_root")
        self.ready = mem.sem(name + "_ready")

    def init(self, pool):
        pool.memset(self.power[:, :], -0.5).then_inc(self.root, 1)

    def reduce(self, dve, g, tiles):
        c, n = self.chain, 6
        for t in range(TG):
            dve.bn_stats(self.stats[:, t, :], tiles[t]).then_inc(c, 1)
        for t in range(TG):
            wait_alone(dve, c, g * n + 1 + t, self.passed)
            dve.bn_aggr(self.mv[:, t, :], self.stats[:, t, :]).then_inc(c, 1)
        dve.wait_ge(c, g * n + 4)
        dve.tensor_scalar(self.base[:, :], self.mv[:, :, 1], self.eps, None, ALU.add).then_inc(c, 1)
        dve.tensor_scalar(self.negmean[:, :], self.mv[:, :, 0], -1.0, None, ALU.mult).then_inc(c, 1)

    def invert(self, pool, g):
        pool.wait_ge(self.chain, g * 6 + 6)
        pool.wait_ge(self.root, g + 1)
        pool.tensor_tensor(self.rstd[:, :], self.base[:, :], self.power[:, :], ALU.pow).then_inc(self.root, 1)
        pool.wait_ge(self.root, g + 2)
        pool.tensor_tensor(self.shift[:, :], self.negmean[:, :], self.rstd[:, :], ALU.mult).then_inc(self.ready, 1)


def after(n, count):
    return (n + 1) & (count - 1)


def keys_pass(nc, x, wq, wk, wv, omega, xn_d, u_d, kv_d, z_d, n_batches, groups_per_batch):
    G = n_batches * groups_per_batch
    GB = groups_per_batch
    x_g, xn_g, u_g = by_group(x), by_group(xn_d), by_group(u_d)

    mem = Scope(nc, "keys_")
    ctx = ExitStack()
    with ctx:
        def sb(name, shape, dt=FP32):
            return ctx.enter_context(mem.sbuf_tensor(name, shape, dt))

        def sem(name):
            return mem.sem(name)

        w = {n: Pair(mem, ctx, "w" + n, [P, NC, D]) for n in "qkv"}
        bd = Pair(mem, ctx, "omegaT", [P, HC * M])
        ident = sb("ident", [P, P])
        om4 = sb("om4", [P, HC * KD])
        xin = sb("xin", [P, TG, D])
        xn = sb("xn", [P, TG, D])
        xT = Pair(mem, ctx, "xT", [P, NC, GT])
        uq = sb("uq", [P, TG, D])
        uk = sb("uk", [P, TG, D])
        squares = [sb(f"squares{t}", [P, D]) for t in range(TG)]
        kT = Pair(mem, ctx, "kT", [P, NC, GT])
        v = Pair(mem, ctx, "v", [P, TG, D])
        sq = sb("sq", [P, TG, H])
        top = sb("top", [P, TG, H])
        below = sb("below", [P, TG, H])
        e = [sb(f"e{t}", [P, HC * M]) for t in range(TG)]
        pk = [[Pair(mem, ctx, f"pk{c}{t}", [P, HC * M]) for t in range(TG)] for c in range(2)]
        kv_sum = sb("kv_sum", [P, NC, M])
        z_sum = sb("z_sum", [P, NC, HC * M])
        norm = Norm(mem, ctx, "n0", EPS0)

        dense = [Bank(mem, ctx, f"dense{t}") for t in range(TG)]
        turn_x = Bank(mem, ctx, "turn_x")
        turn_k = Bank(mem, ctx, "turn_k")
        proj = [Bank(mem, ctx, f"proj{t}") for t in range(TG)]
        kv = [Bank(mem, ctx, f"kv{n}") for n in range(2)]

        sp_passed, pool_passed, dve_passed = sem("sp_passed"), sem("pool_passed"), sem("dve_passed")
        ident_made = sem("ident_made")
        x_loaded, xn_ready, xn_stored = sem("x_loaded"), sem("xn_ready"), sem("xn_stored")
        xT_hi, u_stored = sem("xT_hi"), sem("u_stored")
        kT_hi, v_hi = sem("kT_hi"), sem("v_hi")
        sq_ready = [sem(f"sq_ready{t}") for t in range(TG)]
        top_ready = [sem(f"top_ready{t}") for t in range(TG)]
        below_ready = [sem(f"below_ready{t}") for t in range(TG)]
        e_ready = [sem(f"e_ready{t}") for t in range(TG)]
        pk_hi = [sem(f"pk_hi{t}") for t in range(TG)]
        pk_ready = [sem(f"pk_ready{t}") for t in range(TG)]
        z_added = [sem(f"z_added{t}") for t in range(TG)]
        kv_cleared, z_cleared, sums_stored = sem("kv_cleared"), sem("z_cleared"), sem("sums_stored")

        stages = [uq[:, :, :], uk[:, :, :]]
        halves_of = []
        for n, src in (("q", wq), ("k", wk), ("v", wv)):
            view = src.rearrange("(c p) h k -> p c (h k)", p=P)
            for c in range(0, NC, TG):
                halves_of.append((view[:, c:c + TG, :], w[n][:, c:c + TG, :], False))
        load_w, _, hi_w, lo_w, w_split, _ = split_weights(mem, ctx, "w1", halves_of, stages)
        n_w = len(halves_of)
        om_load, om_clear, om_turn, om_hi, om_lo, om_ready = omega_transposed(
            mem, ctx, omega, om4, bd, ident, ident_made, kv[0])

        BODY = [("x", 0, 2), ("proj", 0, 0), ("q", 0, 1), ("pk", 0, 0), ("proj", 1, 0), ("q", 1, 1), ("pk", 1, 0),
                ("norm", 0, 2), ("kv", 0, 0), ("proj", 2, 0), ("k", 0, 1), ("pk", 2, 0), ("kv", 1, 0), ("proj", 3, 0),
                ("k", 1, 1), ("pk", 3, 0), ("kv", 2, 0), ("v", 0, 1), ("turn_k", 0, 1), ("turn_k", 1, 1),
                ("kv", 3, 0), ("v_out", 0, 1), ("v", 1, 1), ("v_out", 1, 1), ("turn_x", 0, 2), ("turn_x", 1, 2)]
        HEAD = [("x", 0, 0), ("norm", 0, 0), ("turn_x", 0, 0), ("turn_x", 1, 0), ("x", 0, 1), ("norm", 0, 1),
                ("q", 0, 0), ("q", 1, 0), ("k", 0, 0), ("k", 1, 0), ("v", 0, 0), ("turn_k", 0, 0), ("turn_k", 1, 0),
                ("v_out", 0, 0), ("v", 1, 0), ("v_out", 1, 0), ("turn_x", 0, 1), ("turn_x", 1, 1)]

        def run(eng, do, batch_end):
            def body(g, b, ahead=2):
                for job, n, lead in BODY:
                    if lead <= ahead:
                        do(job, n, g + lead, b)
            for job, n, g in HEAD:
                do(job, n, g, 0)
            body(0, 0)
            with eng.Fori(1, GB) as i:
                body(i, 0)
            batch_end(0)
            with eng.Fori(1, n_batches - 1) as b:
                with eng.Fori(0, GB) as i:
                    body(b * GB + i, b)
                batch_end(b)
            last = n_batches - 1
            with eng.Fori(0, GB - 2) as i:
                body(i + last * GB, last)
            body(G - 2, last, ahead=1)
            body(G - 1, last, ahead=0)
            batch_end(last)

        block = ctx.enter_context(nc.Block())

        @block.sync
        def _(sp):
            om_load(sp)
            load_w(sp)

            def do(job, n, g, b):
                if job == "x":
                    wait(sp, xn_ready, TG * g)
                    sp.dma_start(xin[:, :, :], x_g[g]).then_inc(x_loaded, 16)
                if job == "norm":
                    sp.wait_ge(xn_ready, TG * g + TG)
                    sp.dma_start(xn_g[g], xn[:, :, :]).then_inc(xn_stored, 16)
                if job == "q" and n == 1:
                    for t in range(TG):
                        sp.wait_ge(dense[t].free, 3 * g + 1)
                    sp.dma_start(u_g[g], uq[:, :, :]).then_inc(u_stored, 16)

            def batch_end(b):
                for t in range(TG):
                    wait_alone(sp, z_added[t], (b + 1) * (GB * NC), sp_passed)
                    wait_alone(sp, kv[t].free, (b + 1) * (GB * 2), sp_passed)
                sp.dma_start(z_d[b], z_sum[:, :, :]).then_inc(sums_stored, 16)
                sp.dma_start(kv_d[b], kv_sum[:, :, :]).then_inc(sums_stored, 16)

            run(sp, do, batch_end)
            sp.wait_ge(xn_stored, 16 * G)
            sp.wait_ge(u_stored, 16 * G)
            sp.wait_ge(sums_stored, 32 * n_batches)

        @block.gpsimd
        def _(pool):
            make_identity(pool, ident, ident_made)
            om_clear(pool)
            norm.init(pool)
            pool.memset(z_sum[:, :, :], 0.0).then_inc(z_cleared, 1)

            def do(job, n, g, b):
                if job == "norm":
                    norm.invert(pool, g)
                if job == "proj":
                    pool.wait_ge(z_cleared, b + 1)
                    for t in range(TG):
                        pool.wait_ge(e_ready[t], NC * g + n + 1)
                        wait(pool, z_added[1 - t], NC * g + n + t)
                        pool.tensor_tensor(z_sum[:, n, :], z_sum[:, n, :], e[t][:, :], ALU.add)\
                            .then_inc(z_added[t], 1)

            def batch_end(b):
                wait_alone(pool, sums_stored, b * 32 + 32, pool_passed)
                pool.memset(z_sum[:, :, :], 0.0).then_inc(z_cleared, 1)

            run(pool, do, batch_end)

        @block.scalar
        def _(act):
            om_hi(act)
            hi_w(act)

            def do(job, n, g, b):
                if job == "norm":
                    act.wait_ge(norm.ready, g + 1)
                    wait(act, turn_x.full, 2 * g)
                    wait(act, xn_stored, 16 * g)
                    for t in range(TG):
                        act.activation(xn[:, t, :], xin[:, t, :], ACT.Identity, bias=norm.shift[:, t:t + 1],
                                       scale=norm.rstd[:, t:t + 1]).then_inc(xn_ready, 1)
                if job == "turn_x":
                    for t in range(TG):
                        wait(act, dense[t].full, 3 * g)
                    act.wait_ge(turn_x.full, 2 * g + n + 1)
                    act.activation(xT.hi[:, 2 * n:2 * n + 2, :], halves(turn_x), ACT.Copy).then_inc(xT_hi, 1)
                if job == "q":
                    act.wait_ge(dense[n].full, 3 * g + 1)
                    wait(act, u_stored, 16 * g)
                    if isinstance(g, int) and g == 0:
                        act.wait_ge(w_split, n_w)
                    act.activation(uq[:, n, :], dense[n].t[:, :], ACT.Copy, scale=USCALE).then_inc(dense[n].free, 1)
                if job == "k":
                    act.wait_ge(dense[n].full, 3 * g + 2)
                    wait(act, turn_k.full, 2 * g)
                    wait(act, sq_ready[n], g)
                    act.activation(uk[:, n, :], dense[n].t[:, :], ACT.Copy, scale=USCALE)
                    act.activation(squares[n][:, :], dense[n].t[:, :], ACT.Square, scale=USCALE)\
                        .then_inc(dense[n].free, 1)
                if job == "v_out":
                    act.wait_ge(dense[n].full, 3 * g + 3)
                    for m in range(2):
                        wait(act, kv[m].full, 2 * g)
                    act.activation(v.hi[:, n, :], dense[n].t[:, :], ACT.Copy).then_inc(v_hi, 1)
                if job == "turn_k":
                    for t in range(TG):
                        wait(act, proj[t].full, NC * g)
                    act.wait_ge(turn_k.full, 2 * g + n + 1)
                    act.activation(kT.hi[:, 2 * n:2 * n + 2, :], halves(turn_k), ACT.Copy).then_inc(kT_hi, 1)
                if job == "proj":
                    for t in range(TG):
                        act.wait_ge(below_ready[t], NC * g + n + 1)
                        wait(act, pk_ready[t], NC * g + n)
                        wait(act, z_added[t], NC * g + n)
                        for j in range(HC):
                            last = act.activation(e[t][:, j * M:(j + 1) * M], proj[t].t[:, j * M:(j + 1) * M],
                                                  ACT.Exp, bias=below[:, t, n * HC + j:n * HC + j + 1])
                        last.then_inc(e_ready[t], 1)
                    wait(act, kv[n % 2].full, 2 * g + n // 2)
                    for t in range(TG):
                        act.wait_ge(e_ready[t], NC * g + n + 1)
                        act.activation(pk[n % 2][t].hi[:, :], e[t][:, :], ACT.Copy, bias=FLOOR).then_inc(pk_hi[t], 1)

            run(act, do, lambda b: None)

        @block.vector
        def _(dve):
            dve.memset(kv_sum[:, :, :], 0.0).then_inc(kv_cleared, 1)
            om_lo(dve)
            lo_w(dve)

            def do(job, n, g, b):
                if job == "norm":
                    dve.wait_ge(x_loaded, 16 * g + 16)
                    wait(dve, norm.ready, g)
                    norm.reduce(dve, g, [xin[:, t, :] for t in range(TG)])
                if job == "turn_x":
                    dve.wait_ge(xT_hi, 2 * g + n + 1)
                    dve.tensor_tensor(xT.lo[:, 2 * n:2 * n + 2, :], halves(turn_x),
                                      f32(xT.hi[:, 2 * n:2 * n + 2, :]), ALU.subtract).then_inc(turn_x.free, 1)
                if job == "v_out":
                    dve.wait_ge(v_hi, TG * g + n + 1)
                    dve.tensor_tensor(v.lo[:, n, :], dense[n].t[:, :], f32(v.hi[:, n, :]), ALU.subtract)\
                        .then_inc(dense[n].free, 1)
                if job == "turn_k":
                    dve.wait_ge(kT_hi, 2 * g + n + 1)
                    dve.tensor_tensor(kT.lo[:, 2 * n:2 * n + 2, :], halves(turn_k),
                                      f32(kT.hi[:, 2 * n:2 * n + 2, :]), ALU.subtract).then_inc(turn_k.free, 1)
                    dve.wait_ge(dense[n].free, 3 * g + 2)
                    dve.tensor_reduce(sq[:, n, :], squares[n][:, :].rearrange("p (h k) -> p h k", h=H), AX.X,
                                      ALU.add).then_inc(sq_ready[n], 1)
                if job == "proj":
                    heads = slice(n * HC, (n + 1) * HC)
                    for t in range(TG):
                        dve.wait_ge(proj[t].full, NC * g + n + 1)
                        dve.tensor_reduce(top[:, t, heads], proj[t].t[:, :].rearrange("p (h m) -> p h m", h=HC),
                                          AX.X, ALU.max).then_inc(top_ready[t], 1)
                    for t in range(TG):
                        dve.wait_ge(sq_ready[t], g + 1)
                        dve.wait_ge(top_ready[t], NC * g + n + 1)
                        dve.scalar_tensor_tensor(out=below[:, t, heads], in0=sq[:, t, heads], scalar=-0.5,
                                                 in1=top[:, t, heads], op0=ALU.mult, op1=ALU.subtract)\
                            .then_inc(below_ready[t], 1)
                if job == "pk":
                    for t in range(TG):
                        dve.wait_ge(pk_hi[t], NC * g + n + 1)
                        dve.scalar_tensor_tensor(out=pk[n % 2][t].lo[:, :], in0=e[t][:, :], scalar=FLOOR,
                                                 in1=f32(pk[n % 2][t].hi[:, :]), op0=ALU.add, op1=ALU.subtract)\
                            .then_inc(pk_ready[t], 1)
                if job == "kv":
                    bank = kv[n % 2]
                    dve.wait_ge(kv_cleared, b + 1)
                    dve.wait_ge(bank.full, 2 * g + n // 2 + 1)
                    wait(dve, bank.free, 2 * g + n // 2)
                    for j in range(HC):
                        q = slice(j * KD, (j + 1) * KD)
                        last = dve.tensor_tensor(kv_sum[q, n, :], bank.t[q, j * M:(j + 1) * M], kv_sum[q, n, :],
                                                 ALU.add)
                    last.then_inc(bank.free, 1)

            def batch_end(b):
                wait_alone(dve, sums_stored, b * 32 + 32, dve_passed)
                dve.memset(kv_sum[:, :, :], 0.0).then_inc(kv_cleared, 1)

            run(dve, do, batch_end)

        @block.tensor
        def _(pe):
            om_turn(pe)
            pe.wait_ge(om_ready, 1)

            def do(job, n, g, b):
                if job in ("turn_x", "turn_k"):
                    bank, src = (turn_x, xn) if job == "turn_x" else (turn_k, uk)
                    if job == "turn_x":
                        pe.wait_ge(xn_ready, TG * g + TG)
                    else:
                        for t in range(TG):
                            pe.wait_ge(dense[t].free, 3 * g + 2)
                    wait(pe, bank.free, 2 * g + n)
                    for c in range(2):
                        for t in range(TG):
                            last = pe.transpose(bank.t[:, c * GT + t * P:c * GT + (t + 1) * P],
                                                src[:, t, (2 * n + c) * P:(2 * n + c + 1) * P], ident[:, :])
                    last.then_inc(bank.full, 1)
                if job in ("q", "k", "v"):
                    k = "qkv".index(job)
                    if isinstance(g, int) and g == 0:
                        pe.wait_ge(w_split, (k + 1) * (n_w // 3))
                    pe.wait_ge(turn_x.free, 2 * g + 2)
                    wait(pe, dense[n].free, 3 * g + k)
                    for c in range(NC):
                        last = product(pe, dense[n].t[:, :], xT[:, c, n * P:(n + 1) * P], w[job][:, c, :],
                                       start=c == 0, stop=c == NC - 1)
                    last.then_inc(dense[n].full, 1)
                if job == "proj":
                    pe.wait_ge(turn_k.free, 2 * g + n // 2 + 1)
                    for t in range(TG):
                        wait(pe, e_ready[t], NC * g + n)
                        product(pe, proj[t].t[:, :], kT[:, n, t * P:(t + 1) * P], bd[:, :], start=True, stop=True)\
                            .then_inc(proj[t].full, 1)
                if job == "kv":
                    wait(pe, kv[n % 2].free, 2 * g + n // 2)
                    for t in range(TG):
                        pe.wait_ge(dense[t].free, 3 * g + 3)
                        pe.wait_ge(pk_ready[t], NC * g + n + 1)
                        last = product(pe, kv[n % 2].t[:, :], v[:, t, n * P:(n + 1) * P], pk[n % 2][t][:, :],
                                       start=t == 0, stop=t == TG - 1)
                    last.then_inc(kv[n % 2].full, 1)

            run(pe, do, lambda b: None)

    mem.end()


def attend_pass(nc, wo, omega, ln1_g, ln1_b, w_r, w_k, w_v, mu_r, mu_k, xn_d, u_d, kv_d, z_d, y_d, r_d,
                n_batches, groups_per_batch):
    G = n_batches * groups_per_batch
    GB = groups_per_batch
    S = GB * GT
    xn_g, u_g, y_g, r_g = by_group(xn_d), by_group(u_d), by_group(y_d), by_group(r_d)

    mem = Scope(nc, "attend_")
    ctx = ExitStack()
    with ctx:
        def sb(name, shape, dt=FP32):
            return ctx.enter_context(mem.sbuf_tensor(name, shape, dt))

        def sem(name):
            return mem.sem(name)

        w = {n: Pair(mem, ctx, "w" + n, [P, NC, D]) for n in ("o", "r", "k", "v")}
        bd = Pair(mem, ctx, "omegaT", [P, HC * M])
        ident = sb("ident", [P, P])
        ones = sb("ones", [P, P])
        gain, offset = sb("gain", [P, D]), sb("offset", [P, D])
        mu = sb("mu", [P, 2, NC])
        rest = sb("rest", [P, 2, NC])
        uq = sb("uq", [P, TG, D])
        xa = sb("xa", [P, TG, D])
        xb = sb("xb", [P, TG, D])
        y = sb("y", [P, TG, D])
        squares = sb("squares", [P, D])
        qT = Pair(mem, ctx, "qT", [P, NC, GT])
        xT = sb("xTf", [P, NC, 1 + GT])
        mixed = sb("mixed", [P, NC, GT])
        mix = [Pair(mem, ctx, f"mix{n}", [P, NC, GT]) for n in range(2)]
        act_k = sb("act_k", [P, 2, GT])
        act_k2 = sb("act_k2", [P, 2, GT])
        ka = Pair(mem, ctx, "ka", [P, NC, GT])
        gate = sb("gate", [P, TG, D])
        sq = sb("sq", [P, TG, H])
        top = sb("top", [P, TG, H])
        below = sb("below", [P, TG, H])
        e = [[sb(f"e{t}{c}", [P, HC * M]) for c in range(2)] for t in range(TG)]
        ez = [sb(f"ez{t}", [P, HC * M]) for t in range(TG)]
        dsum = sb("dsum", [P, TG, HC])
        den = sb("den", [P, TG, HC])
        rden = sb("rden", [P, TG, HC])
        pT = [Pair(mem, ctx, f"pT{n}", [P, 2 * GT]) for n in range(2)]
        kvp = Pair(mem, ctx, "kvp", [P, NC, HC, P])
        kv_in = sb("kv_in", [P, NC, M])
        z_in = sb("z_in", [P, NC, HC * M])
        z_all = sb("z_all", [P, NC, HC * M])
        z_floor = sb("z_floor", [P, H])
        z_heads = sb("z_heads", [P, H])
        oT = Pair(mem, ctx, "oT", [P, NC, GT])
        norm = Norm(mem, ctx, "n1", EPS1)

        turn = Bank(mem, ctx, "turn")
        proj = [Bank(mem, ctx, f"proj{t}") for t in range(TG)]
        probs = [Bank(mem, ctx, f"probs{n}") for n in range(2)]
        num = Bank(mem, ctx, "num")
        gated = [Bank(mem, ctx, f"gated{t}") for t in range(TG)]

        sp_passed = sem("sp_passed")
        ident_made = sem("ident_made")
        consts_loaded, consts_ready, ones_made = sem("consts_loaded"), sem("consts_ready"), sem("ones_made")
        q_loaded, xa_loaded, xb_loaded, sums_loaded = sem("q_loaded"), sem("xa_loaded"), sem("xb_loaded"), sem("sums_loaded")
        kvp_cleared, kvp_hi, kvp_ready = sem("kvp_cleared"), sem("kvp_hi"), sem("kvp_ready")
        z_ready, z_chain, z_floor_ready = sem("z_ready"), sem("z_chain"), sem("z_floor_ready")
        squared, sq_ready = sem("squared"), sem("sq_ready")
        qT_hi, carried = sem("qT_hi"), sem("carried")
        mix_chain, mix_full, mix_hi, mix_ready = sem("mix_chain"), sem("mix_full"), sem("mix_hi"), sem("mix_ready")
        act_k_ready, act_k2_ready, ka_hi, ka_ready = sem("act_k_ready"), sem("act_k2_ready"), sem("ka_hi"), sem("ka_ready")
        gate_ready, r_stored = sem("gate_ready"), sem("r_stored")
        top_ready = [sem(f"top_ready{t}") for t in range(TG)]
        below_ready = [sem(f"below_ready{t}") for t in range(TG)]
        e_ready = [sem(f"e_ready{t}") for t in range(TG)]
        ez_ready = [sem(f"ez_ready{t}") for t in range(TG)]
        den_chain = [sem(f"den_chain{t}") for t in range(TG)]
        den_ready = [sem(f"den_ready{t}") for t in range(TG)]
        p_ready = [sem(f"p_ready{t}") for t in range(TG)]
        pT_hi = [sem(f"pT_hi{n}") for n in range(2)]
        num_done = [sem(f"num_done{n}") for n in range(2)]
        oT_hi, wo_done = sem("oT_hi"), sem("wo_done")
        sum_ready, y_ready, gained, offsets, y_stored = sem("sum_ready"), sem("y_ready"), sem("gained"), sem("offsets"), sem("y_stored")

        stages = [xa[:, :, :], xb[:, :, :], y[:, :, :]]
        halves_of = []
        for n, src in (("o", wo), ("r", w_r), ("k", w_k), ("v", w_v)):
            view = src.rearrange("(c p) n -> p c n", p=P)
            for c in range(0, NC, TG):
                if n == "o":
                    halves_of.append((view[:, c:c + TG, :], w[n][:, c:c + TG, :], False))
                else:
                    halves_of.append((view[:, c:c + TG, :], w[n][:, :, c * P:(c + TG) * P], True))
        load_w, turn_w, hi_w, lo_w, w_split, w_through = split_weights(
            mem, ctx, "w2", halves_of, stages, gated, ident)
        n_w = w_through[-1]
        om_load, om_clear, om_turn, om_hi, om_lo, om_ready = omega_transposed(
            mem, ctx, omega, squares[:, 0:HC * KD], bd, ident, ident_made, num)

        TB = 5 + 4 * GB

        BODY = [("turn_q", 0), ("turn_q", 1), ("turn_x", 0), ("turn_x", 1), ("out", 0), ("out", 1), ("mix", 0),
                ("proj", 0), ("proj", 1), ("den", 0), ("r", 0), ("den", 1), ("mix", 1), ("probs", 0), ("probs", 1), ("num", 0),
                ("num", 1), ("proj", 2), ("r", 1), ("probs", 2), ("den", 2), ("probs", 3), ("num", 2), ("attn", 0), ("num", 3),
                ("proj", 3), ("k", 0), ("probs", 4), ("den", 3), ("probs", 5), ("num", 4), ("num", 5), ("probs", 6),
                ("probs", 7), ("num", 6), ("num", 7), ("attn", 1), ("k", 1), ("wo", 0), ("wo", 1), ("norm", 0)]

        def run(eng, do, batch_start):
            def body(g, b, i, first=False):
                for job, n in BODY:
                    if job == "out":
                        if not first:
                            do(job, n, g - 1, b, i)
                    else:
                        do(job, n, g, b, i)
            batch_start(0)
            body(0, 0, 0, first=True)
            with eng.Fori(1, GB) as i:
                body(i, 0, i)
            with eng.Fori(1, n_batches) as b:
                batch_start(b)
                with eng.Fori(0, GB) as i:
                    body(b * GB + i, b, i)
            for t in range(TG):
                do("out", t, G - 1, n_batches - 1, GB - 1)

        block = ctx.enter_context(nc.Block())

        @block.sync
        def _(sp):
            om_load(sp)
            load_w(sp)
            for dst, src in ((gain[:, :], row_on_all(ln1_g, D)), (offset[:, :], row_on_all(ln1_b, D)),
                             (mu[:, 0, :], mu_r.rearrange("(c p) -> p c", p=P)),
                             (mu[:, 1, :], mu_k.rearrange("(c p) -> p c", p=P))):
                with nc.allow_non_contiguous_dma(reason="one vector of the model width"):
                    sp.dma_start(dst, src).then_inc(consts_loaded, 16)
            sp.dma_start(kv_in[:, :, :], kv_d[0]).then_inc(sums_loaded, 16)
            sp.dma_start(z_in[:, :, :], z_d[0]).then_inc(sums_loaded, 16)
            sp.dma_start(uq[:, :, :], u_g[0]).then_inc(q_loaded, 16)
            sp.wait_ge(w_split, n_w)
            sp.dma_start(xa[:, :, :], xn_g[0]).then_inc(xa_loaded, 16)

            def do(job, n, g, b, i):
                if job == "turn_x" and n == 1:
                    sp.wait_ge(turn.full, b * TB + 5 + i * 4 + 4)
                    wait_alone(sp, squared, TG * g + TG, sp_passed)
                    sp.dma_start(uq[:, :, :], u_g[after(g, G)]).then_inc(q_loaded, 16)
                    sp.dma_start(xa[:, :, :], xn_g[after(g, G)]).then_inc(xa_loaded, 16)
                    wait(sp, sum_ready, TG * g)
                    sp.dma_start(xb[:, :, :], xn_g[g]).then_inc(xb_loaded, 16)
                if job == "out" and n == 1:
                    for t in range(TG):
                        sp.wait_ge(gated[t].free, 3 * g + 3)
                    sp.dma_start(r_g[g], gate[:, :, :]).then_inc(r_stored, 16)
                if job == "norm":
                    sp.wait_ge(offsets, TG * g + TG)
                    sp.dma_start(y_g[g], y[:, :, :]).then_inc(y_stored, 16)

            def batch_start(b):
                wait_alone(sp, z_floor_ready, b + 1, sp_passed)
                sp.dma_start(kv_in[:, :, :], kv_d[after(b, n_batches)]).then_inc(sums_loaded, 16)
                sp.dma_start(z_in[:, :, :], z_d[after(b, n_batches)]).then_inc(sums_loaded, 16)

            run(sp, do, batch_start)
            sp.wait_ge(r_stored, 16 * G)
            sp.wait_ge(y_stored, 16 * G)
            for s, n in ((q_loaded, G + 1), (xa_loaded, G + 1), (sums_loaded, 2 * (n_batches + 1))):
                sp.wait_ge(s, 16 * n)

        @block.gpsimd
        def _(pool):
            make_identity(pool, ident, ident_made)
            om_clear(pool)
            norm.init(pool)
            pool.memset(ones[:, :], 1.0).then_inc(ones_made, 1)
            pool.memset(f32(kvp.hi[:, :, :, :]), 0.0).then_inc(kvp_cleared, 1)
            pool.memset(f32(kvp.lo[:, :, :, :]), 0.0).then_inc(kvp_cleared, 1)
            pool.wait_ge(consts_loaded, 16 * 4)

            def do(job, n, g, b, i):
                if job == "proj":
                    pool.wait_ge(z_ready, NC * b + NC)
                    for t in range(TG):
                        pool.wait_ge(e_ready[t], NC * g + n + 1)
                        wait(pool, den_ready[t], NC * g + n)
                        pool.tensor_tensor(ez[t][:, :], e[t][n % 2][:, :], z_all[:, n, :], ALU.mult)\
                            .then_inc(ez_ready[t], 1)
                if job == "norm":
                    norm.invert(pool, g)
                    for t in range(TG):
                        pool.wait_ge(y_ready, TG * g + t + 1)
                        pool.tensor_tensor(y[:, t, :], y[:, t, :], gain[:, :], ALU.mult).then_inc(gained, 1)
                        pool.wait_ge(gained, TG * g + t + 1)
                        pool.tensor_tensor(y[:, t, :], y[:, t, :], offset[:, :], ALU.add).then_inc(offsets, 1)

            run(pool, do, lambda b: None)

        @block.scalar
        def _(act):
            om_hi(act)
            hi_w(act)

            def do(job, n, g, b, i):
                if job == "turn_q":
                    if n == 0:
                        act.wait_ge(q_loaded, 16 * g + 16)
                        for t in range(TG):
                            wait(act, sq_ready, TG * g + t)
                            act.activation(squares[:, :], uq[:, t, :], ACT.Square).then_inc(squared, 1)
                    for t in range(TG):
                        wait(act, proj[t].full, NC * g)
                    act.wait_ge(turn.full, b * TB + 5 + i * 4 + n + 1)
                    act.activation(qT.hi[:, 2 * n:2 * n + 2, :], halves(turn), ACT.Copy).then_inc(qT_hi, 1)
                if job == "turn_x":
                    act.wait_ge(turn.full, b * TB + 5 + i * 4 + n + 3)
                    wait(act, carried, g)
                    act.activation(xT[:, 2 * n:2 * n + 2, 1:1 + GT], halves(turn), ACT.Copy).then_inc(turn.free, 1)
                if job == "mix":
                    act.wait_ge(mix_full, 2 * g + n + 1)
                    for t in range(TG):
                        wait(act, gated[t].full, 3 * g - 2 + n)
                    act.activation(mix[n].hi[:, :, :], mixed[:, :, :], ACT.Copy).then_inc(mix_hi, 1)
                if job == "proj":
                    wait(act, probs[1].full, NC * g + max(n - 1, 0))
                    for t in range(TG):
                        act.wait_ge(below_ready[t], NC * g + n + 1)
                        for j in range(HC):
                            last = act.activation(e[t][n % 2][:, j * M:(j + 1) * M], proj[t].t[:, j * M:(j + 1) * M],
                                                  ACT.Exp, bias=below[:, t, n * HC + j:n * HC + j + 1])
                        last.then_inc(e_ready[t], 1)
                if job == "probs":
                    act.wait_ge(probs[n % 2].full, NC * g + n // 2 + 1)
                    wait(act, num_done[n % 2], NC * g + n // 2)
                    act.activation(pT[n % 2].hi[:, :], probs[n % 2].t[:, :], ACT.Copy).then_inc(pT_hi[n % 2], 1)
                if job == "attn":
                    act.wait_ge(num_done[1], NC * g + 2 * n + 2)
                    wait(act, wo_done, TG * g)
                    act.activation(oT.hi[:, 2 * n:2 * n + 2, :], halves(num), ACT.Copy).then_inc(oT_hi, 1)
                if job == "r":
                    act.wait_ge(gated[n].full, 3 * g + 1)
                    wait(act, r_stored, 16 * g)
                    act.activation(gate[:, n, :], gated[n].t[:, :], ACT.Tanh, scale=0.5).then_inc(gated[n].free, 1)
                if job == "k":
                    act.wait_ge(gated[n].full, 3 * g + 2)
                    wait(act, ka_ready, 2 * g + n)
                    act.activation(act_k[:, :, :], halves(gated[n]), ACT.Relu).then_inc(gated[n].free, 1)
                    act.wait_ge(gated[n].free, 3 * g + 2)
                    act.activation(act_k2[:, :, :], act_k[:, :, :], ACT.Square).then_inc(act_k2_ready, 1)
                if job == "norm":
                    act.wait_ge(norm.ready, g + 1)
                    for t in range(TG):
                        act.activation(y[:, t, :], y[:, t, :], ACT.Identity, bias=norm.shift[:, t:t + 1],
                                       scale=norm.rstd[:, t:t + 1]).then_inc(y_ready, 1)

            def batch_start(b):
                act.wait_ge(turn.full, b * TB + 1)
                act.wait_ge(kvp_cleared, 2)
                wait(act, num_done[1], b * (GB * NC))
                for j in range(HC):
                    act.activation(kvp.hi[:, :, j, j * KD:(j + 1) * KD],
                                   turn.t[:, :].rearrange("p (c n) -> p c n", c=NC)[:, :, j * KD:(j + 1) * KD],
                                   ACT.Copy).then_inc(kvp_hi, 1)
                for t in range(TG):
                    wait(act, ez_ready[t], b * (GB * NC))
                for c in range(NC):
                    act.wait_ge(turn.full, b * TB + 2 + c)
                    act.activation(z_all[:, c, :], turn.t[:, :], ACT.Copy, bias=FLOOR * S).then_inc(z_ready, 1)

            run(act, do, batch_start)

        @block.vector
        def _(dve):
            om_lo(dve)
            lo_w(dve)
            dve.wait_ge(consts_loaded, 16 * 4)
            dve.tensor_scalar(rest[:, :, :], mu[:, :, :], -1.0, 1.0, ALU.mult, ALU.add).then_inc(consts_ready, 1)
            dve.wait_ge(consts_ready, 1)

            def do(job, n, g, b, i):
                if job == "turn_q":
                    if n == 0:
                        for t in range(TG):
                            dve.wait_ge(squared, TG * g + t + 1)
                            dve.tensor_reduce(sq[:, t, :], squares[:, :].rearrange("p (h k) -> p h k", h=H), AX.X,
                                              ALU.add).then_inc(sq_ready, 1)
                    dve.wait_ge(qT_hi, 2 * g + n + 1)
                    dve.tensor_tensor(qT.lo[:, 2 * n:2 * n + 2, :], halves(turn), f32(qT.hi[:, 2 * n:2 * n + 2, :]),
                                      ALU.subtract).then_inc(turn.free, 1)
                if job == "mix":
                    if n == 0:
                        dve.wait_ge(turn.free, 4 * g + 4)
                    wait(dve, mix_ready, 2 * g + n)
                    for c in range(NC):
                        dve.tensor_scalar(mixed[:, c, :], xT[:, c, 0:GT], rest[:, n, c:c + 1], None, ALU.mult)\
                            .then_inc(mix_chain, 1)
                    for c in range(NC):
                        dve.wait_ge(mix_chain, (2 * g + n) * NC + c + 1)
                        last = dve.scalar_tensor_tensor(out=mixed[:, c, :], in0=xT[:, c, 1:1 + GT],
                                                        scalar=mu[:, n, c:c + 1], in1=mixed[:, c, :],
                                                        op0=ALU.mult, op1=ALU.add)
                    last.then_inc(mix_full, 1)
                    if n == 1:
                        dve.wait_ge(mix_full, 2 * g + 2)
                        dve.tensor_copy(xT[:, :, 0:1], xT[:, :, GT:GT + 1]).then_inc(carried, 1)
                    dve.wait_ge(mix_hi, 2 * g + n + 1)
                    dve.tensor_tensor(mix[n].lo[:, :, :], mixed[:, :, :], f32(mix[n].hi[:, :, :]), ALU.subtract)\
                        .then_inc(mix_ready, 1)
                if job == "proj":
                    heads = slice(n * HC, (n + 1) * HC)
                    for t in range(TG):
                        dve.wait_ge(proj[t].full, NC * g + n + 1)
                        dve.tensor_reduce(top[:, t, heads], proj[t].t[:, :].rearrange("p (h m) -> p h m", h=HC),
                                          AX.X, ALU.max).then_inc(top_ready[t], 1)
                    for t in range(TG):
                        dve.wait_ge(sq_ready, TG * g + TG)
                        dve.wait_ge(top_ready[t], NC * g + n + 1)
                        dve.scalar_tensor_tensor(out=below[:, t, heads], in0=sq[:, t, heads], scalar=-0.5,
                                                 in1=top[:, t, heads], op0=ALU.mult, op1=ALU.subtract)\
                            .then_inc(below_ready[t], 1)
                if job == "den":
                    heads = slice(n * HC, (n + 1) * HC)
                    if n == 0:
                        dve.wait_ge(z_floor_ready, b + 1)
                    for t in range(TG):
                        dve.wait_ge(ez_ready[t], NC * g + n + 1)
                        dve.tensor_reduce(dsum[:, t, :], ez[t][:, :].rearrange("p (h m) -> p h m", h=HC), AX.X,
                                          ALU.add).then_inc(den_ready[t], 1)
                    for t in range(TG):
                        dve.wait_ge(den_ready[t], NC * g + n + 1)
                        dve.tensor_tensor(den[:, t, :], dsum[:, t, :], z_floor[:, heads], ALU.add)\
                            .then_inc(den_chain[t], 1)
                    for t in range(TG):
                        dve.wait_ge(den_chain[t], 2 * (NC * g + n) + 1)
                        dve.reciprocal(rden[:, t, :], den[:, t, :]).then_inc(den_chain[t], 1)
                    for t in range(TG):
                        dve.wait_ge(den_chain[t], 2 * (NC * g + n) + 2)
                        eh = e[t][n % 2][:, :].rearrange("p (h m) -> p h m", h=HC)
                        dve.scalar_tensor_tensor(out=eh, in0=eh, scalar=FLOOR,
                                                 in1=rden[:, t, :].unsqueeze(2).broadcast_to([P, HC, M]),
                                                 op0=ALU.add, op1=ALU.mult).then_inc(p_ready[t], 1)
                if job == "probs":
                    dve.wait_ge(pT_hi[n % 2], NC * g + n // 2 + 1)
                    dve.tensor_tensor(pT[n % 2].lo[:, :], probs[n % 2].t[:, :], f32(pT[n % 2].hi[:, :]), ALU.subtract)\
                        .then_inc(probs[n % 2].free, 1)
                if job == "attn":
                    dve.wait_ge(oT_hi, 2 * g + n + 1)
                    dve.tensor_tensor(oT.lo[:, 2 * n:2 * n + 2, :], halves(num), f32(oT.hi[:, 2 * n:2 * n + 2, :]),
                                      ALU.subtract).then_inc(num.free, 1)
                if job == "k":
                    dve.wait_ge(act_k2_ready, 2 * g + n + 1)
                    for t in range(TG):
                        wait(dve, gated[t].full, 3 * g)
                    dve.tensor_copy(ka.hi[:, 2 * n:2 * n + 2, :], act_k2[:, :, :]).then_inc(ka_hi, 1)
                    dve.wait_ge(ka_hi, 2 * g + n + 1)
                    dve.tensor_tensor(ka.lo[:, 2 * n:2 * n + 2, :], act_k2[:, :, :],
                                      f32(ka.hi[:, 2 * n:2 * n + 2, :]), ALU.subtract).then_inc(ka_ready, 1)
                if job == "out":
                    dve.wait_ge(gated[n].full, 3 * g + 3)
                    dve.scalar_tensor_tensor(out=gate[:, n, :], in0=gate[:, n, :], scalar=1.0, in1=gated[n].t[:, :],
                                             op0=ALU.add, op1=ALU.mult).then_inc(gated[n].free, 1)
                if job == "wo":
                    dve.wait_ge(wo_done, TG * g + n + 1)
                    if n == 0:
                        dve.wait_ge(xb_loaded, 16 * g + 16)
                        wait(dve, y_stored, 16 * g)
                    dve.tensor_tensor(y[:, n, :], num.t[:, :], xb[:, n, :], ALU.add).then_inc(sum_ready, 1)
                if job == "norm":
                    dve.wait_ge(sum_ready, TG * g + TG)
                    wait(dve, norm.ready, g)
                    norm.reduce(dve, g, [y[:, t, :] for t in range(TG)])

            def batch_start(b):
                wait(dve, carried, b * GB)
                dve.memset(xT[:, :, 0:1], 0.0).then_inc(z_chain, 1)
                dve.wait_ge(kvp_hi, HC * b + HC)
                for j in range(HC):
                    last = dve.tensor_tensor(kvp.lo[:, :, j, j * KD:(j + 1) * KD],
                                             turn.t[:, :].rearrange("p (c n) -> p c n", c=NC)[:, :, j * KD:(j + 1) * KD],
                                             f32(kvp.hi[:, :, j, j * KD:(j + 1) * KD]), ALU.subtract)
                last.then_inc(kvp_ready, 1)
                dve.wait_ge(z_ready, NC * b + NC)
                dve.tensor_reduce(z_heads[:, :], z_all[:, :, :].rearrange("p c (h m) -> p (c h) m", h=HC), AX.X,
                                  ALU.add).then_inc(z_chain, 1)
                dve.wait_ge(z_chain, 2 * b + 2)
                dve.tensor_scalar(z_floor[:, :], z_heads[:, :], FLOOR, None, ALU.mult).then_inc(z_floor_ready, 1)

            run(dve, do, batch_start)

        @block.tensor
        def _(pe):
            om_turn(pe)
            pe.wait_ge(om_ready, 1)
            turn_w(pe)
            pe.wait_ge(ones_made, 1)
            pe.wait_ge(w_split, n_w)

            def do(job, n, g, b, i):
                if job in ("turn_q", "turn_x"):
                    if job == "turn_q":
                        pe.wait_ge(q_loaded, 16 * g + 16)
                        src, k = uq, n
                    else:
                        pe.wait_ge(xa_loaded, 16 * g + 16)
                        src, k = xa, 2 + n
                    wait(pe, turn.free, 4 * g + k)
                    pe.wait_ge(z_ready, NC * b + NC)
                    for c in range(2):
                        for t in range(TG):
                            last = pe.transpose(turn.t[:, c * GT + t * P:c * GT + (t + 1) * P],
                                                src[:, t, (2 * n + c) * P:(2 * n + c + 1) * P], ident[:, :])
                    last.then_inc(turn.full, 1)
                if job == "proj":
                    if n == 0:
                        pe.wait_ge(turn.free, 4 * g + 2)
                    for t in range(TG):
                        wait(pe, e_ready[t], NC * g + n)
                        product(pe, proj[t].t[:, :], qT[:, n, t * P:(t + 1) * P], bd[:, :], start=True, stop=True)\
                            .then_inc(proj[t].full, 1)
                if job == "probs":
                    bank = probs[n % 2]
                    wait(pe, bank.free, NC * g + n // 2)
                    for t in range(TG):
                        pe.wait_ge(p_ready[t], NC * g + n // 2 + 1)
                    for a in range(2):
                        j = 2 * (n % 2) + a
                        for t in range(TG):
                            last = pe.transpose(bank.t[:, a * GT + t * P:a * GT + (t + 1) * P],
                                                e[t][n // 2 % 2][:, j * M:(j + 1) * M], ident[:, :])
                    last.then_inc(bank.full, 1)
                if job == "num":
                    c = n // 2
                    if n == 0:
                        pe.wait_ge(kvp_ready, b + 1)
                    if n == 0:
                        wait(pe, sum_ready, TG * g)
                    if n == 4:
                        pe.wait_ge(num.free, 2 * g + 1)
                    pe.wait_ge(probs[n % 2].free, NC * g + n // 2 + 1)
                    for a in range(2):
                        j = 2 * (n % 2) + a
                        last = product(pe, num.t[:, (c % 2) * GT:(c % 2 + 1) * GT], kvp[:, c, j, :],
                                       pT[n % 2][:, a * GT:(a + 1) * GT], start=j == 0, stop=j == HC - 1)
                    last.then_inc(num_done[n % 2], 1)
                if job == "wo":
                    pe.wait_ge(num.free, 2 * g + 2)
                    wait(pe, sum_ready, TG * g + n)
                    for c in range(NC):
                        last = product(pe, num.t[:, :], oT[:, c, n * P:(n + 1) * P], w["o"][:, c, :],
                                       start=c == 0, stop=c == NC - 1)
                    last.then_inc(wo_done, 1)
                if job == "r":
                    pe.wait_ge(mix_ready, 2 * g + 1)
                    wait(pe, gated[n].free, 3 * g)
                    for c in range(NC):
                        last = product(pe, gated[n].t[:, :], mix[0][:, c, n * P:(n + 1) * P], w["r"][:, c, :],
                                       start=c == 0, stop=c == NC - 1)
                    last.then_inc(gated[n].full, 1)
                if job == "k":
                    pe.wait_ge(mix_ready, 2 * g + 2)
                    pe.wait_ge(gated[n].free, 3 * g + 1)
                    for a in range(2):
                        o = 2 * n + a
                        for c in range(NC):
                            last = product(pe, gated[n].t[:, a * GT:(a + 1) * GT], w["k"][:, c, o * P:(o + 1) * P],
                                           mix[1][:, c, :], start=c == 0, stop=c == NC - 1)
                    last.then_inc(gated[n].full, 1)
                if job == "out":
                    pe.wait_ge(ka_ready, 2 * g + 2)
                    pe.wait_ge(gated[n].free, 3 * g + 2)
                    for c in range(NC):
                        last = product(pe, gated[n].t[:, :], ka[:, c, n * P:(n + 1) * P], w["v"][:, c, :],
                                       start=c == 0, stop=c == NC - 1)
                    last.then_inc(gated[n].full, 1)

            def batch_start(b):
                pe.wait_ge(sums_loaded, b * 32 + 32)
                wait(pe, turn.free, b * (4 * GB))
                for c in range(NC):
                    last = pe.transpose(turn.t[:, c * P:(c + 1) * P], kv_in[:, c, :], ident[:, :])
                last.then_inc(turn.full, 1)
                for c in range(NC):
                    if c == 0:
                        pe.wait_ge(kvp_ready, b + 1)
                    wait(pe, z_ready, NC * b + c)
                    pe.matmul(turn.t[:, :], ones[:, :], z_in[:, c, :], start=True, stop=True).then_inc(turn.full, 1)

            run(pe, do, batch_start)

    mem.end()


def feed_forward_pass(nc, x, w1, b1, w2, b2, ln2_g, ln2_b, y_d, r_d, out, n_groups):
    G = n_groups
    x_g, y_g, r_g, out_g = by_group(x), by_group(y_d), by_group(r_d), by_group(out)
    NH = FC // 2
    HB = 4

    mem = Scope(nc, "ffn_")
    ctx = ExitStack()
    with ctx:
        def sb(name, shape, dt=FP32):
            return ctx.enter_context(mem.sbuf_tensor(name, shape, dt))

        def sem(name):
            return mem.sem(name)

        wa = Pair(mem, ctx, "wa", [P, NC, FF])
        wb = Pair(mem, ctx, "wb", [P, FC, D])
        ident = sb("ident", [P, P])
        bias1 = sb("bias1", [P, FC])
        bias2, gain, offset = sb("bias2", [P, D]), sb("gain2", [P, D]), sb("offset2", [P, D])
        y = sb("y_in", [P, TG, D])
        yb = sb("yb", [P, TG, D])
        s = sb("s", [P, TG, D])
        x_in = sb("x_in", [P, TG, D])
        r_in = sb("r_in", [P, TG, D])
        yT = Pair(mem, ctx, "yT", [P, NC, GT])
        hid = [sb(f"hid{n}", [P, 2, GT]) for n in range(2)]
        hT = [Pair(mem, ctx, f"hT{n}", [P, 2, GT]) for n in range(HB)]
        norm = Norm(mem, ctx, "n2", EPS1)

        turn = [Bank(mem, ctx, f"turn{n}") for n in range(2)]
        hidden = [Bank(mem, ctx, f"hidden{n}") for n in range(HB)]
        result = [Bank(mem, ctx, f"result{t}") for t in range(TG)]

        sp_passed = sem("sp_passed")
        ident_made = sem("ident_made")
        consts_loaded = sem("consts_loaded")
        y_loaded, xr_loaded, yT_hi, yb_ready = sem("y_loaded"), sem("xr_loaded"), sem("yT_hi"), sem("yb_ready")
        gelu_ready = [sem(f"gelu{n}") for n in range(2)]
        h_hi = [sem(f"h_hi{n}") for n in range(2)]
        h_ready = [sem(f"h_ready{n}") for n in range(HB)]
        used = [sem(f"used{n}") for n in range(HB)]
        sum_ready, normed, gained, offsets, base_ready, done, stored = (
            sem("sum_ready"), sem("normed"), sem("gained"), sem("offsets"), sem("base_ready"), sem("done"), sem("stored"))

        stages = [y[:, :, :], yb[:, :, :], s[:, :, :], x_in[:, :, :]]
        stages = [a.rearrange("p t n -> p (t n)") for a in stages]
        pieces = []
        a_view = w1.rearrange("(c p) n -> p c n", p=P)
        b_view = w2.rearrange("(c p) n -> p c n", p=P)
        for h in range(2):
            for c in range(NC):
                cols = slice(h * FF // 2, (h + 1) * FF // 2)
                pieces.append((a_view[:, c, cols], wa[:, c, cols], None))
        n_wa = len(pieces)
        for c in range(0, FC, 2):
            pieces.append((b_view[:, c:c + 2, :], (wb.hi[:, c:c + 2, :], wb.lo[:, c:c + 2, :]), 2))

        def flat(piece):
            src, dst, c = piece
            if c is None:
                return src, dst
            return src, tuple(d.rearrange("p c n -> p (c n)") for d in dst)

        loaded = [sem(f"w3_loaded{n}") for n in range(len(stages))]
        rounded, w_split = sem("w3_rounded"), sem("w3_split")
        ns = len(stages)

        BODY = ([("w1", 0, 0), ("w1", 1, 0), ("w1", 2, 0), ("base", 0, 0)]
                + [job for n in range(3, NH) for job in (("w2", n - 3, 0), ("w1", n, 0))]
                + [("turn", 0, 1), ("w2", NH - 3, 0), ("w2", NH - 2, 0), ("w2", NH - 1, 0), ("end", 0, 0)])

        def run(eng, do):
            do("turn", 0, 0)
            for job, n, lead in BODY:
                do(job, n, lead)
            with eng.Fori(1, G - 1) as g:
                for job, n, lead in BODY:
                    do(job, n, g + lead)
            for job, n, lead in BODY:
                if lead == 0:
                    do(job, n, G - 1)

        block = ctx.enter_context(nc.Block())

        @block.sync
        def _(sp):
            for n, piece in enumerate(pieces):
                wait(sp, w_split, n - ns + 1)
                dst = stages[n % ns]
                if piece[2]:
                    dst = dst.rearrange("p (c n) -> p c n", c=piece[2])
                sp.dma_start(dst, piece[0]).then_inc(loaded[n % ns], 16)
            for dst, src in ((bias2[:, :], row_on_all(b2, D)), (gain[:, :], row_on_all(ln2_g, D)),
                             (offset[:, :], row_on_all(ln2_b, D)), (bias1[:, :], b1.rearrange("(c p) -> p c", p=P))):
                with nc.allow_non_contiguous_dma(reason="one vector of the layer's width"):
                    sp.dma_start(dst, src).then_inc(consts_loaded, 16)
            sp.wait_ge(w_split, len(pieces))
            sp.dma_start(y[:, :, :], y_g[0]).then_inc(y_loaded, 16)

            def do(job, n, g):
                if job == "base":
                    for m in range(2):
                        sp.wait_ge(turn[m].full, g + 1)
                    wait_alone(sp, yb_ready, g + 1, sp_passed)
                    sp.dma_start(y[:, :, :], y_g[after(g, G)]).then_inc(y_loaded, 16)
                    wait_alone(sp, base_ready, g, sp_passed)
                    wait(sp, stored, 16 * g)
                    sp.dma_start(x_in[:, :, :], x_g[g]).then_inc(xr_loaded, 16)
                    sp.dma_start(r_in[:, :, :], r_g[g]).then_inc(xr_loaded, 16)
                if job == "end":
                    sp.wait_ge(done, g + 1)
                    sp.dma_start(out_g[g], x_in[:, :, :]).then_inc(stored, 16)

            run(sp, do)
            sp.wait_ge(y_loaded, 16 * (G + 1))
            sp.wait_ge(stored, 16 * G)

        @block.gpsimd
        def _(pool):
            make_identity(pool, ident, ident_made)
            norm.init(pool)
            pool.wait_ge(consts_loaded, 16 * 4)

            def do(job, n, g):
                if job == "base":
                    pool.wait_ge(y_loaded, 16 * g + 16)
                    wait(pool, sum_ready, TG * g)
                    pool.tensor_tensor(yb[:, :, :], y[:, :, :], bias2[:, :].unsqueeze(1).broadcast_to([P, TG, D]),
                                       ALU.add).then_inc(yb_ready, 1)
                if job == "end":
                    norm.invert(pool, g)
                    pool.wait_ge(normed, TG * g + TG)
                    pool.tensor_tensor(s[:, :, :], s[:, :, :], gain[:, :].unsqueeze(1).broadcast_to([P, TG, D]),
                                       ALU.mult).then_inc(gained, 1)
                    pool.wait_ge(gained, g + 1)
                    pool.tensor_tensor(s[:, :, :], s[:, :, :], offset[:, :].unsqueeze(1).broadcast_to([P, TG, D]),
                                       ALU.add).then_inc(offsets, 1)
                    pool.wait_ge(offsets, g + 1)
                    pool.wait_ge(base_ready, g + 1)
                    pool.tensor_tensor(x_in[:, :, :], s[:, :, :], x_in[:, :, :], ALU.add).then_inc(done, 1)

            run(pool, do)

        @block.scalar
        def _(act):
            for n, piece in enumerate(pieces):
                act.wait_ge(loaded[n % ns], 16 * (n // ns + 1))
                act.activation(flat(piece)[1][0], stages[n % ns], ACT.Copy).then_inc(rounded, 1)
            act.wait_ge(consts_loaded, 16 * 4)

            def do(job, n, g):
                if job == "turn":
                    for m in range(HB):
                        wait(act, hidden[m].full, (NH // HB) * g)
                    for m in range(2):
                        act.wait_ge(turn[m].full, g + 1)
                        act.activation(yT.hi[:, 2 * m:2 * m + 2, :], halves(turn[m]), ACT.Copy).then_inc(yT_hi, 1)
                if job == "w1":
                    bank = hidden[n % HB]
                    act.wait_ge(bank.full, (NH // HB) * g + n // HB + 1)
                    prev = n - 2 if n >= 2 else n - 2 + NH
                    wait(act, h_ready[prev % HB], (NH // HB) * g + (prev // HB + 1 if n >= 2 else 0))
                    for a in range(2):
                        last = act.activation(hid[n % 2][:, a, :], bank.t[:, a * GT:(a + 1) * GT], ACT.Gelu,
                                              bias=bias1[:, 2 * n + a:2 * n + a + 1])
                    last.then_inc(bank.free, 1)
                    act.wait_ge(bank.free, (NH // HB) * g + n // HB + 1)
                    if n < HB:
                        for t in range(TG):
                            wait(act, result[t].full, g)
                    else:
                        act.wait_ge(used[n % HB], (NH // HB - 1) * g + n // HB)
                    act.activation(hT[n % HB].hi[:, :, :], hid[n % 2][:, :, :], ACT.Copy).then_inc(h_hi[n % 2], 1)
                if job == "end":
                    act.wait_ge(norm.ready, g + 1)
                    for t in range(TG):
                        act.activation(s[:, t, :], s[:, t, :], ACT.Identity, bias=norm.shift[:, t:t + 1],
                                       scale=norm.rstd[:, t:t + 1]).then_inc(normed, 1)

            run(act, do)

        @block.vector
        def _(dve):
            for n, piece in enumerate(pieces):
                dst = flat(piece)[1]
                dve.wait_ge(rounded, n + 1)
                dve.tensor_tensor(dst[1], stages[n % ns], f32(dst[0]), ALU.subtract).then_inc(w_split, 1)

            def do(job, n, g):
                if job == "turn":
                    for m in range(2):
                        dve.wait_ge(yT_hi, 2 * g + m + 1)
                        dve.tensor_tensor(yT.lo[:, 2 * m:2 * m + 2, :], halves(turn[m]),
                                          f32(yT.hi[:, 2 * m:2 * m + 2, :]), ALU.subtract).then_inc(turn[m].free, 1)
                if job == "w1":
                    dve.wait_ge(h_hi[n % 2], (NH // 2) * g + n // 2 + 1)
                    dve.tensor_tensor(hT[n % HB].lo[:, :, :], hid[n % 2][:, :, :], f32(hT[n % HB].hi[:, :, :]),
                                      ALU.subtract).then_inc(h_ready[n % HB], 1)
                if job == "base":
                    dve.wait_ge(xr_loaded, 32 * g + 32)
                    dve.scalar_tensor_tensor(out=x_in[:, :, :], in0=r_in[:, :, :], scalar=0.5, in1=x_in[:, :, :],
                                             op0=ALU.mult, op1=ALU.add).then_inc(base_ready, 1)
                if job == "end":
                    for t in range(TG):
                        dve.wait_ge(result[t].full, g + 1)
                        dve.wait_ge(yb_ready, g + 1)
                        wait(dve, done, g)
                        dve.tensor_tensor(s[:, t, :], result[t].t[:, :], yb[:, t, :], ALU.add).then_inc(sum_ready, 1)
                    dve.wait_ge(sum_ready, TG * g + TG)
                    wait(dve, norm.ready, g)
                    norm.reduce(dve, g, [s[:, t, :] for t in range(TG)])

            run(dve, do)

        @block.tensor
        def _(pe):
            pe.wait_ge(ident_made, 2)

            def do(job, n, g):
                if job == "turn":
                    pe.wait_ge(y_loaded, 16 * g + 16)
                    for m in range(2):
                        wait(pe, turn[m].free, g)
                        for c in range(2):
                            for t in range(TG):
                                last = pe.transpose(turn[m].t[:, c * GT + t * P:c * GT + (t + 1) * P],
                                                    y[:, t, (2 * m + c) * P:(2 * m + c + 1) * P], ident[:, :])
                        last.then_inc(turn[m].full, 1)
                if job == "w1":
                    bank = hidden[n % HB]
                    if n == 0:
                        for m in range(2):
                            pe.wait_ge(turn[m].free, g + 1)
                        pe.wait_ge(w_split, len(pieces))
                    wait(pe, bank.free, (NH // HB) * g + n // HB)
                    for a in range(2):
                        o = 2 * n + a
                        for c in range(NC):
                            last = product(pe, bank.t[:, a * GT:(a + 1) * GT], wa[:, c, o * P:(o + 1) * P],
                                           yT[:, c, :], start=c == 0, stop=c == NC - 1)
                    last.then_inc(bank.full, 1)
                if job == "w2":
                    pe.wait_ge(h_ready[n % HB], (NH // HB) * g + n // HB + 1)
                    for t in range(TG):
                        if n == 0:
                            wait(pe, sum_ready, TG * g)
                        for a in range(2):
                            last = product(pe, result[t].t[:, :], hT[n % HB][:, a, t * P:(t + 1) * P],
                                           wb[:, 2 * n + a, :], start=n == 0 and a == 0, stop=n == NH - 1 and a == 1)
                        if n == NH - 1:
                            last.then_inc(result[t].full, 1)
                    if n < NH - HB:
                        last.then_inc(used[n % HB], 1)

            run(pe, do)

    mem.end()


def performer_and_gated_block(nc, x, wq, wk, wv, wo, omega, ln1_g, ln1_b, w1, b1, w2, b2, ln2_g, ln2_b,
                              w_r, w_k, w_v, mu_r, mu_k, out):
    B, S, _ = x.shape
    n_groups = B * S // GT
    rows = [B * S, D]
    x_rows = x.rearrange("b s d -> (b s) d")
    out_rows = out.rearrange("b s d -> (b s) d")
    xn_d = nc.dram_tensor("xn_d", rows, FP32, kind="Internal").ap()
    u_d = nc.dram_tensor("u_d", rows, FP32, kind="Internal").ap()
    y_d = nc.dram_tensor("y_d", rows, FP32, kind="Internal").ap()
    r_d = nc.dram_tensor("r_d", rows, FP32, kind="Internal").ap()
    kv_d = nc.dram_tensor("kv_d", [B, P, NC, M], FP32, kind="Internal").ap()
    z_d = nc.dram_tensor("z_d", [B, P, NC, HC * M], FP32, kind="Internal").ap()
    keys_pass(nc, x_rows, wq, wk, wv, omega, xn_d, u_d, kv_d, z_d, B, S // GT)
    attend_pass(nc, wo, omega, ln1_g, ln1_b, w_r, w_k, w_v, mu_r, mu_k, xn_d, u_d, kv_d, z_d, y_d, r_d,
                B, S // GT)
    feed_forward_pass(nc, x_rows, w1, b1, w2, b2, ln2_g, ln2_b, y_d, r_d, out_rows, n_groups)


_INS = ['L0_attn_x', 'L0_attn_wq', 'L0_attn_wk', 'L0_attn_wv', 'L0_attn_wo', 'L0_attn_omega', 'L0_attn_ln1_g',
        'L0_attn_ln1_b', 'L0_attn_w1', 'L0_attn_b1', 'L0_attn_w2', 'L0_attn_b2', 'L0_attn_ln2_g', 'L0_attn_ln2_b',
        'L0_ffn_W_r', 'L0_ffn_W_k', 'L0_ffn_W_v', 'L0_ffn_mu_r', 'L0_ffn_mu_k']
_OUTS = [((8, 1024, 512), 'float32')]


def kernel(**inputs):
    import numpy as _np
    import concourse.bacc as _bacc
    from concourse import mybir as _mybir
    from concourse.bass_utils import run_bass_kernel_spmd as _run

    nc = _bacc.Bacc("TRN2", target_bir_lowering=False, num_devices=1)
    arrays, args = {}, []
    for name in _INS:
        a = _np.ascontiguousarray(inputs[name])
        arrays[f"in_{name}_dram"] = a
        args.append(nc.dram_tensor(f"in_{name}_dram", a.shape, _mybir.dt.from_np(a.dtype), kind="ExternalInput").ap())
    for i, (shape, dtype) in enumerate(_OUTS):
        dt = _mybir.dt.from_np(_np.dtype(dtype))
        args.append(nc.dram_tensor(f"out_{i}_dram", shape, dt, kind="ExternalOutput").ap())
    performer_and_gated_block(nc, *args)
    r = _run(nc, [arrays], core_ids=[0])
    got = tuple(r.results[0][f"out_{i}_dram"] for i in range(len(_OUTS)))
    return got[0]
```

```python
import concourse.bass as bass
from concourse import mybir
from contextlib import ExitStack

FP32 = mybir.dt.float32
FP32R = mybir.dt.float32r
ALU = mybir.AluOpType
ACT = mybir.ActivationFunctionType
AX = mybir.AxisListType

P = 128
D = 512
H = 16
KD = D // H
M = 128
FF = 2048
NC = D // P
HC = P // KD
FC = FF // P
TG = 2
GT = TG * P
W = D

USCALE = float(KD) ** -0.25
FLOOR = 1e-6 * float(M) ** 0.5
EPS0, EPS1 = 1e-5, 1e-6

TERMS = ((0, 0), (0, 1), (1, 0))


class Scope:

    def __init__(self, nc, name):
        self.nc, self.name, self.sems = nc, name, []

    def sbuf_tensor(self, name, shape, dt):
        return self.nc.sbuf_tensor(self.name + name, shape, dt)

    def psum_tensor(self, name, shape, dt):
        return self.nc.psum_tensor(self.name + name, shape, dt)

    def sem(self, name):
        self.sems.append(self.nc.alloc_semaphore(self.name + name))
        return self.sems[-1]

    def end(self):
        self.nc.all_engine_barrier()
        self.nc.clear_and_free_semaphores(self.sems)
        self.nc.all_engine_barrier()


class Bank:

    def __init__(self, mem, ctx, name):
        self.t = ctx.enter_context(mem.psum_tensor(name, [P, W], FP32))
        self.full = mem.sem(name + "_full")
        self.free = mem.sem(name + "_free")


class Pair:

    def __init__(self, mem, ctx, name, shape):
        self.hi = ctx.enter_context(mem.sbuf_tensor(name + "_hi", shape, FP32R))
        self.lo = ctx.enter_context(mem.sbuf_tensor(name + "_lo", shape, FP32R))

    def __getitem__(self, key):
        return (self.hi[key], self.lo[key])


def f32(ap):
    return ap.bitcast(FP32)


def wait(eng, sem, value):
    if isinstance(value, int) and value <= 0:
        return
    eng.wait_ge(sem, value)


def wait_alone(eng, sem, value, passed):
    wait(eng, sem, value)
    eng.sem_inc(passed, 1)


def product(pe, out, stationary, moving, start, stop):
    for n, (a, b) in enumerate(TERMS):
        last = pe.matmul(out, stationary[a], moving[b], start=start and n == 0,
                         stop=stop and n == len(TERMS) - 1)
    return last


def halves(bank):
    return bank.t[:, :].rearrange("p (a n) -> p a n", a=2)


def by_group(dram):
    return dram.rearrange("(g t p) d -> g p t d", t=TG, p=P)


def row_on_all(vector, n):
    return vector.rearrange("(a n) -> a n", a=1).broadcast_to([P, n])


def make_identity(pool, ident, made):
    pool.memset(ident[:, :], 0.0).then_inc(made, 1)
    pool.wait_ge(made, 1)
    pool.affine_select(out=ident[:, :], in_=ident[:, :], compare_op=ALU.not_equal, fill=1.0, base=0,
                       pattern=[[-1, P]], channel_multiplier=1).then_inc(made, 1)


def split_weights(mem, ctx, name, weights, stages, banks=(), ident=None):
    loaded = [mem.sem(f"{name}_loaded{s}") for s in range(len(stages))]
    turned_full = mem.sem(name + "_turned")
    rounded = mem.sem(name + "_rounded")
    done = mem.sem(name + "_split")
    ns = len(stages)
    steps, through, fills = [], [], 0
    for n, (_, dst, turned) in enumerate(weights):
        if turned:
            for m in range(TG):
                cols = tuple(d[:, :, m * P:(m + 1) * P] for d in dst)
                bank = banks[fills % len(banks)].t[:, :].rearrange("p (c n) -> p c n", c=NC)
                steps.append((n, bank, cols, fills, m))
                fills += 1
        else:
            steps.append((n, stages[n % ns], dst, None, None))
        through.append(len(steps))

    def load(sp):
        for n, (src, _, _) in enumerate(weights):
            if n >= ns:
                sp.wait_ge(done, through[n - ns])
            sp.dma_start(stages[n % ns], src).then_inc(loaded[n % ns], 16)

    def turn(pe):
        for k, (n, _, _, fill, m) in enumerate(steps):
            if fill is None:
                continue
            pe.wait_ge(loaded[n % ns], 16 * (n // ns + 1))
            if fill >= len(banks):
                pe.wait_ge(done, k - len(banks) + 1)
            for c in range(NC):
                last = pe.transpose(banks[fill % len(banks)].t[:, c * P:(c + 1) * P],
                                    stages[n % ns][:, m, c * P:(c + 1) * P], ident[:, :])
            last.then_inc(turned_full, 1)

    def hi(act):
        for n, src, dst, fill, _ in steps:
            if fill is None:
                act.wait_ge(loaded[n % ns], 16 * (n // ns + 1))
            else:
                act.wait_ge(turned_full, fill + 1)
            act.activation(dst[0], src, ACT.Copy).then_inc(rounded, 1)

    def lo(dve):
        for k, (_, src, dst, _, _) in enumerate(steps):
            dve.wait_ge(rounded, k + 1)
            dve.tensor_tensor(dst[1], src, f32(dst[0]), ALU.subtract).then_inc(done, 1)

    return load, turn, hi, lo, done, through


def omega_transposed(mem, ctx, omega, om4, bd, ident, ident_made, bank):
    loaded = mem.sem("omega_loaded")
    cleared = mem.sem("omega_cleared")
    turned = mem.sem("omega_turned")
    rounded = mem.sem("omega_rounded")
    ready = mem.sem("omega_ready")

    def load(sp):
        for j in range(HC):
            sp.dma_start(om4[:, j * KD:(j + 1) * KD], omega).then_inc(loaded, 16)

    def clear(pool):
        pool.memset(f32(bd.hi[:, :]), 0.0).then_inc(cleared, 1)
        pool.memset(f32(bd.lo[:, :]), 0.0).then_inc(cleared, 1)

    def transpose(pe):
        pe.wait_ge(loaded, 16 * HC)
        pe.wait_ge(ident_made, 2)
        pe.transpose(bank.t[:, 0:P], om4[:, :], ident[:, :]).then_inc(turned, 1)

    def hi(act):
        act.wait_ge(turned, 1)
        act.wait_ge(cleared, 2)
        for j in range(HC):
            q = slice(j * KD, (j + 1) * KD)
            last = act.activation(bd.hi[q, j * M:(j + 1) * M], bank.t[q, 0:M], ACT.Copy)
        last.then_inc(rounded, 1)

    def lo(dve):
        dve.wait_ge(rounded, 1)
        for j in range(HC):
            q = slice(j * KD, (j + 1) * KD)
            last = dve.tensor_tensor(bd.lo[q, j * M:(j + 1) * M], bank.t[q, 0:M],
                                     f32(bd.hi[q, j * M:(j + 1) * M]), ALU.subtract)
        last.then_inc(ready, 1)

    return load, clear, transpose, hi, lo, ready


class Norm:

    def __init__(self, mem, ctx, name, eps):
        def sb(n, shape):
            return ctx.enter_context(mem.sbuf_tensor(f"{name}_{n}", shape, FP32))
        self.eps = eps
        self.stats = sb("stats", [P, TG, 6])
        self.mv = sb("mv", [P, TG, 2])
        self.base = sb("base", [P, TG])
        self.negmean = sb("negmean", [P, TG])
        self.power = sb("power", [P, TG])
        self.rstd = sb("rstd", [P, TG])
        self.shift = sb("shift", [P, TG])
        self.chain = mem.sem(name + "_chain")
        self.passed = mem.sem(name + "_passed")
        self.root = mem.sem(name + "_root")
        self.ready = mem.sem(name + "_ready")

    def init(self, pool):
        pool.memset(self.power[:, :], -0.5).then_inc(self.root, 1)

    def reduce(self, dve, g, tiles):
        c, n = self.chain, 6
        for t in range(TG):
            dve.bn_stats(self.stats[:, t, :], tiles[t]).then_inc(c, 1)
        for t in range(TG):
            wait_alone(dve, c, g * n + 1 + t, self.passed)
            dve.bn_aggr(self.mv[:, t, :], self.stats[:, t, :]).then_inc(c, 1)
        dve.wait_ge(c, g * n + 4)
        dve.tensor_scalar(self.base[:, :], self.mv[:, :, 1], self.eps, None, ALU.add).then_inc(c, 1)
        dve.tensor_scalar(self.negmean[:, :], self.mv[:, :, 0], -1.0, None, ALU.mult).then_inc(c, 1)

    def invert(self, pool, g):
        pool.wait_ge(self.chain, g * 6 + 6)
        pool.wait_ge(self.root, g + 1)
        pool.tensor_tensor(self.rstd[:, :], self.base[:, :], self.power[:, :], ALU.pow).then_inc(self.root, 1)
        pool.wait_ge(self.root, g + 2)
        pool.tensor_tensor(self.shift[:, :], self.negmean[:, :], self.rstd[:, :], ALU.mult).then_inc(self.ready, 1)


def after(n, count):
    return (n + 1) & (count - 1)


def keys_pass(nc, x, wq, wk, wv, omega, xn_d, u_d, kv_d, z_d, n_batches, groups_per_batch):
    G = n_batches * groups_per_batch
    GB = groups_per_batch
    x_g, xn_g, u_g = by_group(x), by_group(xn_d), by_group(u_d)

    mem = Scope(nc, "keys_")
    ctx = ExitStack()
    with ctx:
        def sb(name, shape, dt=FP32):
            return ctx.enter_context(mem.sbuf_tensor(name, shape, dt))

        def sem(name):
            return mem.sem(name)

        w = {n: Pair(mem, ctx, "w" + n, [P, NC, D]) for n in "qkv"}
        bd = Pair(mem, ctx, "omegaT", [P, HC * M])
        ident = sb("ident", [P, P])
        om4 = sb("om4", [P, HC * KD])
        xin = sb("xin", [P, TG, D])
        xn = sb("xn", [P, TG, D])
        xT = Pair(mem, ctx, "xT", [P, NC, GT])
        uq = sb("uq", [P, TG, D])
        uk = sb("uk", [P, TG, D])
        squares = [sb(f"squares{t}", [P, D]) for t in range(TG)]
        kT = Pair(mem, ctx, "kT", [P, NC, GT])
        v = Pair(mem, ctx, "v", [P, TG, D])
        sq = sb("sq", [P, TG, H])
        top = sb("top", [P, TG, H])
        below = sb("below", [P, TG, H])
        e = [sb(f"e{t}", [P, HC * M]) for t in range(TG)]
        pk = [[Pair(mem, ctx, f"pk{c}{t}", [P, HC * M]) for t in range(TG)] for c in range(2)]
        kv_sum = sb("kv_sum", [P, NC, M])
        z_sum = sb("z_sum", [P, NC, HC * M])
        norm = Norm(mem, ctx, "n0", EPS0)

        dense = [Bank(mem, ctx, f"dense{t}") for t in range(TG)]
        turn = [Bank(mem, ctx, f"turn{n}") for n in range(2)]
        proj = [Bank(mem, ctx, f"proj{t}") for t in range(TG)]
        kv = [Bank(mem, ctx, f"kv{n}") for n in range(2)]

        sp_passed, pool_passed, dve_passed = sem("sp_passed"), sem("pool_passed"), sem("dve_passed")
        ident_made = sem("ident_made")
        x_loaded, xn_ready, xn_stored = sem("x_loaded"), sem("xn_ready"), sem("xn_stored")
        xT_hi, u_stored = sem("xT_hi"), sem("u_stored")
        kT_hi, v_hi = sem("kT_hi"), sem("v_hi")
        sq_ready = [sem(f"sq_ready{t}") for t in range(TG)]
        top_ready = [sem(f"top_ready{t}") for t in range(TG)]
        below_ready = [sem(f"below_ready{t}") for t in range(TG)]
        e_ready = [sem(f"e_ready{t}") for t in range(TG)]
        pk_hi = [sem(f"pk_hi{t}") for t in range(TG)]
        pk_ready = [sem(f"pk_ready{t}") for t in range(TG)]
        z_added = [sem(f"z_added{t}") for t in range(TG)]
        kv_cleared, z_cleared, sums_stored = sem("kv_cleared"), sem("z_cleared"), sem("sums_stored")

        stages = [uq[:, :, :], uk[:, :, :]]
        halves_of = []
        for n, src in (("k", wk), ("q", wq), ("v", wv)):
            view = src.rearrange("(c p) h k -> p c (h k)", p=P)
            for c in range(0, NC, TG):
                halves_of.append((view[:, c:c + TG, :], w[n][:, c:c + TG, :], False))
        load_w, _, hi_w, lo_w, w_split, _ = split_weights(mem, ctx, "w1", halves_of, stages)
        n_w = len(halves_of)
        om_load, om_clear, om_turn, om_hi, om_lo, om_ready = omega_transposed(
            mem, ctx, omega, om4, bd, ident, ident_made, kv[0])

        BODY = [("x", 0, 2), ("proj", 0, 0), ("top", 0, 0), ("k", 0, 1), ("pk", 0, 0), ("proj", 1, 0), ("top", 1, 0),
                ("k", 1, 1), ("pk", 1, 0), ("kv", 0, 0), ("proj", 2, 0), ("top", 2, 0), ("stats", 0, 2), ("q", 0, 1),
                ("norm", 0, 2), ("pk", 2, 0), ("kv", 1, 0), ("proj", 3, 0), ("top", 3, 0), ("q", 1, 1), ("pk", 3, 0),
                ("kv", 2, 0), ("turn_k", 0, 1), ("turn_k", 1, 1),
                ("v", 0, 1), ("kv", 3, 0), ("v_out", 0, 1), ("v", 1, 1), ("v_out", 1, 1), ("turn_x", 0, 2),
                ("turn_x", 1, 2)]
        HEAD = [("x", 0, 0), ("stats", 0, 0), ("norm", 0, 0), ("turn_x", 0, 0), ("turn_x", 1, 0), ("x", 0, 1),
                ("stats", 0, 1), ("k", 0, 0), ("k", 1, 0), ("norm", 0, 1), ("q", 0, 0), ("q", 1, 0), ("turn_k", 0, 0),
                ("turn_k", 1, 0), ("v", 0, 0), ("v_out", 0, 0), ("v", 1, 0), ("v_out", 1, 0), ("turn_x", 0, 1),
                ("turn_x", 1, 1)]

        def run(eng, do, batch_end):
            def body(g, b, ahead=2):
                for job, n, lead in BODY:
                    if lead <= ahead:
                        do(job, n, g + lead, b)
            for job, n, g in HEAD:
                do(job, n, g, 0)
            body(0, 0)
            with eng.Fori(1, GB) as i:
                body(i, 0)
            batch_end(0)
            with eng.Fori(1, n_batches - 1) as b:
                with eng.Fori(0, GB) as i:
                    body(b * GB + i, b)
                batch_end(b)
            last = n_batches - 1
            with eng.Fori(0, GB - 2) as i:
                body(i + last * GB, last)
            body(G - 2, last, ahead=1)
            body(G - 1, last, ahead=0)
            batch_end(last)

        block = ctx.enter_context(nc.Block())

        @block.sync
        def _(sp):
            om_load(sp)
            load_w(sp)

            def do(job, n, g, b):
                if job == "x":
                    wait(sp, xn_ready, TG * g)
                    sp.dma_start(xin[:, :, :], x_g[g]).then_inc(x_loaded, 16)
                if job == "norm":
                    sp.wait_ge(xn_ready, TG * g + TG)
                    sp.dma_start(xn_g[g], xn[:, :, :]).then_inc(xn_stored, 16)
                if job == "q" and n == 1:
                    for t in range(TG):
                        sp.wait_ge(dense[t].free, 3 * g + 2)
                    sp.dma_start(u_g[g], uq[:, :, :]).then_inc(u_stored, 16)

            def batch_end(b):
                for t in range(TG):
                    wait_alone(sp, z_added[t], (b + 1) * (GB * NC), sp_passed)
                    wait_alone(sp, kv[t].free, (b + 1) * (GB * 2), sp_passed)
                sp.dma_start(z_d[b], z_sum[:, :, :]).then_inc(sums_stored, 16)
                sp.dma_start(kv_d[b], kv_sum[:, :, :]).then_inc(sums_stored, 16)

            run(sp, do, batch_end)
            sp.wait_ge(xn_stored, 16 * G)
            sp.wait_ge(u_stored, 16 * G)
            sp.wait_ge(sums_stored, 32 * n_batches)

        @block.gpsimd
        def _(pool):
            make_identity(pool, ident, ident_made)
            om_clear(pool)
            norm.init(pool)
            pool.memset(z_sum[:, :, :], 0.0).then_inc(z_cleared, 1)

            def do(job, n, g, b):
                if job == "stats":
                    norm.invert(pool, g)
                if job == "proj":
                    pool.wait_ge(z_cleared, b + 1)
                    for t in range(TG):
                        pool.wait_ge(e_ready[t], NC * g + n + 1)
                        wait(pool, z_added[1 - t], NC * g + n + t)
                        pool.tensor_tensor(z_sum[:, n, :], z_sum[:, n, :], e[t][:, :], ALU.add)\
                            .then_inc(z_added[t], 1)

            def batch_end(b):
                wait_alone(pool, sums_stored, b * 32 + 32, pool_passed)
                pool.memset(z_sum[:, :, :], 0.0).then_inc(z_cleared, 1)

            run(pool, do, batch_end)

        @block.scalar
        def _(act):
            om_hi(act)
            hi_w(act)

            def do(job, n, g, b):
                if job == "norm":
                    act.wait_ge(norm.ready, g + 1)
                    for m in range(2):
                        wait(act, turn[m].full, 2 * g - 1)
                    wait(act, xn_stored, 16 * g)
                    for t in range(TG):
                        act.activation(xn[:, t, :], xin[:, t, :], ACT.Identity, bias=norm.shift[:, t:t + 1],
                                       scale=norm.rstd[:, t:t + 1]).then_inc(xn_ready, 1)
                if job == "turn_x":
                    for t in range(TG):
                        wait(act, dense[t].full, 3 * g)
                    act.wait_ge(turn[n].full, 2 * g + 1)
                    act.activation(xT.hi[:, 2 * n:2 * n + 2, :], halves(turn[n]), ACT.Copy).then_inc(xT_hi, 1)
                if job == "q":
                    act.wait_ge(dense[n].full, 3 * g + 2)
                    wait(act, u_stored, 16 * g)
                    act.activation(uq[:, n, :], dense[n].t[:, :], ACT.Copy, scale=USCALE).then_inc(dense[n].free, 1)
                if job == "k":
                    act.wait_ge(dense[n].full, 3 * g + 1)
                    for m in range(2):
                        wait(act, turn[m].full, 2 * g)
                    wait(act, sq_ready[n], g)
                    if isinstance(g, int) and g == 0:
                        act.wait_ge(w_split, n_w)
                    act.activation(uk[:, n, :], dense[n].t[:, :], ACT.Copy, scale=USCALE)
                    act.activation(squares[n][:, :], dense[n].t[:, :], ACT.Square, scale=USCALE)\
                        .then_inc(dense[n].free, 1)
                if job == "v_out":
                    act.wait_ge(dense[n].full, 3 * g + 3)
                    for m in range(2):
                        wait(act, kv[m].full, 2 * g)
                    act.activation(v.hi[:, n, :], dense[n].t[:, :], ACT.Copy).then_inc(v_hi, 1)
                if job == "turn_k":
                    for t in range(TG):
                        wait(act, proj[t].full, NC * g)
                    act.wait_ge(turn[n].full, 2 * g + 2)
                    act.activation(kT.hi[:, 2 * n:2 * n + 2, :], halves(turn[n]), ACT.Copy).then_inc(kT_hi, 1)
                if job == "proj":
                    for t in range(TG):
                        act.wait_ge(below_ready[t], NC * g + n + 1)
                        wait(act, pk_ready[t], NC * g + n)
                        wait(act, z_added[t], NC * g + n)
                        for j in range(HC):
                            last = act.activation(e[t][:, j * M:(j + 1) * M], proj[t].t[:, j * M:(j + 1) * M],
                                                  ACT.Exp, bias=below[:, t, n * HC + j:n * HC + j + 1])
                        last.then_inc(e_ready[t], 1)
                    wait(act, kv[n % 2].full, 2 * g + n // 2)
                    for t in range(TG):
                        act.wait_ge(e_ready[t], NC * g + n + 1)
                        act.activation(pk[n % 2][t].hi[:, :], e[t][:, :], ACT.Copy, bias=FLOOR).then_inc(pk_hi[t], 1)

            run(act, do, lambda b: None)

        @block.vector
        def _(dve):
            dve.memset(kv_sum[:, :, :], 0.0).then_inc(kv_cleared, 1)
            om_lo(dve)
            lo_w(dve)

            def do(job, n, g, b):
                if job == "stats":
                    dve.wait_ge(x_loaded, 16 * g + 16)
                    wait(dve, norm.ready, g)
                    norm.reduce(dve, g, [xin[:, t, :] for t in range(TG)])
                if job == "turn_x":
                    dve.wait_ge(xT_hi, 2 * g + n + 1)
                    dve.tensor_tensor(xT.lo[:, 2 * n:2 * n + 2, :], halves(turn[n]),
                                      f32(xT.hi[:, 2 * n:2 * n + 2, :]), ALU.subtract).then_inc(turn[n].free, 1)
                if job == "v_out":
                    dve.wait_ge(v_hi, TG * g + n + 1)
                    dve.tensor_tensor(v.lo[:, n, :], dense[n].t[:, :], f32(v.hi[:, n, :]), ALU.subtract)\
                        .then_inc(dense[n].free, 1)
                if job == "turn_k":
                    dve.wait_ge(kT_hi, 2 * g + n + 1)
                    dve.tensor_tensor(kT.lo[:, 2 * n:2 * n + 2, :], halves(turn[n]),
                                      f32(kT.hi[:, 2 * n:2 * n + 2, :]), ALU.subtract).then_inc(turn[n].free, 1)
                    dve.wait_ge(dense[n].free, 3 * g + 1)
                    dve.tensor_reduce(sq[:, n, :], squares[n][:, :].rearrange("p (h k) -> p h k", h=H), AX.X,
                                      ALU.add).then_inc(sq_ready[n], 1)
                if job == "top":
                    heads = slice(n * HC, (n + 1) * HC)
                    for t in range(TG):
                        dve.wait_ge(proj[t].full, NC * g + n + 1)
                        dve.tensor_reduce(top[:, t, heads], proj[t].t[:, :].rearrange("p (h m) -> p h m", h=HC),
                                          AX.X, ALU.max).then_inc(top_ready[t], 1)
                    for t in range(TG):
                        dve.wait_ge(sq_ready[t], g + 1)
                        dve.wait_ge(top_ready[t], NC * g + n + 1)
                        dve.scalar_tensor_tensor(out=below[:, t, heads], in0=sq[:, t, heads], scalar=-0.5,
                                                 in1=top[:, t, heads], op0=ALU.mult, op1=ALU.subtract)\
                            .then_inc(below_ready[t], 1)
                if job == "pk":
                    for t in range(TG):
                        dve.wait_ge(pk_hi[t], NC * g + n + 1)
                        dve.scalar_tensor_tensor(out=pk[n % 2][t].lo[:, :], in0=e[t][:, :], scalar=FLOOR,
                                                 in1=f32(pk[n % 2][t].hi[:, :]), op0=ALU.add, op1=ALU.subtract)\
                            .then_inc(pk_ready[t], 1)
                if job == "kv":
                    bank = kv[n % 2]
                    dve.wait_ge(kv_cleared, b + 1)
                    dve.wait_ge(bank.full, 2 * g + n // 2 + 1)
                    wait(dve, bank.free, 2 * g + n // 2)
                    for j in range(HC):
                        q = slice(j * KD, (j + 1) * KD)
                        last = dve.tensor_tensor(kv_sum[q, n, :], bank.t[q, j * M:(j + 1) * M], kv_sum[q, n, :],
                                                 ALU.add)
                    last.then_inc(bank.free, 1)

            def batch_end(b):
                wait_alone(dve, sums_stored, b * 32 + 32, dve_passed)
                dve.memset(kv_sum[:, :, :], 0.0).then_inc(kv_cleared, 1)

            run(dve, do, batch_end)

        @block.tensor
        def _(pe):
            om_turn(pe)
            pe.wait_ge(om_ready, 1)

            def do(job, n, g, b):
                if job in ("turn_x", "turn_k"):
                    bank, src, fill = (turn[n], xn, 0) if job == "turn_x" else (turn[n], uk, 1)
                    if job == "turn_x":
                        pe.wait_ge(xn_ready, TG * g + TG)
                    else:
                        for t in range(TG):
                            pe.wait_ge(dense[t].free, 3 * g + 1)
                    wait(pe, bank.free, 2 * g + fill)
                    for c in range(2):
                        for t in range(TG):
                            last = pe.transpose(bank.t[:, c * GT + t * P:c * GT + (t + 1) * P],
                                                src[:, t, (2 * n + c) * P:(2 * n + c + 1) * P], ident[:, :])
                    last.then_inc(bank.full, 1)
                if job in ("q", "k", "v"):
                    k = "kqv".index(job)
                    if isinstance(g, int) and g == 0:
                        pe.wait_ge(w_split, (k + 1) * (n_w // 3))
                    for m in range(2):
                        pe.wait_ge(turn[m].free, 2 * g + 1)
                    wait(pe, dense[n].free, 3 * g + k)
                    for c in range(NC):
                        last = product(pe, dense[n].t[:, :], xT[:, c, n * P:(n + 1) * P], w[job][:, c, :],
                                       start=c == 0, stop=c == NC - 1)
                    last.then_inc(dense[n].full, 1)
                if job == "proj":
                    pe.wait_ge(turn[n // 2].free, 2 * g + 2)
                    for t in range(TG):
                        wait(pe, e_ready[t], NC * g + n)
                        product(pe, proj[t].t[:, :], kT[:, n, t * P:(t + 1) * P], bd[:, :], start=True, stop=True)\
                            .then_inc(proj[t].full, 1)
                if job == "kv":
                    wait(pe, kv[n % 2].free, 2 * g + n // 2)
                    for t in range(TG):
                        pe.wait_ge(dense[t].free, 3 * g + 3)
                        pe.wait_ge(pk_ready[t], NC * g + n + 1)
                        last = product(pe, kv[n % 2].t[:, :], v[:, t, n * P:(n + 1) * P], pk[n % 2][t][:, :],
                                       start=t == 0, stop=t == TG - 1)
                    last.then_inc(kv[n % 2].full, 1)

            run(pe, do, lambda b: None)

    mem.end()


def attend_pass(nc, wo, omega, ln1_g, ln1_b, w_r, w_k, w_v, mu_r, mu_k, xn_d, u_d, kv_d, z_d, y_d, r_d,
                n_batches, groups_per_batch):
    G = n_batches * groups_per_batch
    GB = groups_per_batch
    S = GB * GT
    xn_g, u_g, y_g, r_g = by_group(xn_d), by_group(u_d), by_group(y_d), by_group(r_d)

    mem = Scope(nc, "attend_")
    ctx = ExitStack()
    with ctx:
        def sb(name, shape, dt=FP32):
            return ctx.enter_context(mem.sbuf_tensor(name, shape, dt))

        def sem(name):
            return mem.sem(name)

        w = {n: Pair(mem, ctx, "w" + n, [P, NC, D]) for n in ("o", "r", "k", "v")}
        bd = Pair(mem, ctx, "omegaT", [P, HC * M])
        ident = sb("ident", [P, P])
        ones = sb("ones", [P, P])
        gain, offset = sb("gain", [P, D]), sb("offset", [P, D])
        mu = sb("mu", [P, 2, NC])
        uq = sb("uq", [P, TG, D])
        xa = sb("xa", [P, TG, D])
        xb = sb("xb", [P, TG, D])
        y = sb("y", [P, TG, D])
        squares = sb("squares", [P, D])
        qT = Pair(mem, ctx, "qT", [P, NC, GT])
        xT = sb("xTf", [P, NC, 1 + GT])
        diff = sb("diff", [P, NC, GT])
        mixed = sb("mixed", [P, NC, GT])
        mix = [Pair(mem, ctx, f"mix{n}", [P, NC, GT]) for n in range(2)]
        act_k2 = [sb(f"act_k2{n}", [P, 2, GT]) for n in range(2)]
        ka = Pair(mem, ctx, "ka", [P, NC, GT])
        gate = sb("gate", [P, TG, D])
        sq = sb("sq", [P, TG, H])
        top = sb("top", [P, TG, H])
        below = sb("below", [P, TG, H])
        e = [[sb(f"e{t}{c}", [P, HC * M]) for c in range(2)] for t in range(TG)]
        ez = [sb(f"ez{t}", [P, HC * M]) for t in range(TG)]
        dsum = sb("dsum", [P, TG, HC])
        den = sb("den", [P, TG, HC])
        rden = sb("rden", [P, TG, HC])
        pT = [Pair(mem, ctx, f"pT{n}", [P, 2 * GT]) for n in range(2)]
        kvp = Pair(mem, ctx, "kvp", [P, NC, HC, P])
        kv_in = sb("kv_in", [P, NC, M])
        z_in = sb("z_in", [P, NC, HC * M])
        z_all = sb("z_all", [P, NC, HC * M])
        z_floor = sb("z_floor", [P, H])
        z_heads = sb("z_heads", [P, H])
        oT = Pair(mem, ctx, "oT", [P, NC, GT])
        norm = Norm(mem, ctx, "n1", EPS1)

        turn = ctx.enter_context(mem.psum_tensor("turn", [P, W], FP32))
        turn_halves = turn[:, :].rearrange("p (a n) -> p a n", a=2)
        proj = [Bank(mem, ctx, f"proj{t}") for t in range(TG)]
        probs = [Bank(mem, ctx, f"probs{n}") for n in range(2)]
        num = Bank(mem, ctx, "num")
        gated = [Bank(mem, ctx, f"gated{t}") for t in range(TG)]

        sp_passed = sem("sp_passed")
        ident_made = sem("ident_made")
        consts_loaded, ones_made = sem("consts_loaded"), sem("ones_made")
        q_loaded, xa_loaded, xb_loaded = sem("q_loaded"), sem("xa_loaded"), sem("xb_loaded")
        kv_loaded, z_loaded = sem("kv_loaded"), sem("z_loaded")
        q_turned, x_turned, kv_turned, z_turned = sem("q_turned"), sem("x_turned"), sem("kv_turned"), sem("z_turned")
        q_split, x_copied = sem("q_split"), sem("x_copied")
        kvp_cleared, kvp_hi, kvp_ready = sem("kvp_cleared"), sem("kvp_hi"), sem("kvp_ready")
        z_ready, z_chain, z_floor_ready = sem("z_ready"), sem("z_chain"), sem("z_floor_ready")
        squared, sq_ready = sem("squared"), sem("sq_ready")
        qT_hi, carried, diff_ready = sem("qT_hi"), sem("carried"), sem("diff_ready")
        mix_full, mix_hi, mix_ready = sem("mix_full"), sem("mix_hi"), sem("mix_ready")
        act_k2_ready, ka_hi, ka_ready = sem("act_k2_ready"), sem("ka_hi"), sem("ka_ready")
        r_stored = sem("r_stored")
        top_ready = [sem(f"top_ready{t}") for t in range(TG)]
        below_ready = [sem(f"below_ready{t}") for t in range(TG)]
        e_ready = [sem(f"e_ready{t}") for t in range(TG)]
        ez_ready = [sem(f"ez_ready{t}") for t in range(TG)]
        den_chain = [sem(f"den_chain{t}") for t in range(TG)]
        den_ready = [sem(f"den_ready{t}") for t in range(TG)]
        p_ready = [sem(f"p_ready{t}") for t in range(TG)]
        pT_hi = [sem(f"pT_hi{n}") for n in range(2)]
        num_done = [sem(f"num_done{n}") for n in range(2)]
        oT_hi = sem("oT_hi")
        y_ready, gained, offsets, y_stored = sem("y_ready"), sem("gained"), sem("offsets"), sem("y_stored")

        stages = [xa[:, :, :], xb[:, :, :], y[:, :, :]]
        halves_of = []
        for n, src in (("o", wo), ("r", w_r), ("k", w_k), ("v", w_v)):
            view = src.rearrange("(c p) n -> p c n", p=P)
            for c in range(0, NC, TG):
                if n == "o":
                    halves_of.append((view[:, c:c + TG, :], w[n][:, c:c + TG, :], False))
                else:
                    halves_of.append((view[:, c:c + TG, :], w[n][:, :, c * P:(c + TG) * P], True))
        load_w, turn_w, hi_w, lo_w, w_split, w_through = split_weights(
            mem, ctx, "w2", halves_of, stages, gated, ident)
        n_w = w_through[-1]
        om_load, om_clear, om_turn, om_hi, om_lo, om_ready = omega_transposed(
            mem, ctx, omega, squares[:, 0:HC * KD], bd, ident, ident_made, num)

        BODY = [("probs", 0, 0), ("probs", 1, 0), ("proj", 2, 0), ("den", 1, 0), ("wo", 0, -1), ("num", 0, 0),
                ("num", 1, 0), ("turn_q", 0, 1), ("wo", 1, -1), ("z", 0, 1), ("mix", 1, 0), ("stats", 0, -1),
                ("probs", 2, 0), ("turn_q", 1, 1), ("probs", 3, 0), ("proj", 3, 0), ("den", 2, 0), ("r", 0, 0),
                ("sq", 0, 1), ("num", 2, 0), ("num", 3, 0), ("norm", 0, -1), ("attn", 0, 0), ("r", 1, 0),
                ("z", 1, 1), ("sq", 1, 1), ("xb", 0, 0), ("probs", 4, 0), ("probs", 5, 0), ("z", 2, 1), ("k", 0, 0),
                ("proj", 0, 1), ("den", 3, 0), ("z", 3, 1), ("k", 1, 0), ("num", 4, 0), ("num", 5, 0),
                ("z_floor", 0, 1), ("store_y", 0, -1), ("probs", 6, 0), ("turn_x", 0, 1), ("probs", 7, 0),
                ("turn_x", 1, 1), ("diff", 0, 1), ("proj", 1, 1), ("den", 0, 1), ("out", 0, 0), ("num", 6, 0),
                ("num", 7, 0), ("attn", 1, 0), ("mix", 0, 1), ("out", 1, 0), ("store_r", 0, 0), ("kv", 0, 1)]
        HEAD = [(job, n) for job, n, lead in BODY if lead == 1]
        OF_BATCH = ("z", "z_floor", "kv")

        def run(eng, do):
            def body(g, b, first=False, ends=False, final=False):
                for job, n, lead in BODY:
                    if lead < 0 and first or lead > 0 and final or job in OF_BATCH and not ends:
                        continue
                    do(job, n, g + lead, b + 1 if lead > 0 and ends else b, ends)
            for job, n in HEAD:
                do(job, n, 0, 0, False)
            for g in range(GB):
                body(g, 0, first=g == 0, ends=g == GB - 1)
            with eng.Fori(1, n_batches - 1) as b:
                with eng.Fori(0, GB - 1) as i:
                    body(b * GB + i, b)
                body(b * GB + (GB - 1), b, ends=True)
            b = n_batches - 1
            with eng.Fori(0, GB - 1) as i:
                body(i + b * GB, b)
            body(G - 1, b, final=True)
            for job, n, lead in BODY:
                if lead < 0:
                    do(job, n, G - 1, b, False)

        block = ctx.enter_context(nc.Block())

        @block.sync
        def _(sp):
            om_load(sp)
            load_w(sp)
            for dst, src in ((gain[:, :], row_on_all(ln1_g, D)), (offset[:, :], row_on_all(ln1_b, D)),
                             (mu[:, 0, :], mu_r.rearrange("(c p) -> p c", p=P)),
                             (mu[:, 1, :], mu_k.rearrange("(c p) -> p c", p=P))):
                with nc.allow_non_contiguous_dma(reason="one vector of the model width"):
                    sp.dma_start(dst, src).then_inc(consts_loaded, 16)
            sp.dma_start(kv_in[:, :, :], kv_d[0]).then_inc(kv_loaded, 16)
            sp.dma_start(z_in[:, :, :], z_d[0]).then_inc(z_loaded, 16)
            sp.dma_start(uq[:, :, :], u_g[0]).then_inc(q_loaded, 16)
            sp.wait_ge(w_split, n_w)
            sp.dma_start(xa[:, :, :], xn_g[0]).then_inc(xa_loaded, 16)

            def do(job, n, g, b, ends):
                if job == "sq" and n == 1:
                    sp.wait_ge(q_turned, 2 * g + 2)
                    wait_alone(sp, squared, TG * g + TG, sp_passed)
                    sp.dma_start(uq[:, :, :], u_g[after(g, G)]).then_inc(q_loaded, 16)
                if job == "turn_x" and n == 1:
                    wait_alone(sp, x_turned, 2 * g + 2, sp_passed)
                    sp.dma_start(xa[:, :, :], xn_g[after(g, G)]).then_inc(xa_loaded, 16)
                if job == "z" and n == NC - 1:
                    wait_alone(sp, z_turned, NC * b + NC, sp_passed)
                    sp.dma_start(z_in[:, :, :], z_d[after(b, n_batches)]).then_inc(z_loaded, 16)
                if job == "kv":
                    wait_alone(sp, kv_turned, b + 1, sp_passed)
                    sp.dma_start(kv_in[:, :, :], kv_d[after(b, n_batches)]).then_inc(kv_loaded, 16)
                if job == "xb":
                    wait(sp, gated[0].free, 4 * g)
                    wait_alone(sp, gated[1].free, 4 * g, sp_passed)
                    sp.dma_start(xb[:, :, :], xn_g[g]).then_inc(xb_loaded, 16)
                if job == "store_r":
                    for t in range(TG):
                        sp.wait_ge(gated[t].free, 4 * g + 3)
                    sp.dma_start(r_g[g], gate[:, :, :]).then_inc(r_stored, 16)
                if job == "store_y":
                    sp.wait_ge(offsets, TG * g + TG)
                    sp.dma_start(y_g[g], y[:, :, :]).then_inc(y_stored, 16)

            run(sp, do)
            sp.wait_ge(r_stored, 16 * G)
            sp.wait_ge(y_stored, 16 * G)
            for s, n in ((q_loaded, G + 1), (xa_loaded, G + 1), (kv_loaded, n_batches + 1), (z_loaded, n_batches + 1)):
                sp.wait_ge(s, 16 * n)

        @block.gpsimd
        def _(pool):
            make_identity(pool, ident, ident_made)
            om_clear(pool)
            norm.init(pool)
            pool.memset(ones[:, :], 1.0).then_inc(ones_made, 1)
            pool.memset(f32(kvp.hi[:, :, :, :]), 0.0).then_inc(kvp_cleared, 1)
            pool.memset(f32(kvp.lo[:, :, :, :]), 0.0).then_inc(kvp_cleared, 1)
            pool.wait_ge(consts_loaded, 16 * 4)

            def do(job, n, g, b, ends):
                if job == "proj":
                    pool.wait_ge(z_ready, NC * b + n + 1)
                    for t in range(TG):
                        pool.wait_ge(e_ready[t], NC * g + n + 1)
                        wait(pool, den_ready[t], NC * g + n)
                        pool.tensor_tensor(ez[t][:, :], e[t][n % 2][:, :], z_all[:, n, :], ALU.mult)\
                            .then_inc(ez_ready[t], 1)
                if job == "diff":
                    pool.wait_ge(x_copied, 2 * g + 2)
                    pool.wait_ge(carried, g + 1)
                    wait(pool, mix_full, 2 * g)
                    pool.tensor_tensor(diff[:, :, :], xT[:, :, 1:1 + GT], xT[:, :, 0:GT], ALU.subtract)\
                        .then_inc(diff_ready, 1)
                if job == "mix":
                    pool.wait_ge(mix_hi, 2 * g + n + 1)
                    pool.tensor_tensor(mix[n].lo[:, :, :], mixed[:, :, :], f32(mix[n].hi[:, :, :]), ALU.subtract)\
                        .then_inc(mix_ready, 1)
                if job == "k":
                    pool.wait_ge(ka_hi, 2 * g + n + 1)
                    pool.tensor_tensor(ka.lo[:, 2 * n:2 * n + 2, :], act_k2[n][:, :, :],
                                       f32(ka.hi[:, 2 * n:2 * n + 2, :]), ALU.subtract).then_inc(ka_ready, 1)
                if job == "stats":
                    norm.invert(pool, g)
                if job == "norm":
                    for t in range(TG):
                        pool.wait_ge(y_ready, TG * g + t + 1)
                        pool.tensor_tensor(y[:, t, :], y[:, t, :], gain[:, :], ALU.mult).then_inc(gained, 1)
                        pool.wait_ge(gained, TG * g + t + 1)
                        pool.tensor_tensor(y[:, t, :], y[:, t, :], offset[:, :], ALU.add).then_inc(offsets, 1)

            run(pool, do)

        @block.scalar
        def _(act):
            om_hi(act)
            hi_w(act)

            def do(job, n, g, b, ends):
                if job == "sq":
                    act.wait_ge(q_loaded, 16 * g + 16)
                    wait(act, sq_ready, TG * g + n)
                    act.activation(squares[:, :], uq[:, n, :], ACT.Square).then_inc(squared, 1)
                if job == "turn_q":
                    for t in range(TG):
                        wait(act, proj[t].full, NC * g + 2 * n - 2)
                    act.wait_ge(q_turned, 2 * g + n + 1)
                    act.activation(qT.hi[:, 2 * n:2 * n + 2, :], turn_halves, ACT.Copy).then_inc(qT_hi, 1)
                if job == "turn_x":
                    act.wait_ge(x_turned, 2 * g + n + 1)
                    act.wait_ge(carried, g + 1)
                    act.activation(xT[:, 2 * n:2 * n + 2, 1:1 + GT], turn_halves, ACT.Copy).then_inc(x_copied, 1)
                if job == "mix":
                    act.wait_ge(mix_full, 2 * g + n + 1)
                    for t in range(TG):
                        wait(act, gated[t].full, 4 * g - 3 + n)
                    act.activation(mix[n].hi[:, :, :], mixed[:, :, :], ACT.Copy).then_inc(mix_hi, 1)
                if job == "proj":
                    wait(act, probs[1].full, NC * g + n - 1)
                    for t in range(TG):
                        act.wait_ge(below_ready[t], NC * g + n + 1)
                        for j in range(HC):
                            last_exp = act.activation(e[t][n % 2][:, j * M:(j + 1) * M],
                                                      proj[t].t[:, j * M:(j + 1) * M], ACT.Exp,
                                                      bias=below[:, t, n * HC + j:n * HC + j + 1])
                        last_exp.then_inc(e_ready[t], 1)
                if job == "probs":
                    act.wait_ge(probs[n % 2].full, NC * g + n // 2 + 1)
                    wait(act, num_done[n % 2], NC * g + n // 2)
                    act.activation(pT[n % 2].hi[:, :], probs[n % 2].t[:, :], ACT.Copy).then_inc(pT_hi[n % 2], 1)
                if job == "attn":
                    act.wait_ge(num_done[1], NC * g + 2 * n + 2)
                    for t in range(TG):
                        wait(act, gated[t].full, 4 * g)
                    act.activation(oT.hi[:, 2 * n:2 * n + 2, :], halves(num), ACT.Copy).then_inc(oT_hi, 1)
                if job == "r":
                    act.wait_ge(gated[n].full, 4 * g + 1)
                    wait(act, r_stored, 16 * g)
                    act.activation(gate[:, n, :], gated[n].t[:, :], ACT.Tanh, scale=0.5).then_inc(gated[n].free, 1)
                if job == "k":
                    act.wait_ge(gated[n].full, 4 * g + 2)
                    wait(act, ka_ready, 2 * g + n - 1)
                    act.activation(act_k2[n][:, :, :], halves(gated[n]), ACT.Relu).then_inc(gated[n].free, 1)
                    act.wait_ge(gated[n].free, 4 * g + 2)
                    act.activation(act_k2[n][:, :, :], act_k2[n][:, :, :], ACT.Square).then_inc(act_k2_ready, 1)
                    for t in range(TG):
                        wait(act, gated[t].full, 4 * g - 1)
                    act.wait_ge(act_k2_ready, 2 * g + n + 1)
                    act.activation(ka.hi[:, 2 * n:2 * n + 2, :], act_k2[n][:, :, :], ACT.Copy).then_inc(ka_hi, 1)
                if job == "norm":
                    act.wait_ge(norm.ready, g + 1)
                    for t in range(TG):
                        act.activation(y[:, t, :], y[:, t, :], ACT.Identity, bias=norm.shift[:, t:t + 1],
                                       scale=norm.rstd[:, t:t + 1]).then_inc(y_ready, 1)

                if job == "kv":
                    act.wait_ge(kv_turned, b + 1)
                    act.wait_ge(kvp_cleared, 2)
                    wait(act, num_done[1], NC * g)
                    for j in range(HC):
                        act.activation(kvp.hi[:, :, j, j * KD:(j + 1) * KD],
                                       turn[:, :].rearrange("p (c n) -> p c n", c=NC)[:, :, j * KD:(j + 1) * KD],
                                       ACT.Copy).then_inc(kvp_hi, 1)
                if job == "z":
                    for t in range(TG):
                        wait(act, ez_ready[t], NC * (g - 1) + n + 1)
                    act.wait_ge(z_turned, NC * b + n + 1)
                    act.activation(z_all[:, n, :], turn[:, :], ACT.Copy, bias=FLOOR * S).then_inc(z_ready, 1)

            run(act, do)

        @block.vector
        def _(dve):
            om_lo(dve)
            lo_w(dve)
            dve.wait_ge(consts_loaded, 16 * 4)
            dve.memset(xT[:, :, 0:1], 0.0).then_inc(carried, 1)

            def do(job, n, g, b, ends):
                if job == "sq":
                    dve.wait_ge(squared, TG * g + n + 1)
                    dve.tensor_reduce(sq[:, n, :], squares[:, :].rearrange("p (h k) -> p h k", h=H), AX.X,
                                      ALU.add).then_inc(sq_ready, 1)
                if job == "turn_q":
                    dve.wait_ge(qT_hi, 2 * g + n + 1)
                    dve.tensor_tensor(qT.lo[:, 2 * n:2 * n + 2, :], turn_halves, f32(qT.hi[:, 2 * n:2 * n + 2, :]),
                                      ALU.subtract).then_inc(q_split, 1)
                if job == "mix":
                    dve.wait_ge(diff_ready, g + 1)
                    wait(dve, mix_ready, 2 * g + n)
                    for c in range(NC):
                        last_mix = dve.scalar_tensor_tensor(out=mixed[:, c, :], in0=diff[:, c, :],
                                                            scalar=mu[:, n, c:c + 1], in1=xT[:, c, 0:GT],
                                                            op0=ALU.mult, op1=ALU.add)
                    last_mix.then_inc(mix_full, 1)
                    if n == 1 and ends:
                        dve.wait_ge(mix_full, 2 * g + 2)
                        dve.memset(xT[:, :, 0:1], 0.0).then_inc(carried, 1)
                    elif n == 1:
                        dve.wait_ge(mix_full, 2 * g + 2)
                        dve.tensor_copy(xT[:, :, 0:1], xT[:, :, GT:GT + 1]).then_inc(carried, 1)
                if job == "proj":
                    heads = slice(n * HC, (n + 1) * HC)
                    for t in range(TG):
                        dve.wait_ge(proj[t].full, NC * g + n + 1)
                        dve.tensor_reduce(top[:, t, heads], proj[t].t[:, :].rearrange("p (h m) -> p h m", h=HC),
                                          AX.X, ALU.max).then_inc(top_ready[t], 1)
                    for t in range(TG):
                        dve.wait_ge(sq_ready, TG * g + TG)
                        dve.wait_ge(top_ready[t], NC * g + n + 1)
                        dve.scalar_tensor_tensor(out=below[:, t, heads], in0=sq[:, t, heads], scalar=-0.5,
                                                 in1=top[:, t, heads], op0=ALU.mult, op1=ALU.subtract)\
                            .then_inc(below_ready[t], 1)
                if job == "den":
                    heads = slice(n * HC, (n + 1) * HC)
                    dve.wait_ge(z_floor_ready, b + 1)
                    for t in range(TG):
                        dve.wait_ge(ez_ready[t], NC * g + n + 1)
                        dve.tensor_reduce(dsum[:, t, :], ez[t][:, :].rearrange("p (h m) -> p h m", h=HC), AX.X,
                                          ALU.add).then_inc(den_ready[t], 1)
                    for t in range(TG):
                        dve.wait_ge(den_ready[t], NC * g + n + 1)
                        dve.tensor_tensor(den[:, t, :], dsum[:, t, :], z_floor[:, heads], ALU.add)\
                            .then_inc(den_chain[t], 1)
                    for t in range(TG):
                        dve.wait_ge(den_chain[t], 2 * (NC * g + n) + 1)
                        dve.reciprocal(rden[:, t, :], den[:, t, :]).then_inc(den_chain[t], 1)
                    for t in range(TG):
                        dve.wait_ge(den_chain[t], 2 * (NC * g + n) + 2)
                        eh = e[t][n % 2][:, :].rearrange("p (h m) -> p h m", h=HC)
                        dve.scalar_tensor_tensor(out=eh, in0=eh, scalar=FLOOR,
                                                 in1=rden[:, t, :].unsqueeze(2).broadcast_to([P, HC, M]),
                                                 op0=ALU.add, op1=ALU.mult).then_inc(p_ready[t], 1)
                if job == "probs":
                    dve.wait_ge(pT_hi[n % 2], NC * g + n // 2 + 1)
                    dve.tensor_tensor(pT[n % 2].lo[:, :], probs[n % 2].t[:, :], f32(pT[n % 2].hi[:, :]), ALU.subtract)\
                        .then_inc(probs[n % 2].free, 1)
                if job == "attn":
                    dve.wait_ge(oT_hi, 2 * g + n + 1)
                    dve.tensor_tensor(oT.lo[:, 2 * n:2 * n + 2, :], halves(num), f32(oT.hi[:, 2 * n:2 * n + 2, :]),
                                      ALU.subtract).then_inc(num.free, 1)
                if job == "out":
                    dve.wait_ge(gated[n].full, 4 * g + 3)
                    dve.scalar_tensor_tensor(out=gate[:, n, :], in0=gate[:, n, :], scalar=1.0, in1=gated[n].t[:, :],
                                             op0=ALU.add, op1=ALU.mult).then_inc(gated[n].free, 1)
                if job == "wo":
                    dve.wait_ge(gated[n].full, 4 * g + 4)
                    if n == 0:
                        dve.wait_ge(xb_loaded, 16 * g + 16)
                        wait(dve, y_stored, 16 * g)
                    dve.tensor_tensor(y[:, n, :], gated[n].t[:, :], xb[:, n, :], ALU.add)\
                        .then_inc(gated[n].free, 1)
                if job == "stats":
                    for t in range(TG):
                        dve.wait_ge(gated[t].free, 4 * g + 4)
                    wait(dve, norm.ready, g)
                    norm.reduce(dve, g, [y[:, t, :] for t in range(TG)])

                if job == "kv":
                    dve.wait_ge(kvp_hi, HC * b + HC)
                    for j in range(HC):
                        last_kv = dve.tensor_tensor(
                            kvp.lo[:, :, j, j * KD:(j + 1) * KD],
                            turn[:, :].rearrange("p (c n) -> p c n", c=NC)[:, :, j * KD:(j + 1) * KD],
                            f32(kvp.hi[:, :, j, j * KD:(j + 1) * KD]), ALU.subtract)
                    last_kv.then_inc(kvp_ready, 1)
                if job == "z_floor":
                    dve.wait_ge(z_ready, NC * b + NC)
                    dve.tensor_reduce(z_heads[:, :], z_all[:, :, :].rearrange("p c (h m) -> p (c h) m", h=HC), AX.X,
                                      ALU.add).then_inc(z_chain, 1)
                    dve.wait_ge(z_chain, b + 1)
                    dve.tensor_scalar(z_floor[:, :], z_heads[:, :], FLOOR, None, ALU.mult).then_inc(z_floor_ready, 1)

            run(dve, do)

        @block.tensor
        def _(pe):
            om_turn(pe)
            pe.wait_ge(om_ready, 1)
            turn_w(pe)
            pe.wait_ge(ones_made, 1)
            pe.wait_ge(w_split, n_w)

            def do(job, n, g, b, ends):
                if job in ("turn_q", "turn_x"):
                    if job == "turn_q":
                        pe.wait_ge(q_loaded, 16 * g + 16)
                        src, full = uq, q_turned
                        if n == 0:
                            wait(pe, x_copied, 2 * g)
                            if not (isinstance(g, int) and g == 0):
                                pe.wait_ge(kvp_ready, b if ends else b + 1)
                        else:
                            pe.wait_ge(q_split, 2 * g + 1)
                            pe.wait_ge(z_ready, NC * b + 1)
                    else:
                        pe.wait_ge(xa_loaded, 16 * g + 16)
                        src, full = xa, x_turned
                        if n == 0:
                            pe.wait_ge(q_split, 2 * g + 2)
                            pe.wait_ge(z_ready, NC * b + NC)
                        else:
                            pe.wait_ge(x_copied, 2 * g + 1)
                    for c in range(2):
                        for t in range(TG):
                            last_turn = pe.transpose(turn[:, c * GT + t * P:c * GT + (t + 1) * P],
                                                     src[:, t, (2 * n + c) * P:(2 * n + c + 1) * P], ident[:, :])
                    last_turn.then_inc(full, 1)
                if job == "proj":
                    if n % 2 == 0:
                        pe.wait_ge(q_split, 2 * g + n // 2 + 1)
                    for t in range(TG):
                        wait(pe, e_ready[t], NC * g + n)
                        product(pe, proj[t].t[:, :], qT[:, n, t * P:(t + 1) * P], bd[:, :], start=True, stop=True)\
                            .then_inc(proj[t].full, 1)
                if job == "probs":
                    bank = probs[n % 2]
                    wait(pe, bank.free, NC * g + n // 2)
                    for t in range(TG):
                        pe.wait_ge(p_ready[t], NC * g + n // 2 + 1)
                    for a in range(2):
                        j = 2 * (n % 2) + a
                        for t in range(TG):
                            last = pe.transpose(bank.t[:, a * GT + t * P:a * GT + (t + 1) * P],
                                                e[t][n // 2 % 2][:, j * M:(j + 1) * M], ident[:, :])
                    last.then_inc(bank.full, 1)
                if job == "num":
                    c = n // 2
                    if n == 0:
                        pe.wait_ge(kvp_ready, b + 1)
                    if n % 4 == 0:
                        wait(pe, num.free, 2 * g + n // 4)
                    pe.wait_ge(probs[n % 2].free, NC * g + n // 2 + 1)
                    for a in range(2):
                        j = 2 * (n % 2) + a
                        last = product(pe, num.t[:, (c % 2) * GT:(c % 2 + 1) * GT], kvp[:, c, j, :],
                                       pT[n % 2][:, a * GT:(a + 1) * GT], start=j == 0, stop=j == HC - 1)
                    last.then_inc(num_done[n % 2], 1)
                if job == "wo":
                    pe.wait_ge(num.free, 2 * g + 2)
                    pe.wait_ge(gated[n].free, 4 * g + 3)
                    for c in range(NC):
                        last = product(pe, gated[n].t[:, :], oT[:, c, n * P:(n + 1) * P], w["o"][:, c, :],
                                       start=c == 0, stop=c == NC - 1)
                    last.then_inc(gated[n].full, 1)
                if job == "r":
                    pe.wait_ge(mix_ready, 2 * g + 1)
                    wait(pe, gated[n].free, 4 * g)
                    for c in range(NC):
                        last = product(pe, gated[n].t[:, :], mix[0][:, c, n * P:(n + 1) * P], w["r"][:, c, :],
                                       start=c == 0, stop=c == NC - 1)
                    last.then_inc(gated[n].full, 1)
                if job == "k":
                    pe.wait_ge(mix_ready, 2 * g + 2)
                    pe.wait_ge(gated[n].free, 4 * g + 1)
                    for a in range(2):
                        o = 2 * n + a
                        for c in range(NC):
                            last = product(pe, gated[n].t[:, a * GT:(a + 1) * GT], w["k"][:, c, o * P:(o + 1) * P],
                                           mix[1][:, c, :], start=c == 0, stop=c == NC - 1)
                    last.then_inc(gated[n].full, 1)
                if job == "out":
                    pe.wait_ge(ka_ready, 2 * g + 2)
                    pe.wait_ge(gated[n].free, 4 * g + 2)
                    for c in range(NC):
                        last = product(pe, gated[n].t[:, :], ka[:, c, n * P:(n + 1) * P], w["v"][:, c, :],
                                       start=c == 0, stop=c == NC - 1)
                    last.then_inc(gated[n].full, 1)

                if job == "kv":
                    pe.wait_ge(kv_loaded, 16 * b + 16)
                    pe.wait_ge(x_copied, 2 * g + 2)
                    for c in range(NC):
                        last_kv = pe.transpose(turn[:, c * P:(c + 1) * P], kv_in[:, c, :], ident[:, :])
                    last_kv.then_inc(kv_turned, 1)
                if job == "z":
                    pe.wait_ge(z_loaded, 16 * b + 16)
                    pe.wait_ge(q_split, 2 * g + min(n + 1, 2))
                    wait(pe, z_ready, NC * b + n)
                    pe.matmul(turn[:, :], ones[:, :], z_in[:, n, :], start=True, stop=True).then_inc(z_turned, 1)

            run(pe, do)

    mem.end()


def feed_forward_pass(nc, x, w1, b1, w2, b2, ln2_g, ln2_b, y_d, r_d, out, n_groups):
    G = n_groups
    x_g, y_g, r_g, out_g = by_group(x), by_group(y_d), by_group(r_d), by_group(out)
    NH = FC // 2
    HB = 4

    mem = Scope(nc, "ffn_")
    ctx = ExitStack()
    with ctx:
        def sb(name, shape, dt=FP32):
            return ctx.enter_context(mem.sbuf_tensor(name, shape, dt))

        def sem(name):
            return mem.sem(name)

        wa = Pair(mem, ctx, "wa", [P, NC, FF])
        wb = Pair(mem, ctx, "wb", [P, FC, D])
        ident = sb("ident", [P, P])
        bias1 = sb("bias1", [P, FC])
        bias2, gain, offset = sb("bias2", [P, D]), sb("gain2", [P, D]), sb("offset2", [P, D])
        y = sb("y_in", [P, TG, D])
        yb = sb("yb", [P, TG, D])
        s = sb("s", [P, TG, D])
        x_in = sb("x_in", [P, TG, D])
        r_in = sb("r_in", [P, TG, D])
        yT = Pair(mem, ctx, "yT", [P, NC, GT])
        hid = [sb(f"hid{n}", [P, 2, GT]) for n in range(2)]
        hT = [Pair(mem, ctx, f"hT{n}", [P, 2, GT]) for n in range(HB)]
        norm = Norm(mem, ctx, "n2", EPS1)

        turn = [Bank(mem, ctx, f"turn{n}") for n in range(2)]
        hidden = [Bank(mem, ctx, f"hidden{n}") for n in range(HB)]
        result = [Bank(mem, ctx, f"result{t}") for t in range(TG)]

        sp_passed = sem("sp_passed")
        ident_made = sem("ident_made")
        consts_loaded = sem("consts_loaded")
        y_loaded, xr_loaded, yT_hi, yb_ready = sem("y_loaded"), sem("xr_loaded"), sem("yT_hi"), sem("yb_ready")
        gelu_ready = [sem(f"gelu{n}") for n in range(2)]
        h_hi = [sem(f"h_hi{n}") for n in range(2)]
        h_ready = [sem(f"h_ready{n}") for n in range(HB)]
        used = [sem(f"used{n}") for n in range(HB)]
        sum_ready, normed, gained, offsets, base_ready, done, stored = (
            sem("sum_ready"), sem("normed"), sem("gained"), sem("offsets"), sem("base_ready"), sem("done"), sem("stored"))

        stages = [y[:, :, :], yb[:, :, :], s[:, :, :], x_in[:, :, :]]
        stages = [a.rearrange("p t n -> p (t n)") for a in stages]
        pieces = []
        a_view = w1.rearrange("(c p) n -> p c n", p=P)
        b_view = w2.rearrange("(c p) n -> p c n", p=P)
        for h in range(2):
            for c in range(NC):
                cols = slice(h * FF // 2, (h + 1) * FF // 2)
                pieces.append((a_view[:, c, cols], wa[:, c, cols], None))
        n_wa = len(pieces)
        for c in range(0, FC, 2):
            pieces.append((b_view[:, c:c + 2, :], (wb.hi[:, c:c + 2, :], wb.lo[:, c:c + 2, :]), 2))

        def flat(piece):
            src, dst, c = piece
            if c is None:
                return src, dst
            return src, tuple(d.rearrange("p c n -> p (c n)") for d in dst)

        loaded = [sem(f"w3_loaded{n}") for n in range(len(stages))]
        rounded, w_split = sem("w3_rounded"), sem("w3_split")
        ns = len(stages)

        BODY = ([("w1", 0, 0), ("w1", 1, 0), ("w1", 2, 0), ("base", 0, 0)]
                + [job for n in range(3, NH) for job in (("w2", n - 3, 0), ("w1", n, 0))]
                + [("turn", 0, 1), ("w2", NH - 3, 0), ("w2", NH - 2, 0), ("w2", NH - 1, 0), ("end", 0, 0)])

        def run(eng, do):
            do("turn", 0, 0)
            for job, n, lead in BODY:
                do(job, n, lead)
            with eng.Fori(1, G - 1) as g:
                for job, n, lead in BODY:
                    do(job, n, g + lead)
            for job, n, lead in BODY:
                if lead == 0:
                    do(job, n, G - 1)

        block = ctx.enter_context(nc.Block())

        @block.sync
        def _(sp):
            for n, piece in enumerate(pieces):
                wait(sp, w_split, n - ns + 1)
                dst = stages[n % ns]
                if piece[2]:
                    dst = dst.rearrange("p (c n) -> p c n", c=piece[2])
                sp.dma_start(dst, piece[0]).then_inc(loaded[n % ns], 16)
            for dst, src in ((bias2[:, :], row_on_all(b2, D)), (gain[:, :], row_on_all(ln2_g, D)),
                             (offset[:, :], row_on_all(ln2_b, D)), (bias1[:, :], b1.rearrange("(c p) -> p c", p=P))):
                with nc.allow_non_contiguous_dma(reason="one vector of the layer's width"):
                    sp.dma_start(dst, src).then_inc(consts_loaded, 16)
            sp.wait_ge(w_split, len(pieces))
            sp.dma_start(y[:, :, :], y_g[0]).then_inc(y_loaded, 16)

            def do(job, n, g):
                if job == "base":
                    for m in range(2):
                        sp.wait_ge(turn[m].full, g + 1)
                    wait_alone(sp, yb_ready, g + 1, sp_passed)
                    sp.dma_start(y[:, :, :], y_g[after(g, G)]).then_inc(y_loaded, 16)
                    wait_alone(sp, base_ready, g, sp_passed)
                    wait(sp, stored, 16 * g)
                    sp.dma_start(x_in[:, :, :], x_g[g]).then_inc(xr_loaded, 16)
                    sp.dma_start(r_in[:, :, :], r_g[g]).then_inc(xr_loaded, 16)
                if job == "end":
                    sp.wait_ge(done, g + 1)
                    sp.dma_start(out_g[g], x_in[:, :, :]).then_inc(stored, 16)

            run(sp, do)
            sp.wait_ge(y_loaded, 16 * (G + 1))
            sp.wait_ge(stored, 16 * G)

        @block.gpsimd
        def _(pool):
            make_identity(pool, ident, ident_made)
            norm.init(pool)
            pool.wait_ge(consts_loaded, 16 * 4)

            def do(job, n, g):
                if job == "base":
                    pool.wait_ge(y_loaded, 16 * g + 16)
                    wait(pool, sum_ready, TG * g)
                    pool.tensor_tensor(yb[:, :, :], y[:, :, :], bias2[:, :].unsqueeze(1).broadcast_to([P, TG, D]),
                                       ALU.add).then_inc(yb_ready, 1)
                if job == "end":
                    norm.invert(pool, g)
                    pool.wait_ge(normed, TG * g + TG)
                    pool.tensor_tensor(s[:, :, :], s[:, :, :], gain[:, :].unsqueeze(1).broadcast_to([P, TG, D]),
                                       ALU.mult).then_inc(gained, 1)
                    pool.wait_ge(gained, g + 1)
                    pool.tensor_tensor(s[:, :, :], s[:, :, :], offset[:, :].unsqueeze(1).broadcast_to([P, TG, D]),
                                       ALU.add).then_inc(offsets, 1)
                    pool.wait_ge(offsets, g + 1)
                    pool.wait_ge(base_ready, g + 1)
                    pool.tensor_tensor(x_in[:, :, :], s[:, :, :], x_in[:, :, :], ALU.add).then_inc(done, 1)

            run(pool, do)

        @block.scalar
        def _(act):
            for n, piece in enumerate(pieces):
                act.wait_ge(loaded[n % ns], 16 * (n // ns + 1))
                act.activation(flat(piece)[1][0], stages[n % ns], ACT.Copy).then_inc(rounded, 1)
            act.wait_ge(consts_loaded, 16 * 4)

            def do(job, n, g):
                if job == "turn":
                    for m in range(HB):
                        wait(act, hidden[m].full, (NH // HB) * g)
                    for m in range(2):
                        act.wait_ge(turn[m].full, g + 1)
                        act.activation(yT.hi[:, 2 * m:2 * m + 2, :], halves(turn[m]), ACT.Copy).then_inc(yT_hi, 1)
                if job == "w1":
                    bank = hidden[n % HB]
                    act.wait_ge(bank.full, (NH // HB) * g + n // HB + 1)
                    prev = n - 2 if n >= 2 else n - 2 + NH
                    wait(act, h_ready[prev % HB], (NH // HB) * g + (prev // HB + 1 if n >= 2 else 0))
                    for a in range(2):
                        last = act.activation(hid[n % 2][:, a, :], bank.t[:, a * GT:(a + 1) * GT], ACT.Gelu,
                                              bias=bias1[:, 2 * n + a:2 * n + a + 1])
                    last.then_inc(bank.free, 1)
                    act.wait_ge(bank.free, (NH // HB) * g + n // HB + 1)
                    if n < HB:
                        for t in range(TG):
                            wait(act, result[t].full, g)
                    else:
                        act.wait_ge(used[n % HB], (NH // HB - 1) * g + n // HB)
                    act.activation(hT[n % HB].hi[:, :, :], hid[n % 2][:, :, :], ACT.Copy).then_inc(h_hi[n % 2], 1)
                if job == "end":
                    act.wait_ge(norm.ready, g + 1)
                    for t in range(TG):
                        act.activation(s[:, t, :], s[:, t, :], ACT.Identity, bias=norm.shift[:, t:t + 1],
                                       scale=norm.rstd[:, t:t + 1]).then_inc(normed, 1)

            run(act, do)

        @block.vector
        def _(dve):
            for n, piece in enumerate(pieces):
                dst = flat(piece)[1]
                dve.wait_ge(rounded, n + 1)
                dve.tensor_tensor(dst[1], stages[n % ns], f32(dst[0]), ALU.subtract).then_inc(w_split, 1)

            def do(job, n, g):
                if job == "turn":
                    for m in range(2):
                        dve.wait_ge(yT_hi, 2 * g + m + 1)
                        dve.tensor_tensor(yT.lo[:, 2 * m:2 * m + 2, :], halves(turn[m]),
                                          f32(yT.hi[:, 2 * m:2 * m + 2, :]), ALU.subtract).then_inc(turn[m].free, 1)
                if job == "w1":
                    dve.wait_ge(h_hi[n % 2], (NH // 2) * g + n // 2 + 1)
                    dve.tensor_tensor(hT[n % HB].lo[:, :, :], hid[n % 2][:, :, :], f32(hT[n % HB].hi[:, :, :]),
                                      ALU.subtract).then_inc(h_ready[n % HB], 1)
                if job == "base":
                    dve.wait_ge(xr_loaded, 32 * g + 32)
                    dve.scalar_tensor_tensor(out=x_in[:, :, :], in0=r_in[:, :, :], scalar=0.5, in1=x_in[:, :, :],
                                             op0=ALU.mult, op1=ALU.add).then_inc(base_ready, 1)
                if job == "end":
                    for t in range(TG):
                        dve.wait_ge(result[t].full, g + 1)
                        dve.wait_ge(yb_ready, g + 1)
                        wait(dve, done, g)
                        dve.tensor_tensor(s[:, t, :], result[t].t[:, :], yb[:, t, :], ALU.add).then_inc(sum_ready, 1)
                    dve.wait_ge(sum_ready, TG * g + TG)
                    wait(dve, norm.ready, g)
                    norm.reduce(dve, g, [s[:, t, :] for t in range(TG)])

            run(dve, do)

        @block.tensor
        def _(pe):
            pe.wait_ge(ident_made, 2)

            def do(job, n, g):
                if job == "turn":
                    pe.wait_ge(y_loaded, 16 * g + 16)
                    for m in range(2):
                        wait(pe, turn[m].free, g)
                        for c in range(2):
                            for t in range(TG):
                                last = pe.transpose(turn[m].t[:, c * GT + t * P:c * GT + (t + 1) * P],
                                                    y[:, t, (2 * m + c) * P:(2 * m + c + 1) * P], ident[:, :])
                        last.then_inc(turn[m].full, 1)
                if job == "w1":
                    bank = hidden[n % HB]
                    if n == 0:
                        for m in range(2):
                            pe.wait_ge(turn[m].free, g + 1)
                        pe.wait_ge(w_split, len(pieces))
                    wait(pe, bank.free, (NH // HB) * g + n // HB)
                    for a in range(2):
                        o = 2 * n + a
                        for c in range(NC):
                            last = product(pe, bank.t[:, a * GT:(a + 1) * GT], wa[:, c, o * P:(o + 1) * P],
                                           yT[:, c, :], start=c == 0, stop=c == NC - 1)
                    last.then_inc(bank.full, 1)
                if job == "w2":
                    pe.wait_ge(h_ready[n % HB], (NH // HB) * g + n // HB + 1)
                    for t in range(TG):
                        if n == 0:
                            wait(pe, sum_ready, TG * g)
                        for a in range(2):
                            last = product(pe, result[t].t[:, :], hT[n % HB][:, a, t * P:(t + 1) * P],
                                           wb[:, 2 * n + a, :], start=n == 0 and a == 0, stop=n == NH - 1 and a == 1)
                        if n == NH - 1:
                            last.then_inc(result[t].full, 1)
                    if n < NH - HB:
                        last.then_inc(used[n % HB], 1)

            run(pe, do)

    mem.end()


def performer_and_gated_block(nc, x, wq, wk, wv, wo, omega, ln1_g, ln1_b, w1, b1, w2, b2, ln2_g, ln2_b,
                              w_r, w_k, w_v, mu_r, mu_k, out):
    B, S, _ = x.shape
    n_groups = B * S // GT
    rows = [B * S, D]
    x_rows = x.rearrange("b s d -> (b s) d")
    out_rows = out.rearrange("b s d -> (b s) d")
    xn_d = nc.dram_tensor("xn_d", rows, FP32, kind="Internal").ap()
    u_d = nc.dram_tensor("u_d", rows, FP32, kind="Internal").ap()
    y_d = nc.dram_tensor("y_d", rows, FP32, kind="Internal").ap()
    r_d = nc.dram_tensor("r_d", rows, FP32, kind="Internal").ap()
    kv_d = nc.dram_tensor("kv_d", [B, P, NC, M], FP32, kind="Internal").ap()
    z_d = nc.dram_tensor("z_d", [B, P, NC, HC * M], FP32, kind="Internal").ap()
    keys_pass(nc, x_rows, wq, wk, wv, omega, xn_d, u_d, kv_d, z_d, B, S // GT)
    attend_pass(nc, wo, omega, ln1_g, ln1_b, w_r, w_k, w_v, mu_r, mu_k, xn_d, u_d, kv_d, z_d, y_d, r_d,
                B, S // GT)
    feed_forward_pass(nc, x_rows, w1, b1, w2, b2, ln2_g, ln2_b, y_d, r_d, out_rows, n_groups)


_INS = ['L0_attn_x', 'L0_attn_wq', 'L0_attn_wk', 'L0_attn_wv', 'L0_attn_wo', 'L0_attn_omega', 'L0_attn_ln1_g',
        'L0_attn_ln1_b', 'L0_attn_w1', 'L0_attn_b1', 'L0_attn_w2', 'L0_attn_b2', 'L0_attn_ln2_g', 'L0_attn_ln2_b',
        'L0_ffn_W_r', 'L0_ffn_W_k', 'L0_ffn_W_v', 'L0_ffn_mu_r', 'L0_ffn_mu_k']
_OUTS = [((8, 1024, 512), 'float32')]


def kernel(**inputs):
    import numpy as _np
    import concourse.bacc as _bacc
    from concourse import mybir as _mybir
    from concourse.bass_utils import run_bass_kernel_spmd as _run

    nc = _bacc.Bacc("TRN2", target_bir_lowering=False, num_devices=1)
    arrays, args = {}, []
    for name in _INS:
        a = _np.ascontiguousarray(inputs[name])
        arrays[f"in_{name}_dram"] = a
        args.append(nc.dram_tensor(f"in_{name}_dram", a.shape, _mybir.dt.from_np(a.dtype), kind="ExternalInput").ap())
    for i, (shape, dtype) in enumerate(_OUTS):
        dt = _mybir.dt.from_np(_np.dtype(dtype))
        args.append(nc.dram_tensor(f"out_{i}_dram", shape, dt, kind="ExternalOutput").ap())
    performer_and_gated_block(nc, *args)
    r = _run(nc, [arrays], core_ids=[0])
    got = tuple(r.results[0][f"out_{i}_dram"] for i in range(len(_OUTS)))
    return got[0]
```

```python
import concourse.bass as bass
from concourse import mybir
from contextlib import ExitStack

FP32 = mybir.dt.float32
FP32R = mybir.dt.float32r
ALU = mybir.AluOpType
ACT = mybir.ActivationFunctionType
AX = mybir.AxisListType

P = 128
D = 512
H = 16
KD = D // H
M = 128
FF = 2048
NC = D // P
HC = P // KD
FC = FF // P
TG = 2
GT = TG * P
W = D

USCALE = float(KD) ** -0.25
FLOOR = 1e-6 * float(M) ** 0.5
EPS0, EPS1 = 1e-5, 1e-6

TERMS = ((0, 0), (0, 1), (1, 0))


class Scope:

    def __init__(self, nc, name):
        self.nc, self.name, self.sems = nc, name, []

    def sbuf_tensor(self, name, shape, dt):
        return self.nc.sbuf_tensor(self.name + name, shape, dt)

    def psum_tensor(self, name, shape, dt):
        return self.nc.psum_tensor(self.name + name, shape, dt)

    def sem(self, name):
        self.sems.append(self.nc.alloc_semaphore(self.name + name))
        return self.sems[-1]

    def end(self):
        self.nc.all_engine_barrier()
        self.nc.clear_and_free_semaphores(self.sems)
        self.nc.all_engine_barrier()


class Bank:

    def __init__(self, mem, ctx, name):
        self.t = ctx.enter_context(mem.psum_tensor(name, [P, W], FP32))
        self.full = mem.sem(name + "_full")
        self.free = mem.sem(name + "_free")


class Pair:

    def __init__(self, mem, ctx, name, shape):
        self.hi = ctx.enter_context(mem.sbuf_tensor(name + "_hi", shape, FP32R))
        self.lo = ctx.enter_context(mem.sbuf_tensor(name + "_lo", shape, FP32R))

    def __getitem__(self, key):
        return (self.hi[key], self.lo[key])


def f32(ap):
    return ap.bitcast(FP32)


def wait(eng, sem, value):
    if isinstance(value, int) and value <= 0:
        return
    eng.wait_ge(sem, value)


def wait_alone(eng, sem, value, passed):
    wait(eng, sem, value)
    eng.sem_inc(passed, 1)


def product(pe, out, stationary, moving, start, stop):
    for n, (a, b) in enumerate(TERMS):
        last = pe.matmul(out, stationary[a], moving[b], start=start and n == 0,
                         stop=stop and n == len(TERMS) - 1)
    return last


def halves(bank):
    return bank.t[:, :].rearrange("p (a n) -> p a n", a=2)


def by_head(bank):
    return bank[:, :].rearrange("p (h k) -> p h k", h=H)


def by_group(dram):
    return dram.rearrange("(g t p) d -> g p t d", t=TG, p=P)


def row_on_all(vector, n):
    return vector.rearrange("(a n) -> a n", a=1).broadcast_to([P, n])


def make_identity(pool, ident, made):
    pool.memset(ident[:, :], 0.0).then_inc(made, 1)
    pool.wait_ge(made, 1)
    pool.affine_select(out=ident[:, :], in_=ident[:, :], compare_op=ALU.not_equal, fill=1.0, base=0,
                       pattern=[[-1, P]], channel_multiplier=1).then_inc(made, 1)


def split_weights(mem, ctx, name, weights, stages, banks=(), ident=None):
    loaded = [mem.sem(f"{name}_loaded{s}") for s in range(len(stages))]
    turned_full = mem.sem(name + "_turned")
    rounded = mem.sem(name + "_rounded")
    done = mem.sem(name + "_split")
    ns = len(stages)
    steps, through, fills = [], [], 0
    for n, (_, dst, turned) in enumerate(weights):
        if turned:
            for m in range(TG):
                cols = tuple(d[:, :, m * P:(m + 1) * P] for d in dst)
                bank = banks[fills % len(banks)].t[:, :].rearrange("p (c n) -> p c n", c=NC)
                steps.append((n, bank, cols, fills, m))
                fills += 1
        else:
            steps.append((n, stages[n % ns], dst, None, None))
        through.append(len(steps))

    every = range(len(weights))

    def load(sp, part=every):
        for n in part:
            src = weights[n][0]
            if n >= ns:
                sp.wait_ge(done, through[n - ns])
            sp.dma_start(stages[n % ns], src).then_inc(loaded[n % ns], 16)

    def turn(pe, part=every):
        for k, (n, _, _, fill, m) in enumerate(steps):
            if fill is None or n not in part:
                continue
            pe.wait_ge(loaded[n % ns], 16 * (n // ns + 1))
            if fill >= len(banks):
                pe.wait_ge(done, k - len(banks) + 1)
            for c in range(NC):
                last = pe.transpose(banks[fill % len(banks)].t[:, c * P:(c + 1) * P],
                                    stages[n % ns][:, m, c * P:(c + 1) * P], ident[:, :])
            last.then_inc(turned_full, 1)

    def hi(act, part=every):
        for n, src, dst, fill, _ in steps:
            if n not in part:
                continue
            if fill is None:
                act.wait_ge(loaded[n % ns], 16 * (n // ns + 1))
            else:
                act.wait_ge(turned_full, fill + 1)
            act.activation(dst[0], src, ACT.Copy).then_inc(rounded, 1)

    def lo(dve, part=every):
        for k, (n, src, dst, _, _) in enumerate(steps):
            if n not in part:
                continue
            dve.wait_ge(rounded, k + 1)
            dve.tensor_tensor(dst[1], src, f32(dst[0]), ALU.subtract).then_inc(done, 1)

    return load, turn, hi, lo, done, through


def omega_transposed(mem, ctx, omega, om4, bd, ident, ident_made, bank):
    loaded = mem.sem("omega_loaded")
    cleared = mem.sem("omega_cleared")
    turned = mem.sem("omega_turned")
    rounded = mem.sem("omega_rounded")
    ready = mem.sem("omega_ready")

    def load(sp):
        for j in range(HC):
            sp.dma_start(om4[:, j * KD:(j + 1) * KD], omega).then_inc(loaded, 16)

    def clear(pool):
        pool.memset(f32(bd.hi[:, :]), 0.0).then_inc(cleared, 1)
        pool.memset(f32(bd.lo[:, :]), 0.0).then_inc(cleared, 1)

    def transpose(pe):
        pe.wait_ge(loaded, 16 * HC)
        pe.wait_ge(ident_made, 2)
        pe.transpose(bank.t[:, 0:P], om4[:, :], ident[:, :]).then_inc(turned, 1)

    def hi(act):
        act.wait_ge(turned, 1)
        act.wait_ge(cleared, 2)
        for j in range(HC):
            q = slice(j * KD, (j + 1) * KD)
            last = act.activation(bd.hi[q, j * M:(j + 1) * M], bank.t[q, 0:M], ACT.Copy)
        last.then_inc(rounded, 1)

    def lo(dve):
        dve.wait_ge(rounded, 1)
        for j in range(HC):
            q = slice(j * KD, (j + 1) * KD)
            last = dve.tensor_tensor(bd.lo[q, j * M:(j + 1) * M], bank.t[q, 0:M],
                                     f32(bd.hi[q, j * M:(j + 1) * M]), ALU.subtract)
        last.then_inc(ready, 1)

    return load, clear, transpose, hi, lo, ready


class Norm:

    def __init__(self, mem, ctx, name, eps):
        def sb(n, shape):
            return ctx.enter_context(mem.sbuf_tensor(f"{name}_{n}", shape, FP32))
        self.eps = eps
        self.stats = sb("stats", [P, TG, 6])
        self.mv = sb("mv", [P, TG, 2])
        self.base = sb("base", [P, TG])
        self.negmean = sb("negmean", [P, TG])
        self.power = sb("power", [P, TG])
        self.rstd = sb("rstd", [P, TG])
        self.shift = sb("shift", [P, TG])
        self.chain = mem.sem(name + "_chain")
        self.passed = mem.sem(name + "_passed")
        self.root = mem.sem(name + "_root")
        self.ready = mem.sem(name + "_ready")

    def init(self, pool):
        pool.memset(self.power[:, :], -0.5).then_inc(self.root, 1)

    def reduce(self, dve, g, tiles):
        c, n = self.chain, 6
        for t in range(TG):
            dve.bn_stats(self.stats[:, t, :], tiles[t]).then_inc(c, 1)
        for t in range(TG):
            wait_alone(dve, c, g * n + 1 + t, self.passed)
            dve.bn_aggr(self.mv[:, t, :], self.stats[:, t, :]).then_inc(c, 1)
        dve.wait_ge(c, g * n + 4)
        dve.tensor_scalar(self.base[:, :], self.mv[:, :, 1], self.eps, None, ALU.add).then_inc(c, 1)
        dve.tensor_scalar(self.negmean[:, :], self.mv[:, :, 0], -1.0, None, ALU.mult).then_inc(c, 1)

    def invert(self, pool, g):
        pool.wait_ge(self.chain, g * 6 + 6)
        pool.wait_ge(self.root, g + 1)
        pool.tensor_tensor(self.rstd[:, :], self.base[:, :], self.power[:, :], ALU.pow).then_inc(self.root, 1)
        pool.wait_ge(self.root, g + 2)
        pool.tensor_tensor(self.shift[:, :], self.negmean[:, :], self.rstd[:, :], ALU.mult).then_inc(self.ready, 1)


def after(n, count):
    return (n + 1) & (count - 1)


def keys_pass(nc, x, wq, wk, wv, omega, xn_d, xT_d, u_d, kv_d, z_d, n_batches, groups_per_batch):
    G = n_batches * groups_per_batch
    GB = groups_per_batch
    x_g, xn_g, u_g = by_group(x), by_group(xn_d), by_group(u_d)

    mem = Scope(nc, "keys_")
    ctx = ExitStack()
    with ctx:
        def sb(name, shape, dt=FP32):
            return ctx.enter_context(mem.sbuf_tensor(name, shape, dt))

        def sem(name):
            return mem.sem(name)

        w = {n: Pair(mem, ctx, "w" + n, [P, NC, D]) for n in "qkv"}
        bd = Pair(mem, ctx, "omegaT", [P, HC * M])
        ident = sb("ident", [P, P])
        om4 = sb("om4", [P, HC * KD])
        xin = sb("xin", [P, TG, D])
        xn = sb("xn", [P, TG, D])
        xT = Pair(mem, ctx, "xT", [P, NC, GT])
        xT_whole = sb("xT_whole", [P, NC, GT])
        uq = sb("uq", [P, TG, D])
        uk = sb("uk", [P, TG, D])
        squares = [sb(f"squares{t}", [P, D]) for t in range(TG)]
        kT = Pair(mem, ctx, "kT", [P, NC, GT])
        v = sb("v_parts", [P, TG, 2 * D], FP32R)
        v_part = v[:, :, :].rearrange("p t (h s k) -> p t h s k", h=H, s=2)
        sq = sb("sq", [P, TG, H])
        top = sb("top", [P, TG, H])
        below = sb("below", [P, TG, H])
        e = [sb(f"e{t}", [P, HC * M]) for t in range(TG)]
        pk = [[Pair(mem, ctx, f"pk{c}{t}", [P, HC * M]) for t in range(TG)] for c in range(2)]
        kv_sum = sb("kv_sum", [P, H // 2, M])
        z_sum = sb("z_sum", [P, NC, HC * M])
        norm = Norm(mem, ctx, "n0", EPS0)

        dense = [Bank(mem, ctx, f"dense{t}") for t in range(TG)]
        turn = [Bank(mem, ctx, f"turn{n}") for n in range(2)]
        proj = [Bank(mem, ctx, f"proj{t}") for t in range(TG)]
        kv = [Bank(mem, ctx, f"kv{n}") for n in range(2)]

        sp_passed, pool_passed = sem("sp_passed"), sem("pool_passed")
        ident_made = sem("ident_made")
        x_loaded, xn_ready, xn_stored = sem("x_loaded"), sem("xn_ready"), sem("xn_stored")
        xT_hi, u_stored = sem("xT_hi"), sem("u_stored")
        xT_whole_ready, xT_stored = sem("xT_whole_ready"), sem("xT_stored")
        kT_hi, v_hi = sem("kT_hi"), sem("v_hi")
        sq_ready = [sem(f"sq_ready{t}") for t in range(TG)]
        top_ready = [sem(f"top_ready{t}") for t in range(TG)]
        below_ready = [sem(f"below_ready{t}") for t in range(TG)]
        e_ready = [sem(f"e_ready{t}") for t in range(TG)]
        pk_hi = [sem(f"pk_hi{t}") for t in range(TG)]
        pk_ready = [sem(f"pk_ready{t}") for t in range(TG)]
        z_added = [sem(f"z_added{t}") for t in range(TG)]
        sums_stored = sem("sums_stored")

        stages = [sb(f"stage{n}", [P, TG, D])[:, :, :] for n in range(3 * NC // TG)]
        halves_of = []
        for n, src in (("k", wk), ("q", wq), ("v", wv)):
            view = src.rearrange("(c p) h k -> p c (h k)", p=P)
            for c in range(0, NC, TG):
                halves_of.append((view[:, c:c + TG, :], w[n][:, c:c + TG, :], False))
        load_w, _, hi_w, lo_w, w_split, _ = split_weights(mem, ctx, "w1", halves_of, stages)
        n_w = len(halves_of)

        def matrix(n):
            return range(n * n_w // 3, (n + 1) * n_w // 3)

        om_load, om_clear, om_turn, om_hi, om_lo, om_ready = omega_transposed(
            mem, ctx, omega, om4, bd, ident, ident_made, kv[0])

        BODY = [("whole", 0, 1), ("x", 0, 2), ("proj", 0, 0), ("top", 0, 0), ("hi", 0, 0), ("k", 0, 1),
                ("top", 1, 0), ("pk", 0, 0), ("proj", 1, 0), ("hi", 1, 0), ("k", 1, 1), ("proj", 2, 0),
                ("top", 2, 0), ("hi", 2, 0), ("pk", 1, 0), ("kv", 0, 0), ("stats", 0, 2), ("top", 3, 0), ("q", 0, 1),
                ("norm", 0, 2), ("pk", 2, 0), ("kv", 1, 0), ("proj", 3, 0), ("hi", 3, 0), ("q", 1, 1), ("pk", 3, 0),
                ("turn_k", 0, 1), ("turn_k", 1, 1), ("v", 0, 1), ("kv", 2, 0), ("kv", 3, 0), ("v_out", 0, 1),
                ("v", 1, 1), ("v_out", 1, 1), ("turn_x", 0, 2), ("turn_x", 1, 2)]
        HEAD = [("x", 0, 0), ("stats", 0, 0), ("norm", 0, 0), ("turn_x", 0, 0), ("turn_x", 1, 0), ("x", 0, 1),
                ("whole", 0, 0), ("weights", 0, 0), ("weights", 1, 0), ("k", 0, 0), ("weights", 2, 0), ("k", 1, 0),
                ("stats", 0, 1), ("q", 0, 0), ("norm", 0, 1), ("q", 1, 0), ("turn_k", 0, 0), ("turn_k", 1, 0),
                ("v", 0, 0), ("v_out", 0, 0), ("v", 1, 0), ("v_out", 1, 0), ("turn_x", 0, 1), ("turn_x", 1, 1)]

        def run(eng, do, batch_end):
            def body(g, b, ahead=2, first=False):
                for job, n, lead in BODY:
                    if lead <= ahead:
                        do(job, n, g + lead, b, first)
            for job, n, g in HEAD:
                do(job, n, g, 0, False)
            body(0, 0, first=True)
            with eng.Fori(1, GB) as i:
                body(i, 0)
            batch_end(0)
            with eng.Fori(1, n_batches - 1) as b:
                body(b * GB, b, first=True)
                with eng.Fori(1, GB) as i:
                    body(b * GB + i, b)
                batch_end(b)
            last = n_batches - 1
            body(last * GB, last, first=True)
            with eng.Fori(1, GB - 2) as i:
                body(i + last * GB, last)
            body(G - 2, last, ahead=1)
            body(G - 1, last, ahead=0)
            batch_end(last)

        block = ctx.enter_context(nc.Block())

        @block.sync
        def _(sp):
            om_load(sp)

            def do(job, n, g, b, first):
                if job == "x":
                    wait(sp, xn_ready, TG * g)
                    sp.dma_start(xin[:, :, :], x_g[g]).then_inc(x_loaded, 16)
                    if isinstance(g, int) and g == 0:
                        load_w(sp)
                if job == "norm":
                    sp.wait_ge(xn_ready, TG * g + TG)
                    sp.dma_start(xn_g[g], xn[:, :, :]).then_inc(xn_stored, 16)
                if job == "whole":
                    wait_alone(sp, xT_whole_ready, g + 1, sp_passed)
                    sp.dma_start(xT_d[g], xT_whole[:, :, :]).then_inc(xT_stored, 16)
                if job == "q" and n == 1:
                    for t in range(TG):
                        sp.wait_ge(dense[t].free, 3 * g + 2)
                    sp.dma_start(u_g[g], uq[:, :, :]).then_inc(u_stored, 16)

            def batch_end(b):
                for t in range(TG):
                    wait_alone(sp, z_added[t], (b + 1) * (GB * NC), sp_passed)
                    wait_alone(sp, kv[t].free, (b + 1) * (GB * 2), sp_passed)
                sp.dma_start(z_d[b], z_sum[:, :, :]).then_inc(sums_stored, 16)
                sp.dma_start(kv_d[b], kv_sum[:, :, :]).then_inc(sums_stored, 16)

            run(sp, do, batch_end)
            sp.wait_ge(xn_stored, 16 * G)
            sp.wait_ge(xT_stored, 16 * G)
            sp.wait_ge(u_stored, 16 * G)
            sp.wait_ge(sums_stored, 32 * n_batches)

        @block.gpsimd
        def _(pool):
            make_identity(pool, ident, ident_made)
            om_clear(pool)
            norm.init(pool)

            def do(job, n, g, b, first):
                if job == "stats":
                    norm.invert(pool, g)
                if job == "whole":
                    for m in range(2):
                        pool.wait_ge(turn[m].free, 2 * g + 1)
                    wait(pool, xT_stored, 16 * g)
                    pool.tensor_tensor(xT_whole[:, :, :], f32(xT.hi[:, :, :]), f32(xT.lo[:, :, :]), ALU.add)\
                        .then_inc(xT_whole_ready, 1)
                if job == "proj":
                    for t in range(TG):
                        wait(pool, z_added[1 - t], NC * g + n + t)
                        if first and t == 0:
                            if n == 0:
                                wait(pool, sums_stored, b * 32)
                            wait_alone(pool, e_ready[t], NC * g + n + 1, pool_passed)
                            pool.tensor_copy(z_sum[:, n, :], e[t][:, :]).then_inc(z_added[t], 1)
                        else:
                            pool.wait_ge(e_ready[t], NC * g + n + 1)
                            pool.tensor_tensor(z_sum[:, n, :], z_sum[:, n, :], e[t][:, :], ALU.add)\
                                .then_inc(z_added[t], 1)

            run(pool, do, lambda b: None)

        @block.scalar
        def _(act):
            om_hi(act)

            def do(job, n, g, b, first):
                if job == "weights":
                    hi_w(act, matrix(n))
                if job == "norm":
                    act.wait_ge(norm.ready, g + 1)
                    for m in range(2):
                        wait(act, turn[m].full, 2 * g - 1)
                    wait(act, xn_stored, 16 * g)
                    for t in range(TG):
                        act.activation(xn[:, t, :], xin[:, t, :], ACT.Identity, bias=norm.shift[:, t:t + 1],
                                       scale=norm.rstd[:, t:t + 1]).then_inc(xn_ready, 1)
                if job == "turn_x":
                    wait(act, xT_whole_ready, g)
                    act.wait_ge(turn[n].full, 2 * g + 1)
                    for t in range(TG):
                        wait(act, dense[t].full, 3 * g)
                    act.activation(xT.hi[:, 2 * n:2 * n + 2, :], halves(turn[n]), ACT.Copy).then_inc(xT_hi, 1)
                if job == "q":
                    act.wait_ge(dense[n].full, 3 * g + 2)
                    wait(act, u_stored, 16 * g)
                    act.activation(uq[:, n, :], dense[n].t[:, :], ACT.Copy, scale=USCALE).then_inc(dense[n].free, 1)
                if job == "k":
                    act.wait_ge(dense[n].full, 3 * g + 1)
                    for m in range(2):
                        wait(act, turn[m].full, 2 * g)
                    wait(act, sq_ready[n], g)
                    act.activation(uk[:, n, :], dense[n].t[:, :], ACT.Copy, scale=USCALE)
                    act.activation(squares[n][:, :], dense[n].t[:, :], ACT.Square, scale=USCALE)\
                        .then_inc(dense[n].free, 1)
                if job == "v_out":
                    act.wait_ge(dense[n].full, 3 * g + 3)
                    for m in range(2):
                        wait(act, kv[m].full, 2 * g)
                    act.activation(v_part[:, n, :, 0, :], by_head(dense[n].t), ACT.Copy).then_inc(v_hi, 1)
                if job == "turn_k":
                    for t in range(TG):
                        wait(act, proj[t].full, NC * g)
                    act.wait_ge(turn[n].full, 2 * g + 2)
                    act.activation(kT.hi[:, 2 * n:2 * n + 2, :], halves(turn[n]), ACT.Copy).then_inc(kT_hi, 1)
                if job == "proj":
                    for t in range(TG):
                        act.wait_ge(below_ready[t], NC * g + n + 1)
                        wait(act, pk_ready[t], NC * g + n)
                        wait(act, z_added[t], NC * g + n)
                        for j in range(HC):
                            last = act.activation(e[t][:, j * M:(j + 1) * M], proj[t].t[:, j * M:(j + 1) * M],
                                                  ACT.Exp, bias=below[:, t, n * HC + j:n * HC + j + 1])
                        last.then_inc(e_ready[t], 1)
                if job == "hi":
                    wait(act, kv[n % 2].full, 2 * g + n // 2)
                    for t in range(TG):
                        act.wait_ge(e_ready[t], NC * g + n + 1)
                        act.activation(pk[n % 2][t].hi[:, :], e[t][:, :], ACT.Copy, bias=FLOOR).then_inc(pk_hi[t], 1)

            run(act, do, lambda b: None)

        @block.vector
        def _(dve):
            om_lo(dve)

            def do(job, n, g, b, first):
                if job == "weights":
                    lo_w(dve, matrix(n))
                if job == "stats":
                    dve.wait_ge(x_loaded, 16 * g + 16)
                    wait(dve, norm.ready, g)
                    norm.reduce(dve, g, [xin[:, t, :] for t in range(TG)])
                if job == "turn_x":
                    dve.wait_ge(xT_hi, 2 * g + n + 1)
                    dve.tensor_tensor(xT.lo[:, 2 * n:2 * n + 2, :], halves(turn[n]),
                                      f32(xT.hi[:, 2 * n:2 * n + 2, :]), ALU.subtract).then_inc(turn[n].free, 1)
                if job == "v_out":
                    dve.wait_ge(v_hi, TG * g + n + 1)
                    dve.tensor_tensor(v_part[:, n, :, 1, :], by_head(dense[n].t), f32(v_part[:, n, :, 0, :]),
                                      ALU.subtract)\
                        .then_inc(dense[n].free, 1)
                if job == "turn_k":
                    dve.wait_ge(kT_hi, 2 * g + n + 1)
                    dve.tensor_tensor(kT.lo[:, 2 * n:2 * n + 2, :], halves(turn[n]),
                                      f32(kT.hi[:, 2 * n:2 * n + 2, :]), ALU.subtract).then_inc(turn[n].free, 1)
                    dve.wait_ge(dense[n].free, 3 * g + 1)
                    dve.tensor_reduce(sq[:, n, :], squares[n][:, :].rearrange("p (h k) -> p h k", h=H), AX.X,
                                      ALU.add).then_inc(sq_ready[n], 1)
                if job == "top":
                    heads = slice(n * HC, (n + 1) * HC)
                    for t in range(TG):
                        dve.wait_ge(proj[t].full, NC * g + n + 1)
                        dve.tensor_reduce(top[:, t, heads], proj[t].t[:, :].rearrange("p (h m) -> p h m", h=HC),
                                          AX.X, ALU.max).then_inc(top_ready[t], 1)
                    for t in range(TG):
                        dve.wait_ge(sq_ready[t], g + 1)
                        dve.wait_ge(top_ready[t], NC * g + n + 1)
                        dve.scalar_tensor_tensor(out=below[:, t, heads], in0=sq[:, t, heads], scalar=-0.5,
                                                 in1=top[:, t, heads], op0=ALU.mult, op1=ALU.subtract)\
                            .then_inc(below_ready[t], 1)
                if job == "pk":
                    for t in range(TG):
                        dve.wait_ge(pk_hi[t], NC * g + n + 1)
                        dve.scalar_tensor_tensor(out=pk[n % 2][t].lo[:, :], in0=e[t][:, :], scalar=FLOOR,
                                                 in1=f32(pk[n % 2][t].hi[:, :]), op0=ALU.add, op1=ALU.subtract)\
                            .then_inc(pk_ready[t], 1)
                if job == "kv":
                    bank = kv[n % 2]
                    if first and n == 0:
                        wait(dve, sums_stored, b * 32)
                    dve.wait_ge(bank.full, 2 * g + n // 2 + 1)
                    wait(dve, bank.free, 2 * g + n // 2)
                    for a in range(2):
                        rows = slice(a * 2 * KD, (a + 1) * 2 * KD)
                        own = bank.t[rows, :].rearrange("p (q a m) -> p q a m", q=2, a=2)[:, :, a, :]
                        if first:
                            last = dve.tensor_copy(kv_sum[rows, 2 * n:2 * n + 2, :], own)
                        else:
                            last = dve.tensor_tensor(kv_sum[rows, 2 * n:2 * n + 2, :], own,
                                                     kv_sum[rows, 2 * n:2 * n + 2, :], ALU.add)
                    last.then_inc(bank.free, 1)

            run(dve, do, lambda b: None)

        @block.tensor
        def _(pe):
            om_turn(pe)
            pe.wait_ge(om_ready, 1)

            def do(job, n, g, b, first):
                if job in ("turn_x", "turn_k"):
                    bank, src, fill = (turn[n], xn, 0) if job == "turn_x" else (turn[n], uk, 1)
                    if job == "turn_x":
                        pe.wait_ge(xn_ready, TG * g + TG)
                    else:
                        for t in range(TG):
                            pe.wait_ge(dense[t].free, 3 * g + 1)
                    wait(pe, bank.free, 2 * g + fill)
                    for c in range(2):
                        for t in range(TG):
                            last = pe.transpose(bank.t[:, c * GT + t * P:c * GT + (t + 1) * P],
                                                src[:, t, (2 * n + c) * P:(2 * n + c + 1) * P], ident[:, :])
                    last.then_inc(bank.full, 1)
                if job in ("q", "k", "v"):
                    k = "kqv".index(job)
                    if isinstance(g, int) and g == 0:
                        pe.wait_ge(w_split, (k + 1) * (n_w // 3))
                    for m in range(2):
                        pe.wait_ge(turn[m].free, 2 * g + 1)
                    wait(pe, dense[n].free, 3 * g + k)
                    for c in range(NC):
                        last = product(pe, dense[n].t[:, :], xT[:, c, n * P:(n + 1) * P], w[job][:, c, :],
                                       start=c == 0, stop=c == NC - 1)
                    last.then_inc(dense[n].full, 1)
                if job == "proj":
                    pe.wait_ge(turn[n // 2].free, 2 * g + 2)
                    for t in range(TG):
                        wait(pe, e_ready[t], NC * g + n)
                        product(pe, proj[t].t[:, :], kT[:, n, t * P:(t + 1) * P], bd[:, :], start=True, stop=True)\
                            .then_inc(proj[t].full, 1)
                if job == "kv":
                    wait(pe, kv[n % 2].free, 2 * g + n // 2)
                    for t in range(TG):
                        pe.wait_ge(dense[t].free, 3 * g + 3)
                        pe.wait_ge(pk_ready[t], NC * g + n + 1)
                    for q in range(2):
                        cols = slice(q * 2 * M, (q + 1) * 2 * M)
                        for t in range(TG):
                            for s in range(2):
                                last = pe.matmul(kv[n % 2].t[:, cols],
                                                 v[:, t, (2 * n + q) * P:(2 * n + q + 1) * P],
                                                 pk[n % 2][t][:, cols][s], start=t == 0 and s == 0,
                                                 stop=t == TG - 1 and s == 1)
                    last.then_inc(kv[n % 2].full, 1)

            run(pe, do, lambda b: None)

    mem.end()


def attend_pass(nc, wo, omega, ln1_g, ln1_b, w_r, w_k, w_v, mu_r, mu_k, xn_d, xT_d, u_d, kv_d, z_d, y_d, r_d,
                n_batches, groups_per_batch):
    G = n_batches * groups_per_batch
    GB = groups_per_batch
    S = GB * GT
    xn_g, u_g, y_g, r_g = by_group(xn_d), by_group(u_d), by_group(y_d), by_group(r_d)

    mem = Scope(nc, "attend_")
    ctx = ExitStack()
    with ctx:
        def sb(name, shape, dt=FP32):
            return ctx.enter_context(mem.sbuf_tensor(name, shape, dt))

        def sem(name):
            return mem.sem(name)

        w = {n: Pair(mem, ctx, "w" + n, [P, NC, D]) for n in ("o", "r", "k", "v")}
        bd = Pair(mem, ctx, "omegaT", [P, HC * M])
        ident = sb("ident", [P, P])
        ones = sb("ones", [P, P])
        gain, offset = sb("gain", [P, D]), sb("offset", [P, D])
        mu = sb("mu", [P, 2, NC])
        uq = sb("uq", [P, TG, D])
        xb = sb("xb", [P, TG, D])
        y = sb("y", [P, TG, D])
        squares = sb("squares", [P, D])
        qT = Pair(mem, ctx, "qT", [P, NC, GT])
        xT = sb("xTf", [P, NC, 1 + GT])
        diff = sb("diff", [P, NC, GT])
        mixed = sb("mixed", [P, NC, GT])
        mix = [Pair(mem, ctx, f"mix{n}", [P, NC, GT]) for n in range(2)]
        act_k2 = [sb(f"act_k2{n}", [P, 2, GT]) for n in range(2)]
        ka = Pair(mem, ctx, "ka", [P, NC, GT])
        gate = sb("gate", [P, TG, D])
        sq = sb("sq", [P, TG, H])
        top = sb("top", [P, TG, H])
        below = sb("below", [P, TG, H])
        e = [[sb(f"e{t}{c}", [P, HC * M]) for c in range(2)] for t in range(TG)]
        ez = [sb(f"ez{t}", [P, HC * M]) for t in range(TG)]
        dsum = sb("dsum", [P, TG, HC])
        den = sb("den", [P, TG, HC])
        rden = sb("rden", [P, TG, HC])
        pT = [Pair(mem, ctx, f"pT{n}", [P, 2 * GT]) for n in range(2)]
        kvp = Pair(mem, ctx, "kvp", [P, NC, HC, P])
        fold = sb("fold", [P, 2 * KD])
        z_in = sb("z_in", [P, NC, HC * M])
        kv_in = z_in[:, 0:2, :].rearrange("p c (q m) -> p (c q) m", m=M)
        z_all = sb("z_all", [P, NC, HC * M])
        z_floor = sb("z_floor", [P, H])
        z_heads = sb("z_heads", [P, H])
        oT = Pair(mem, ctx, "oT", [P, NC, GT])
        norm = Norm(mem, ctx, "n1", EPS1)

        turn = ctx.enter_context(mem.psum_tensor("turn", [P, W], FP32))
        turn_halves = turn[:, :].rearrange("p (a n) -> p a n", a=2)
        proj = [Bank(mem, ctx, f"proj{t}") for t in range(TG)]
        probs = [Bank(mem, ctx, f"probs{n}") for n in range(2)]
        num = Bank(mem, ctx, "num")
        gated = [Bank(mem, ctx, f"gated{t}") for t in range(TG)]

        sp_passed = sem("sp_passed")
        ident_made = sem("ident_made")
        consts_loaded, ones_made = sem("consts_loaded"), sem("ones_made")
        q_loaded, x_loaded, xb_loaded = sem("q_loaded"), sem("x_loaded"), sem("xb_loaded")
        kv_loaded, z_loaded = sem("kv_loaded"), sem("z_loaded")
        q_turned, kv_turned, z_turned = sem("q_turned"), sem("kv_turned"), sem("z_turned")
        q_split = sem("q_split")
        kvp_cleared, kvp_hi, kvp_ready = sem("kvp_cleared"), sem("kvp_hi"), sem("kvp_ready")
        z_ready, z_chain, z_floor_ready = sem("z_ready"), sem("z_chain"), sem("z_floor_ready")
        squared, sq_ready = sem("squared"), sem("sq_ready")
        qT_hi, carried, diff_ready = sem("qT_hi"), sem("carried"), sem("diff_ready")
        mix_full, mix_hi, mix_ready = sem("mix_full"), sem("mix_hi"), sem("mix_ready")
        act_k2_ready, ka_hi, ka_ready = sem("act_k2_ready"), sem("ka_hi"), sem("ka_ready")
        r_stored = sem("r_stored")
        top_ready = [sem(f"top_ready{t}") for t in range(TG)]
        below_ready = [sem(f"below_ready{t}") for t in range(TG)]
        e_ready = [sem(f"e_ready{t}") for t in range(TG)]
        ez_ready = [sem(f"ez_ready{t}") for t in range(TG)]
        den_chain = [sem(f"den_chain{t}") for t in range(TG)]
        den_ready = [sem(f"den_ready{t}") for t in range(TG)]
        p_ready = [sem(f"p_ready{t}") for t in range(TG)]
        pT_hi = [sem(f"pT_hi{n}") for n in range(2)]
        num_done = [sem(f"num_done{n}") for n in range(2)]
        oT_hi = sem("oT_hi")
        y_ready, gained, offsets, y_stored = sem("y_ready"), sem("gained"), sem("offsets"), sem("y_stored")

        stages = [gate[:, :, :], xb[:, :, :], y[:, :, :]]
        halves_of = []
        for n, src in (("o", wo), ("r", w_r), ("k", w_k), ("v", w_v)):
            view = src.rearrange("(c p) n -> p c n", p=P)
            for c in range(0, NC, TG):
                if n == "o":
                    halves_of.append((view[:, c:c + TG, :], w[n][:, c:c + TG, :], False))
                else:
                    halves_of.append((view[:, c:c + TG, :], w[n][:, :, c * P:(c + TG) * P], True))
        load_w, turn_w, hi_w, lo_w, w_split, w_through = split_weights(
            mem, ctx, "w2", halves_of, stages, gated, ident)
        n_w = w_through[-1]
        om_load, om_clear, om_turn, om_hi, om_lo, om_ready = omega_transposed(
            mem, ctx, omega, squares[:, 0:HC * KD], bd, ident, ident_made, num)

        BODY = [("probs", 1, 0), ("probs", 0, 0), ("proj", 2, 0), ("den", 1, 0), ("wo", 0, -1), ("num", 0, 0),
                ("turn_q", 0, 1), ("mix", 1, 0), ("wo", 1, -1), ("num", 1, 0), ("stats", 0, -1), ("probs", 2, 0),
                ("probs", 3, 0), ("z", 0, 1), ("r", 0, 0), ("proj", 3, 0), ("den", 2, 0), ("turn_q", 1, 1),
                ("sq", 0, 1), ("attn", 0, 0), ("num", 2, 0), ("num", 3, 0), ("norm", 0, -1), ("r", 1, 0),
                ("z", 1, 1), ("probs", 4, 0), ("xb", 0, 0), ("load_x", 0, 1), ("probs", 5, 0), ("sq", 1, 1),
                ("k", 0, 0), ("z", 2, 1), ("proj", 0, 1), ("den", 3, 0), ("z", 3, 1), ("k", 1, 0), ("num", 4, 0),
                ("z_floor", 0, 1), ("store_y", 0, -1), ("num", 5, 0), ("probs", 6, 0), ("probs", 7, 0),
                ("diff", 0, 1), ("proj", 1, 1), ("num", 6, 0), ("mix", 0, 1), ("num", 7, 0), ("den", 0, 1),
                ("out", 0, 0), ("attn", 1, 0), ("kv", 0, 1), ("store_r", 0, 0), ("out", 1, 0)]
        HEAD = []
        for k, (job, n, lead) in enumerate(job for job in BODY if job[2] == 1):
            HEAD.append((job, n))
            if k < len(halves_of):
                HEAD.append(("weights", k))
        OF_BATCH = ("z", "z_floor", "kv")

        def run(eng, do):
            def body(g, b, first=False, ends=False, final=False):
                for job, n, lead in BODY:
                    if lead < 0 and first or lead > 0 and final or job in OF_BATCH and not ends:
                        continue
                    do(job, n, g + lead, b + 1 if lead > 0 and ends else b, ends)
            for job, n in HEAD:
                do(job, n, 0, 0, False)
            for g in range(GB):
                body(g, 0, first=g == 0, ends=g == GB - 1)
            with eng.Fori(1, n_batches - 1) as b:
                with eng.Fori(0, GB - 1) as i:
                    body(b * GB + i, b)
                body(b * GB + (GB - 1), b, ends=True)
            b = n_batches - 1
            with eng.Fori(0, GB - 1) as i:
                body(i + b * GB, b)
            body(G - 1, b, final=True)
            for job, n, lead in BODY:
                if lead < 0:
                    do(job, n, G - 1, b, False)

        block = ctx.enter_context(nc.Block())

        @block.sync
        def _(sp):
            om_load(sp)
            sp.dma_start(uq[:, :, :], u_g[0]).then_inc(q_loaded, 16)
            load_w(sp, range(0, 2))
            sp.dma_start(z_in[:, :, :], z_d[0]).then_inc(z_loaded, 16)
            load_w(sp, range(2, 3))
            for dst, src in ((gain[:, :], row_on_all(ln1_g, D)), (offset[:, :], row_on_all(ln1_b, D)),
                             (mu[:, 0, :], mu_r.rearrange("(c p) -> p c", p=P)),
                             (mu[:, 1, :], mu_k.rearrange("(c p) -> p c", p=P))):
                with nc.allow_non_contiguous_dma(reason="one vector of the model width"):
                    sp.dma_start(dst, src).then_inc(consts_loaded, 16)
            load_w(sp, range(3, len(halves_of)))

            def do(job, n, g, b, ends):
                if job == "sq" and n == 1:
                    sp.wait_ge(q_turned, 2 * g + 2)
                    wait_alone(sp, squared, TG * g + TG, sp_passed)
                    sp.dma_start(uq[:, :, :], u_g[after(g, G)]).then_inc(q_loaded, 16)
                if job == "load_x":
                    wait_alone(sp, carried, g + 1, sp_passed)
                    sp.dma_start(xT[:, :, 1:1 + GT], xT_d[g]).then_inc(x_loaded, 16)
                if job == "z" and n == NC - 1:
                    wait_alone(sp, z_turned, NC * b + NC, sp_passed)
                    sp.dma_start(kv_in, kv_d[b]).then_inc(kv_loaded, 16)
                if job == "kv":
                    wait_alone(sp, kv_turned, b + 1, sp_passed)
                    sp.dma_start(z_in[:, :, :], z_d[after(b, n_batches)]).then_inc(z_loaded, 16)
                if job == "xb":
                    if isinstance(g, int) and g == 0:
                        sp.wait_ge(w_split, n_w)
                    wait(sp, gated[0].free, 4 * g)
                    wait_alone(sp, gated[1].free, 4 * g, sp_passed)
                    sp.dma_start(xb[:, :, :], xn_g[g]).then_inc(xb_loaded, 16)
                if job == "store_r":
                    for t in range(TG):
                        sp.wait_ge(gated[t].free, 4 * g + 3)
                    sp.dma_start(r_g[g], gate[:, :, :]).then_inc(r_stored, 16)
                if job == "store_y":
                    sp.wait_ge(offsets, TG * g + TG)
                    sp.dma_start(y_g[g], y[:, :, :]).then_inc(y_stored, 16)

            run(sp, do)
            sp.wait_ge(r_stored, 16 * G)
            sp.wait_ge(y_stored, 16 * G)
            for s, n in ((q_loaded, G + 1), (kv_loaded, n_batches), (z_loaded, n_batches + 1)):
                sp.wait_ge(s, 16 * n)

        @block.gpsimd
        def _(pool):
            make_identity(pool, ident, ident_made)
            om_clear(pool)
            norm.init(pool)
            pool.memset(ones[:, :], 1.0).then_inc(ones_made, 1)
            pool.wait_ge(ident_made, 2)
            parts = ident[:, :].rearrange("p (a s k) -> p a s k", a=2, s=2)
            pool.tensor_tensor(fold[:, :].rearrange("p (a k) -> p a k", a=2), parts[:, :, 0, :], parts[:, :, 1, :],
                               ALU.add).then_inc(ones_made, 1)
            pool.memset(f32(kvp.hi[:, :, :, :]), 0.0).then_inc(kvp_cleared, 1)
            pool.memset(f32(kvp.lo[:, :, :, :]), 0.0).then_inc(kvp_cleared, 1)

            def do(job, n, g, b, ends):
                if job == "proj":
                    pool.wait_ge(z_ready, NC * b + n + 1)
                    for t in range(TG):
                        pool.wait_ge(e_ready[t], NC * g + n + 1)
                        wait(pool, den_ready[t], NC * g + n)
                        pool.tensor_tensor(ez[t][:, :], e[t][n % 2][:, :], z_all[:, n, :], ALU.mult)\
                            .then_inc(ez_ready[t], 1)
                if job == "diff":
                    pool.wait_ge(x_loaded, 16 * g + 16)
                    pool.wait_ge(carried, g + 1)
                    wait(pool, mix_full, 2 * g)
                    pool.tensor_tensor(diff[:, :, :], xT[:, :, 1:1 + GT], xT[:, :, 0:GT], ALU.subtract)\
                        .then_inc(diff_ready, 1)
                if job == "mix":
                    pool.wait_ge(mix_hi, 2 * g + n + 1)
                    pool.tensor_tensor(mix[n].lo[:, :, :], mixed[:, :, :], f32(mix[n].hi[:, :, :]), ALU.subtract)\
                        .then_inc(mix_ready, 1)
                if job == "k":
                    pool.wait_ge(ka_hi, 2 * g + n + 1)
                    pool.tensor_tensor(ka.lo[:, 2 * n:2 * n + 2, :], act_k2[n][:, :, :],
                                       f32(ka.hi[:, 2 * n:2 * n + 2, :]), ALU.subtract).then_inc(ka_ready, 1)
                if job == "stats":
                    norm.invert(pool, g)
                if job == "norm":
                    if isinstance(g, int) and g == 0:
                        pool.wait_ge(consts_loaded, 16 * 4)
                    for t in range(TG):
                        pool.wait_ge(y_ready, TG * g + t + 1)
                        pool.tensor_tensor(y[:, t, :], y[:, t, :], gain[:, :], ALU.mult).then_inc(gained, 1)
                        pool.wait_ge(gained, TG * g + t + 1)
                        pool.tensor_tensor(y[:, t, :], y[:, t, :], offset[:, :], ALU.add).then_inc(offsets, 1)

            run(pool, do)

        @block.scalar
        def _(act):
            om_hi(act)

            def do(job, n, g, b, ends):
                if job == "weights":
                    hi_w(act, (n,))
                if job == "sq":
                    act.wait_ge(q_loaded, 16 * g + 16)
                    wait(act, sq_ready, TG * g + n)
                    act.activation(squares[:, :], uq[:, n, :], ACT.Square).then_inc(squared, 1)
                if job == "turn_q":
                    for t in range(TG):
                        wait(act, proj[t].full, NC * g + 2 * n - 2)
                    act.wait_ge(q_turned, 2 * g + n + 1)
                    act.activation(qT.hi[:, 2 * n:2 * n + 2, :], turn_halves, ACT.Copy).then_inc(qT_hi, 1)
                if job == "mix":
                    act.wait_ge(mix_full, 2 * g + n + 1)
                    for t in range(TG):
                        wait(act, gated[t].full, 4 * g - 3 + n)
                    act.activation(mix[n].hi[:, :, :], mixed[:, :, :], ACT.Copy).then_inc(mix_hi, 1)
                if job == "proj":
                    wait(act, probs[1].full, NC * g + n - 1)
                    for t in range(TG):
                        act.wait_ge(below_ready[t], NC * g + n + 1)
                        for j in range(HC):
                            last_exp = act.activation(e[t][n % 2][:, j * M:(j + 1) * M],
                                                      proj[t].t[:, j * M:(j + 1) * M], ACT.Exp,
                                                      bias=below[:, t, n * HC + j:n * HC + j + 1])
                        last_exp.then_inc(e_ready[t], 1)
                if job == "probs":
                    act.wait_ge(probs[n % 2].full, NC * g + n // 2 + 1)
                    wait(act, num_done[n % 2], NC * g + n // 2)
                    act.activation(pT[n % 2].hi[:, :], probs[n % 2].t[:, :], ACT.Copy).then_inc(pT_hi[n % 2], 1)
                if job == "attn":
                    act.wait_ge(num_done[1], NC * g + 2 * n + 2)
                    for t in range(TG):
                        wait(act, gated[t].full, 4 * g)
                    act.activation(oT.hi[:, 2 * n:2 * n + 2, :], halves(num), ACT.Copy).then_inc(oT_hi, 1)
                if job == "r":
                    act.wait_ge(gated[n].full, 4 * g + 1)
                    wait(act, r_stored, 16 * g)
                    if isinstance(g, int) and g == 0:
                        act.wait_ge(w_split, n_w)
                    act.activation(gate[:, n, :], gated[n].t[:, :], ACT.Tanh, scale=0.5).then_inc(gated[n].free, 1)
                if job == "k":
                    act.wait_ge(gated[n].full, 4 * g + 2)
                    wait(act, ka_ready, 2 * g + n - 1)
                    act.activation(act_k2[n][:, :, :], halves(gated[n]), ACT.Relu).then_inc(gated[n].free, 1)
                    act.wait_ge(gated[n].free, 4 * g + 2)
                    act.activation(act_k2[n][:, :, :], act_k2[n][:, :, :], ACT.Square).then_inc(act_k2_ready, 1)
                    for t in range(TG):
                        wait(act, gated[t].full, 4 * g - 1)
                    act.wait_ge(act_k2_ready, 2 * g + n + 1)
                    act.activation(ka.hi[:, 2 * n:2 * n + 2, :], act_k2[n][:, :, :], ACT.Copy).then_inc(ka_hi, 1)
                if job == "norm":
                    act.wait_ge(norm.ready, g + 1)
                    for t in range(TG):
                        act.activation(y[:, t, :], y[:, t, :], ACT.Identity, bias=norm.shift[:, t:t + 1],
                                       scale=norm.rstd[:, t:t + 1]).then_inc(y_ready, 1)

                if job == "kv":
                    act.wait_ge(kv_turned, b + 1)
                    act.wait_ge(kvp_cleared, 2)
                    wait(act, num_done[1], NC * g)
                    for j in range(HC):
                        act.activation(kvp.hi[:, :, j, j * KD:(j + 1) * KD],
                                       turn[:, :].rearrange("p (c n) -> p c n", c=NC)[:, :, j * KD:(j + 1) * KD],
                                       ACT.Copy).then_inc(kvp_hi, 1)
                if job == "z":
                    for t in range(TG):
                        wait(act, ez_ready[t], NC * (g - 1) + n + 1)
                    act.wait_ge(z_turned, NC * b + n + 1)
                    act.activation(z_all[:, n, :], turn[:, :], ACT.Copy, bias=FLOOR * S).then_inc(z_ready, 1)

            run(act, do)

        @block.vector
        def _(dve):
            om_lo(dve)
            dve.memset(xT[:, :, 0:1], 0.0).then_inc(carried, 1)

            def do(job, n, g, b, ends):
                if job == "weights":
                    lo_w(dve, (n,))
                if job == "sq":
                    dve.wait_ge(squared, TG * g + n + 1)
                    dve.tensor_reduce(sq[:, n, :], squares[:, :].rearrange("p (h k) -> p h k", h=H), AX.X,
                                      ALU.add).then_inc(sq_ready, 1)
                if job == "turn_q":
                    dve.wait_ge(qT_hi, 2 * g + n + 1)
                    dve.tensor_tensor(qT.lo[:, 2 * n:2 * n + 2, :], turn_halves, f32(qT.hi[:, 2 * n:2 * n + 2, :]),
                                      ALU.subtract).then_inc(q_split, 1)
                if job == "mix":
                    if isinstance(g, int) and g == 0:
                        dve.wait_ge(consts_loaded, 16 * 4)
                    dve.wait_ge(diff_ready, g + 1)
                    wait(dve, mix_ready, 2 * g + n)
                    for c in range(NC):
                        last_mix = dve.scalar_tensor_tensor(out=mixed[:, c, :], in0=diff[:, c, :],
                                                            scalar=mu[:, n, c:c + 1], in1=xT[:, c, 0:GT],
                                                            op0=ALU.mult, op1=ALU.add)
                    last_mix.then_inc(mix_full, 1)
                    if n == 1 and ends:
                        dve.wait_ge(mix_full, 2 * g + 2)
                        dve.memset(xT[:, :, 0:1], 0.0).then_inc(carried, 1)
                    elif n == 1:
                        dve.wait_ge(mix_full, 2 * g + 2)
                        dve.tensor_copy(xT[:, :, 0:1], xT[:, :, GT:GT + 1]).then_inc(carried, 1)
                if job == "proj":
                    heads = slice(n * HC, (n + 1) * HC)
                    for t in range(TG):
                        dve.wait_ge(proj[t].full, NC * g + n + 1)
                        dve.tensor_reduce(top[:, t, heads], proj[t].t[:, :].rearrange("p (h m) -> p h m", h=HC),
                                          AX.X, ALU.max).then_inc(top_ready[t], 1)
                    for t in range(TG):
                        dve.wait_ge(sq_ready, TG * g + TG)
                        dve.wait_ge(top_ready[t], NC * g + n + 1)
                        dve.scalar_tensor_tensor(out=below[:, t, heads], in0=sq[:, t, heads], scalar=-0.5,
                                                 in1=top[:, t, heads], op0=ALU.mult, op1=ALU.subtract)\
                            .then_inc(below_ready[t], 1)
                if job == "den":
                    heads = slice(n * HC, (n + 1) * HC)
                    dve.wait_ge(z_floor_ready, b + 1)
                    for t in range(TG):
                        dve.wait_ge(ez_ready[t], NC * g + n + 1)
                        dve.tensor_reduce(dsum[:, t, :], ez[t][:, :].rearrange("p (h m) -> p h m", h=HC), AX.X,
                                          ALU.add).then_inc(den_ready[t], 1)
                    for t in range(TG):
                        dve.wait_ge(den_ready[t], NC * g + n + 1)
                        dve.tensor_tensor(den[:, t, :], dsum[:, t, :], z_floor[:, heads], ALU.add)\
                            .then_inc(den_chain[t], 1)
                    for t in range(TG):
                        dve.wait_ge(den_chain[t], 2 * (NC * g + n) + 1)
                        dve.reciprocal(rden[:, t, :], den[:, t, :]).then_inc(den_chain[t], 1)
                    for t in range(TG):
                        dve.wait_ge(den_chain[t], 2 * (NC * g + n) + 2)
                        eh = e[t][n % 2][:, :].rearrange("p (h m) -> p h m", h=HC)
                        dve.scalar_tensor_tensor(out=eh, in0=eh, scalar=FLOOR,
                                                 in1=rden[:, t, :].unsqueeze(2).broadcast_to([P, HC, M]),
                                                 op0=ALU.add, op1=ALU.mult).then_inc(p_ready[t], 1)
                if job == "probs":
                    dve.wait_ge(pT_hi[n % 2], NC * g + n // 2 + 1)
                    dve.tensor_tensor(pT[n % 2].lo[:, :], probs[n % 2].t[:, :], f32(pT[n % 2].hi[:, :]), ALU.subtract)\
                        .then_inc(probs[n % 2].free, 1)
                if job == "attn":
                    dve.wait_ge(oT_hi, 2 * g + n + 1)
                    dve.tensor_tensor(oT.lo[:, 2 * n:2 * n + 2, :], halves(num), f32(oT.hi[:, 2 * n:2 * n + 2, :]),
                                      ALU.subtract).then_inc(num.free, 1)
                if job == "out":
                    dve.wait_ge(gated[n].full, 4 * g + 3)
                    dve.scalar_tensor_tensor(out=gate[:, n, :], in0=gate[:, n, :], scalar=1.0, in1=gated[n].t[:, :],
                                             op0=ALU.add, op1=ALU.mult).then_inc(gated[n].free, 1)
                if job == "wo":
                    dve.wait_ge(gated[n].full, 4 * g + 4)
                    if n == 0:
                        dve.wait_ge(xb_loaded, 16 * g + 16)
                        wait(dve, y_stored, 16 * g)
                    dve.tensor_tensor(y[:, n, :], gated[n].t[:, :], xb[:, n, :], ALU.add)\
                        .then_inc(gated[n].free, 1)
                if job == "stats":
                    for t in range(TG):
                        dve.wait_ge(gated[t].free, 4 * g + 4)
                    wait(dve, norm.ready, g)
                    norm.reduce(dve, g, [y[:, t, :] for t in range(TG)])

                if job == "kv":
                    dve.wait_ge(kvp_hi, HC * b + HC)
                    for j in range(HC):
                        last_kv = dve.tensor_tensor(
                            kvp.lo[:, :, j, j * KD:(j + 1) * KD],
                            turn[:, :].rearrange("p (c n) -> p c n", c=NC)[:, :, j * KD:(j + 1) * KD],
                            f32(kvp.hi[:, :, j, j * KD:(j + 1) * KD]), ALU.subtract)
                    last_kv.then_inc(kvp_ready, 1)
                if job == "z_floor":
                    dve.wait_ge(z_ready, NC * b + NC)
                    dve.tensor_reduce(z_heads[:, :], z_all[:, :, :].rearrange("p c (h m) -> p (c h) m", h=HC), AX.X,
                                      ALU.add).then_inc(z_chain, 1)
                    dve.wait_ge(z_chain, b + 1)
                    dve.tensor_scalar(z_floor[:, :], z_heads[:, :], FLOOR, None, ALU.mult).then_inc(z_floor_ready, 1)

            run(dve, do)

        @block.tensor
        def _(pe):
            om_turn(pe)
            pe.wait_ge(om_ready, 1)
            pe.wait_ge(ones_made, 2)

            def do(job, n, g, b, ends):
                if job == "weights":
                    turn_w(pe, (n,))
                if job == "turn_q":
                    pe.wait_ge(q_loaded, 16 * g + 16)
                    wait(pe, q_split, 2 * g + n)
                    if n == 1:
                        pe.wait_ge(z_ready, NC * b + 1)
                    elif not (isinstance(g, int) and g == 0):
                        pe.wait_ge(kvp_ready, b if ends else b + 1)
                    for c in range(2):
                        for t in range(TG):
                            last_turn = pe.transpose(turn[:, c * GT + t * P:c * GT + (t + 1) * P],
                                                     uq[:, t, (2 * n + c) * P:(2 * n + c + 1) * P], ident[:, :])
                    last_turn.then_inc(q_turned, 1)
                if job == "proj":
                    if n % 2 == 0:
                        pe.wait_ge(q_split, 2 * g + n // 2 + 1)
                    for t in range(TG):
                        wait(pe, e_ready[t], NC * g + n)
                        product(pe, proj[t].t[:, :], qT[:, n, t * P:(t + 1) * P], bd[:, :], start=True, stop=True)\
                            .then_inc(proj[t].full, 1)
                if job == "probs":
                    bank = probs[n % 2]
                    wait(pe, bank.free, NC * g + n // 2)
                    for t in range(TG):
                        pe.wait_ge(p_ready[t], NC * g + n // 2 + 1)
                    for a in range(2):
                        j = 2 * (n % 2) + a
                        for t in range(TG):
                            last = pe.transpose(bank.t[:, a * GT + t * P:a * GT + (t + 1) * P],
                                                e[t][n // 2 % 2][:, j * M:(j + 1) * M], ident[:, :])
                    last.then_inc(bank.full, 1)
                if job == "num":
                    c = n // 2
                    if n == 0:
                        pe.wait_ge(kvp_ready, b + 1)
                    if n % 4 == 0:
                        wait(pe, num.free, 2 * g + n // 4)
                    pe.wait_ge(probs[n % 2].free, NC * g + n // 2 + 1)
                    for a in range(2):
                        j = 2 * (n % 2) + a
                        last = product(pe, num.t[:, (c % 2) * GT:(c % 2 + 1) * GT], kvp[:, c, j, :],
                                       pT[n % 2][:, a * GT:(a + 1) * GT], start=j == 0, stop=j == HC - 1)
                    last.then_inc(num_done[n % 2], 1)
                if job == "wo":
                    pe.wait_ge(num.free, 2 * g + 2)
                    pe.wait_ge(gated[n].free, 4 * g + 3)
                    for c in range(NC):
                        last = product(pe, gated[n].t[:, :], oT[:, c, n * P:(n + 1) * P], w["o"][:, c, :],
                                       start=c == 0, stop=c == NC - 1)
                    last.then_inc(gated[n].full, 1)
                if job == "r":
                    if isinstance(g, int) and g == 0:
                        pe.wait_ge(w_split, n_w)
                    pe.wait_ge(mix_ready, 2 * g + 1)
                    wait(pe, gated[n].free, 4 * g)
                    for c in range(NC):
                        last = product(pe, gated[n].t[:, :], mix[0][:, c, n * P:(n + 1) * P], w["r"][:, c, :],
                                       start=c == 0, stop=c == NC - 1)
                    last.then_inc(gated[n].full, 1)
                if job == "k":
                    pe.wait_ge(mix_ready, 2 * g + 2)
                    pe.wait_ge(gated[n].free, 4 * g + 1)
                    for a in range(2):
                        o = 2 * n + a
                        for c in range(NC):
                            last = product(pe, gated[n].t[:, a * GT:(a + 1) * GT], w["k"][:, c, o * P:(o + 1) * P],
                                           mix[1][:, c, :], start=c == 0, stop=c == NC - 1)
                    last.then_inc(gated[n].full, 1)
                if job == "out":
                    pe.wait_ge(ka_ready, 2 * g + 2)
                    pe.wait_ge(gated[n].free, 4 * g + 2)
                    for c in range(NC):
                        last = product(pe, gated[n].t[:, :], ka[:, c, n * P:(n + 1) * P], w["v"][:, c, :],
                                       start=c == 0, stop=c == NC - 1)
                    last.then_inc(gated[n].full, 1)

                if job == "kv":
                    pe.wait_ge(kv_loaded, 16 * b + 16)
                    pe.wait_ge(z_ready, NC * b + NC)
                    for q in range(H // 2):
                        last_kv = pe.matmul(turn[:, q * 2 * KD:(q + 1) * 2 * KD], kv_in[:, q, :], fold[:, :],
                                            start=True, stop=True)
                    last_kv.then_inc(kv_turned, 1)
                if job == "z":
                    pe.wait_ge(z_loaded, 16 * b + 16)
                    pe.wait_ge(q_split, 2 * g + min(n + 1, 2))
                    wait(pe, z_ready, NC * b + n)
                    pe.matmul(turn[:, :], ones[:, :], z_in[:, n, :], start=True, stop=True).then_inc(z_turned, 1)

            run(pe, do)

    mem.end()


def feed_forward_pass(nc, x, w1, b1, w2, b2, ln2_g, ln2_b, y_d, r_d, out, n_groups):
    G = n_groups
    x_g, y_g, r_g, out_g = by_group(x), by_group(y_d), by_group(r_d), by_group(out)
    NH = FC // 2
    HB = 4

    mem = Scope(nc, "ffn_")
    ctx = ExitStack()
    with ctx:
        def sb(name, shape, dt=FP32):
            return ctx.enter_context(mem.sbuf_tensor(name, shape, dt))

        def sem(name):
            return mem.sem(name)

        wa = Pair(mem, ctx, "wa", [P, NC, FF])
        wb = Pair(mem, ctx, "wb", [P, FC, D])
        ident = sb("ident", [P, P])
        bias1 = sb("bias1", [P, FC])
        bias2, gain, offset = sb("bias2", [P, D]), sb("gain2", [P, D]), sb("offset2", [P, D])
        y = sb("y_in", [P, TG, D])
        yb = sb("yb", [P, TG, D])
        s = sb("s", [P, TG, D])
        x_in = sb("x_in", [P, TG, D])
        r_in = sb("r_in", [P, TG, D])
        yT = Pair(mem, ctx, "yT", [P, NC, GT])
        hid = [sb(f"hid{n}", [P, 2, GT]) for n in range(2)]
        hT = [Pair(mem, ctx, f"hT{n}", [P, 2, GT]) for n in range(HB)]
        norm = Norm(mem, ctx, "n2", EPS1)

        turn = [Bank(mem, ctx, f"turn{n}") for n in range(2)]
        hidden = [Bank(mem, ctx, f"hidden{n}") for n in range(HB)]
        result = [Bank(mem, ctx, f"result{t}") for t in range(TG)]

        sp_passed = sem("sp_passed")
        ident_made = sem("ident_made")
        consts_loaded = sem("consts_loaded")
        y_loaded, xr_loaded, yT_hi, yb_ready = sem("y_loaded"), sem("xr_loaded"), sem("yT_hi"), sem("yb_ready")
        gelu_ready = [sem(f"gelu{n}") for n in range(2)]
        h_hi = [sem(f"h_hi{n}") for n in range(2)]
        h_ready = [sem(f"h_ready{n}") for n in range(HB)]
        used = [sem(f"used{n}") for n in range(HB)]
        sum_ready, normed, gained, offsets = sem("sum_ready"), sem("normed"), sem("gained"), sem("offsets")
        base_ready, done, stored = sem("base_ready"), sem("done"), sem("stored")

        stages = [a.rearrange("p t n -> p (t n)") for a in (s[:, :, :], x_in[:, :, :], r_in[:, :, :])]
        pieces = []
        a_view = w1.rearrange("(c p) n -> p c n", p=P)
        b_view = w2.rearrange("(c p) n -> p c n", p=P)
        for n in range(NH):
            cols = slice(n * 2 * P, (n + 1) * 2 * P)
            pieces.append((a_view[:, :, cols], wa[:, :, cols], NC))
            pieces.append((b_view[:, 2 * n:2 * n + 2, :], wb[:, 2 * n:2 * n + 2, :], 2))

        def stage(k):
            return stages[k % len(stages)].rearrange("p (c n) -> p c n", c=pieces[k][2])

        loaded = [sem(f"w3_loaded{n}") for n in range(len(stages))]
        rounded, w_split = sem("w3_rounded"), sem("w3_split")
        ns = len(stages)

        BODY = ([("w1", 0, 0), ("w1", 1, 0), ("w1", 2, 0), ("base", 0, 0)]
                + [job for n in range(3, NH) for job in (("w2", n - 3, 0), ("w1", n, 0))]
                + [("turn", 0, 1), ("w2", NH - 3, 0), ("w2", NH - 2, 0), ("w2", NH - 1, 0), ("end", 0, 0)])

        def run(eng, do):
            do("weights", 0, 0)
            do("weights", 1, 0)
            do("turn", 0, 0)
            for job, n, lead in BODY:
                if job == "w1" and n + 2 < NH:
                    do("weights", n + 2, 0)
                if job != "base":
                    do(job, n, lead)
                if job == "w1" and n == NH - 1:
                    do("base", 0, 0)
            with eng.Fori(1, G - 1) as g:
                for job, n, lead in BODY:
                    do(job, n, g + lead)
            for job, n, lead in BODY:
                if lead == 0:
                    do(job, n, G - 1)

        block = ctx.enter_context(nc.Block())

        @block.sync
        def _(sp):
            sp.dma_start(y[:, :, :], y_g[0]).then_inc(y_loaded, 16)

            def do(job, n, g):
                if job == "weights":
                    for k in (2 * n, 2 * n + 1):
                        wait(sp, w_split, k - ns + 1)
                        sp.dma_start(stage(k), pieces[k][0]).then_inc(loaded[k % ns], 16)
                    if n == 0:
                        for dst, src in ((bias2[:, :], row_on_all(b2, D)), (gain[:, :], row_on_all(ln2_g, D)),
                                         (offset[:, :], row_on_all(ln2_b, D)),
                                         (bias1[:, :], b1.rearrange("(c p) -> p c", p=P))):
                            with nc.allow_non_contiguous_dma(reason="one vector of the layer's width"):
                                sp.dma_start(dst, src).then_inc(consts_loaded, 16)
                if job == "base":
                    for m in range(2):
                        sp.wait_ge(turn[m].full, g + 1)
                    wait_alone(sp, yb_ready, g + 1, sp_passed)
                    sp.dma_start(y[:, :, :], y_g[after(g, G)]).then_inc(y_loaded, 16)
                    wait_alone(sp, base_ready, g, sp_passed)
                    wait(sp, stored, 16 * g)
                    if isinstance(g, int) and g == 0:
                        sp.wait_ge(w_split, len(pieces))
                    sp.dma_start(x_in[:, :, :], x_g[g]).then_inc(xr_loaded, 16)
                    sp.dma_start(r_in[:, :, :], r_g[g]).then_inc(xr_loaded, 16)
                if job == "end":
                    sp.wait_ge(done, g + 1)
                    sp.dma_start(out_g[g], x_in[:, :, :]).then_inc(stored, 16)

            run(sp, do)
            sp.wait_ge(y_loaded, 16 * (G + 1))
            sp.wait_ge(stored, 16 * G)

        @block.gpsimd
        def _(pool):
            make_identity(pool, ident, ident_made)
            norm.init(pool)
            pool.wait_ge(consts_loaded, 16 * 4)

            def do(job, n, g):
                if job == "base":
                    pool.wait_ge(y_loaded, 16 * g + 16)
                    wait(pool, sum_ready, TG * g)
                    pool.tensor_tensor(yb[:, :, :], y[:, :, :], bias2[:, :].unsqueeze(1).broadcast_to([P, TG, D]),
                                       ALU.add).then_inc(yb_ready, 1)
                if job == "end":
                    norm.invert(pool, g)
                    pool.wait_ge(normed, TG * g + TG)
                    pool.tensor_tensor(s[:, :, :], s[:, :, :], gain[:, :].unsqueeze(1).broadcast_to([P, TG, D]),
                                       ALU.mult).then_inc(gained, 1)
                    pool.wait_ge(gained, g + 1)
                    pool.tensor_tensor(s[:, :, :], s[:, :, :], offset[:, :].unsqueeze(1).broadcast_to([P, TG, D]),
                                       ALU.add).then_inc(offsets, 1)
                    pool.wait_ge(offsets, g + 1)
                    pool.wait_ge(base_ready, g + 1)
                    pool.tensor_tensor(x_in[:, :, :], s[:, :, :], x_in[:, :, :], ALU.add).then_inc(done, 1)

            run(pool, do)

        @block.scalar
        def _(act):
            def do(job, n, g):
                if job == "weights":
                    for k in (2 * n, 2 * n + 1):
                        act.wait_ge(loaded[k % ns], 16 * (k // ns + 1))
                        act.activation(pieces[k][1][0], stage(k), ACT.Copy).then_inc(rounded, 1)
                if job == "turn":
                    for m in range(HB):
                        wait(act, hidden[m].full, (NH // HB) * g)
                    for m in range(2):
                        act.wait_ge(turn[m].full, g + 1)
                        act.activation(yT.hi[:, 2 * m:2 * m + 2, :], halves(turn[m]), ACT.Copy).then_inc(yT_hi, 1)
                if job == "w1":
                    bank = hidden[n % HB]
                    if n == 0 and isinstance(g, int) and g == 0:
                        act.wait_ge(consts_loaded, 16 * 4)
                    act.wait_ge(bank.full, (NH // HB) * g + n // HB + 1)
                    prev = n - 2 if n >= 2 else n - 2 + NH
                    wait(act, h_ready[prev % HB], (NH // HB) * g + (prev // HB + 1 if n >= 2 else 0))
                    for a in range(2):
                        last = act.activation(hid[n % 2][:, a, :], bank.t[:, a * GT:(a + 1) * GT], ACT.Gelu,
                                              bias=bias1[:, 2 * n + a:2 * n + a + 1])
                    last.then_inc(bank.free, 1)
                    act.wait_ge(bank.free, (NH // HB) * g + n // HB + 1)
                    if n < HB:
                        for t in range(TG):
                            wait(act, result[t].full, g)
                    else:
                        act.wait_ge(used[n % HB], (NH // HB - 1) * g + n // HB)
                    act.activation(hT[n % HB].hi[:, :, :], hid[n % 2][:, :, :], ACT.Copy).then_inc(h_hi[n % 2], 1)
                if job == "end":
                    act.wait_ge(norm.ready, g + 1)
                    for t in range(TG):
                        act.activation(s[:, t, :], s[:, t, :], ACT.Identity, bias=norm.shift[:, t:t + 1],
                                       scale=norm.rstd[:, t:t + 1]).then_inc(normed, 1)

            run(act, do)

        @block.vector
        def _(dve):
            def do(job, n, g):
                if job == "weights":
                    for k in (2 * n, 2 * n + 1):
                        dve.wait_ge(rounded, k + 1)
                        dve.tensor_tensor(pieces[k][1][1], stage(k), f32(pieces[k][1][0]), ALU.subtract)\
                            .then_inc(w_split, 1)
                if job == "turn":
                    for m in range(2):
                        dve.wait_ge(yT_hi, 2 * g + m + 1)
                        dve.tensor_tensor(yT.lo[:, 2 * m:2 * m + 2, :], halves(turn[m]),
                                          f32(yT.hi[:, 2 * m:2 * m + 2, :]), ALU.subtract).then_inc(turn[m].free, 1)
                if job == "w1":
                    dve.wait_ge(h_hi[n % 2], (NH // 2) * g + n // 2 + 1)
                    dve.tensor_tensor(hT[n % HB].lo[:, :, :], hid[n % 2][:, :, :], f32(hT[n % HB].hi[:, :, :]),
                                      ALU.subtract).then_inc(h_ready[n % HB], 1)
                if job == "base":
                    dve.wait_ge(xr_loaded, 32 * g + 32)
                    dve.scalar_tensor_tensor(out=x_in[:, :, :], in0=r_in[:, :, :], scalar=0.5, in1=x_in[:, :, :],
                                             op0=ALU.mult, op1=ALU.add).then_inc(base_ready, 1)
                if job == "end":
                    for t in range(TG):
                        dve.wait_ge(result[t].full, g + 1)
                        dve.wait_ge(yb_ready, g + 1)
                        wait(dve, done, g)
                        dve.tensor_tensor(s[:, t, :], result[t].t[:, :], yb[:, t, :], ALU.add).then_inc(sum_ready, 1)
                    dve.wait_ge(sum_ready, TG * g + TG)
                    wait(dve, norm.ready, g)
                    norm.reduce(dve, g, [s[:, t, :] for t in range(TG)])

            run(dve, do)

        @block.tensor
        def _(pe):
            pe.wait_ge(ident_made, 2)

            def do(job, n, g):
                if job == "turn":
                    pe.wait_ge(y_loaded, 16 * g + 16)
                    for m in range(2):
                        wait(pe, turn[m].free, g)
                        for c in range(2):
                            for t in range(TG):
                                last = pe.transpose(turn[m].t[:, c * GT + t * P:c * GT + (t + 1) * P],
                                                    y[:, t, (2 * m + c) * P:(2 * m + c + 1) * P], ident[:, :])
                        last.then_inc(turn[m].full, 1)
                if job == "w1":
                    bank = hidden[n % HB]
                    if n == 0:
                        for m in range(2):
                            pe.wait_ge(turn[m].free, g + 1)
                    if isinstance(g, int) and g == 0:
                        pe.wait_ge(w_split, 2 * n + 1)
                    wait(pe, bank.free, (NH // HB) * g + n // HB)
                    for a in range(2):
                        o = 2 * n + a
                        for c in range(NC):
                            last = product(pe, bank.t[:, a * GT:(a + 1) * GT], wa[:, c, o * P:(o + 1) * P],
                                           yT[:, c, :], start=c == 0, stop=c == NC - 1)
                    last.then_inc(bank.full, 1)
                if job == "w2":
                    pe.wait_ge(h_ready[n % HB], (NH // HB) * g + n // HB + 1)
                    if isinstance(g, int) and g == 0:
                        pe.wait_ge(w_split, 2 * n + 2)
                    for t in range(TG):
                        if n == 0:
                            wait(pe, sum_ready, TG * g)
                        for a in range(2):
                            last = product(pe, result[t].t[:, :], hT[n % HB][:, a, t * P:(t + 1) * P],
                                           wb[:, 2 * n + a, :], start=n == 0 and a == 0, stop=n == NH - 1 and a == 1)
                        if n == NH - 1:
                            last.then_inc(result[t].full, 1)
                    if n < NH - HB:
                        last.then_inc(used[n % HB], 1)

            run(pe, do)

    mem.end()


def performer_and_gated_block(nc, x, wq, wk, wv, wo, omega, ln1_g, ln1_b, w1, b1, w2, b2, ln2_g, ln2_b,
                              w_r, w_k, w_v, mu_r, mu_k, out):
    B, S, _ = x.shape
    n_groups = B * S // GT
    rows = [B * S, D]
    x_rows = x.rearrange("b s d -> (b s) d")
    out_rows = out.rearrange("b s d -> (b s) d")
    xn_d = nc.dram_tensor("xn_d", rows, FP32, kind="Internal").ap()
    xT_d = nc.dram_tensor("xT_d", [n_groups, P, NC, GT], FP32, kind="Internal").ap()
    u_d = nc.dram_tensor("u_d", rows, FP32, kind="Internal").ap()
    y_d = nc.dram_tensor("y_d", rows, FP32, kind="Internal").ap()
    r_d = nc.dram_tensor("r_d", rows, FP32, kind="Internal").ap()
    kv_d = nc.dram_tensor("kv_d", [B, P, H // 2, M], FP32, kind="Internal").ap()
    z_d = nc.dram_tensor("z_d", [B, P, NC, HC * M], FP32, kind="Internal").ap()
    keys_pass(nc, x_rows, wq, wk, wv, omega, xn_d, xT_d, u_d, kv_d, z_d, B, S // GT)
    attend_pass(nc, wo, omega, ln1_g, ln1_b, w_r, w_k, w_v, mu_r, mu_k, xn_d, xT_d, u_d, kv_d, z_d, y_d, r_d,
                B, S // GT)
    feed_forward_pass(nc, x_rows, w1, b1, w2, b2, ln2_g, ln2_b, y_d, r_d, out_rows, n_groups)


_INS = ['L0_attn_x', 'L0_attn_wq', 'L0_attn_wk', 'L0_attn_wv', 'L0_attn_wo', 'L0_attn_omega', 'L0_attn_ln1_g',
        'L0_attn_ln1_b', 'L0_attn_w1', 'L0_attn_b1', 'L0_attn_w2', 'L0_attn_b2', 'L0_attn_ln2_g', 'L0_attn_ln2_b',
        'L0_ffn_W_r', 'L0_ffn_W_k', 'L0_ffn_W_v', 'L0_ffn_mu_r', 'L0_ffn_mu_k']
_OUTS = [((8, 1024, 512), 'float32')]


def kernel(**inputs):
    import numpy as _np
    import concourse.bacc as _bacc
    from concourse import mybir as _mybir
    from concourse.bass_utils import run_bass_kernel_spmd as _run

    nc = _bacc.Bacc("TRN2", target_bir_lowering=False, num_devices=1)
    arrays, args = {}, []
    for name in _INS:
        a = _np.ascontiguousarray(inputs[name])
        arrays[f"in_{name}_dram"] = a
        args.append(nc.dram_tensor(f"in_{name}_dram", a.shape, _mybir.dt.from_np(a.dtype), kind="ExternalInput").ap())
    for i, (shape, dtype) in enumerate(_OUTS):
        dt = _mybir.dt.from_np(_np.dtype(dtype))
        args.append(nc.dram_tensor(f"out_{i}_dram", shape, dt, kind="ExternalOutput").ap())
    performer_and_gated_block(nc, *args)
    r = _run(nc, [arrays], core_ids=[0])
    got = tuple(r.results[0][f"out_{i}_dram"] for i in range(len(_OUTS)))
    return got[0]
```
